# Optimizing a Trainium2 kernel written in Bass

```python
import numpy as np
import jax
import jax.numpy as jnp

def _softmax(x, axis=-1):
    return jax.nn.softmax(x, axis=axis)

def _gelu(x):
    return jax.nn.gelu(x, approximate=True)

def _silu(x):
    return jax.nn.silu(x)

def _sigmoid(x):
    return jax.nn.sigmoid(x)

def _layernorm(x, axis=-1, eps=1e-05):
    m = jnp.mean(x, axis=axis, keepdims=True)
    v = jnp.var(x, axis=axis, keepdims=True)
    return (x - m) / jnp.sqrt(v + eps)

def _scatter_add(tgt, idx, src, axis=0):
    return tgt.at[idx].add(src)

def _segment_sum(src, seg, n):
    return jax.ops.segment_sum(src, seg, n)
kernel_name = 'mk_gnn_preln_d2_gnn_r8_369c3f'

def setup_inputs(seed: int=0):
    np.random.seed(seed)
    _w = jnp.asarray

    def _rec_inputs():
        import jax
        import jax.numpy as jnp
        _gk = jax.random.key(seed)
        x = -0.0003713 + 1 * jax.random.normal(jax.random.fold_in(_gk, 1), (12500, 128), jnp.float32)
        src = jax.random.randint(jax.random.fold_in(_gk, 2), (200000,), 0, 12500, jnp.int32)
        dst = jax.random.randint(jax.random.fold_in(_gk, 3), (200000,), 0, 12500, jnp.int32)
        _o = jnp.argsort(dst, stable=True)
        src = src[_o]
        dst = dst[_o]
        edge_attr_32 = 0.000189758 + 1.00013 * jax.random.normal(jax.random.fold_in(_gk, 11), (200000, 32), jnp.float32)
        return (x, src, dst, edge_attr_32)
    x, src, dst, edge_attr_32 = _rec_inputs()

    def _L0_gnn_setup():
        import jax, jax.numpy as jnp
        import numpy as np
        N = 12500
        E = 200000
        H = 8
        C = 16
        DIM = 128
        EDGE_DIM = 32
        key = jax.random.key(seed)
        ks = jax.random.split(key, 7)
        s = 1.0 / np.sqrt(DIM)
        return {'x': jax.random.normal(ks[0], (N, DIM), dtype=jnp.float32), 'edge_index': jax.random.randint(ks[1], (2, E), 0, N, dtype=jnp.int32), 'edge_attr': jax.random.normal(ks[2], (E, EDGE_DIM), dtype=jnp.float32), 'Wq': jax.random.normal(ks[3], (H * C, DIM), dtype=jnp.float32) * s, 'Wk': jax.random.normal(ks[4], (H * C, DIM), dtype=jnp.float32) * s, 'Wv': jax.random.normal(ks[5], (H * C, DIM), dtype=jnp.float32) * s, 'We': jax.random.normal(ks[6], (H, EDGE_DIM), dtype=jnp.float32) * (1.0 / np.sqrt(EDGE_DIM))}
    _L0_gnn_all = _L0_gnn_setup()
    _L0_gnn_in = {k: v for k, v in _L0_gnn_all.items() if k in ('Wq', 'Wk', 'Wv', 'We')}
    del _L0_gnn_all

    def _L1_gnn_setup():
        import jax, jax.numpy as jnp
        import numpy as np
        N_NODES = 6250
        N_EDGES = 100000
        EPS = 1e-05

        def _gcn_norm(edge_index, num_nodes):
            loop = jnp.arange(num_nodes, dtype=edge_index.dtype)
            src = jnp.concatenate([edge_index[0], loop])
            dst = jnp.concatenate([edge_index[1], loop])
            deg = jax.ops.segment_sum(jnp.ones_like(dst, dtype=jnp.float32), dst, num_segments=num_nodes)
            dinv = jnp.where(deg > 0, jax.lax.rsqrt(deg), 0.0)
            norm = dinv[src] * dinv[dst]
            return (src, dst, norm)

        def _gcn_conv(x, W, b, src, dst, norm, num_nodes):
            h = x @ W
            msg = h[src] * norm[:, None]
            out = jax.ops.segment_sum(msg, dst, num_segments=num_nodes)
            return out + b

        def _batch_norm(x, gamma, beta):
            mean = jnp.mean(x, axis=0)
            var = jnp.mean((x - mean) ** 2, axis=0)
            return (x - mean) * jax.lax.rsqrt(var + EPS) * gamma + beta
        key = jax.random.key(seed)
        ks = jax.random.split(key, 16)
        s = 0.05
        return {'x': jax.random.uniform(ks[0], (N_NODES, 128), dtype=jnp.float32), 'edge_index': jax.random.randint(ks[1], (2, N_EDGES), 0, N_NODES, dtype=jnp.int32), 'W1': jax.random.normal(ks[2], (128, 256), dtype=jnp.float32) * s, 'b1': jnp.zeros((256,), jnp.float32), 'g1': jnp.ones((256,), jnp.float32), 'beta1': jnp.zeros((256,), jnp.float32), 'W2': jax.random.normal(ks[3], (256, 128), dtype=jnp.float32) * s, 'b2': jnp.zeros((128,), jnp.float32), 'g2': jnp.ones((128,), jnp.float32), 'beta2': jnp.zeros((128,), jnp.float32), 'W3': jax.random.normal(ks[4], (128, 128), dtype=jnp.float32) * s, 'b3': jnp.zeros((128,), jnp.float32), 'g3': jnp.ones((128,), jnp.float32), 'beta3': jnp.zeros((128,), jnp.float32)}
    _L1_gnn_all = _L1_gnn_setup()
    _L1_gnn_in = {k: v for k, v in _L1_gnn_all.items() if k in ('W1', 'b1', 'g1', 'beta1', 'W2', 'b2', 'g2', 'beta2', 'W3', 'b3', 'g3', 'beta3')}
    del _L1_gnn_all
    return {'x': x, 'src': src, 'dst': dst, 'edge_attr_32': edge_attr_32, 'L0_gnn_Wq': _L0_gnn_in['Wq'], 'L0_gnn_Wk': _L0_gnn_in['Wk'], 'L0_gnn_Wv': _L0_gnn_in['Wv'], 'L0_gnn_We': _L0_gnn_in['We'], 'L1_gnn_W1': _L1_gnn_in['W1'], 'L1_gnn_b1': _L1_gnn_in['b1'], 'L1_gnn_g1': _L1_gnn_in['g1'], 'L1_gnn_beta1': _L1_gnn_in['beta1'], 'L1_gnn_W2': _L1_gnn_in['W2'], 'L1_gnn_b2': _L1_gnn_in['b2'], 'L1_gnn_g2': _L1_gnn_in['g2'], 'L1_gnn_beta2': _L1_gnn_in['beta2'], 'L1_gnn_W3': _L1_gnn_in['W3'], 'L1_gnn_b3': _L1_gnn_in['b3'], 'L1_gnn_g3': _L1_gnn_in['g3'], 'L1_gnn_beta3': _L1_gnn_in['beta3']}

def reference(x, src, dst, edge_attr_32, L0_gnn_Wq, L0_gnn_Wk, L0_gnn_Wv, L0_gnn_We, L1_gnn_W1, L1_gnn_b1, L1_gnn_g1, L1_gnn_beta1, L1_gnn_W2, L1_gnn_b2, L1_gnn_g2, L1_gnn_beta2, L1_gnn_W3, L1_gnn_b3, L1_gnn_g3, L1_gnn_beta3):
    import jax
    import jax.numpy as jnp

    def _L0_gnn_ref(x, edge_index, edge_attr, Wq, Wk, Wv, We):
        import jax, jax.numpy as jnp
        import numpy as np
        N = 12500
        E = 200000
        H = 8
        C = 16
        DIM = 128
        EDGE_DIM = 32
        q = (x @ Wq.T).reshape(N, H, C)
        k = (x @ Wk.T).reshape(N, H, C)
        v = (x @ Wv.T).reshape(N, H, C)
        src, dst = (edge_index[0], edge_index[1])
        edge_bias = edge_attr @ We.T
        scores = jnp.einsum('ehc,ehc->eh', q[dst], k[src]) / np.sqrt(C) + edge_bias
        seg_max = jax.ops.segment_max(scores, dst, num_segments=N)
        ex = jnp.exp(scores - seg_max[dst])
        denom = jax.ops.segment_sum(ex, dst, num_segments=N)
        alpha = ex / denom[dst]
        msgs = v[src] * alpha[:, :, None]
        out = jax.ops.segment_sum(msgs, dst, num_segments=N)
        return out.reshape(N, H * C)

    def _L1_gnn_ref(x, edge_index, W1, b1, g1, beta1, W2, b2, g2, beta2, W3, b3, g3, beta3):
        import jax, jax.numpy as jnp
        import numpy as np
        N_NODES = 6250
        N_EDGES = 100000
        EPS = 1e-05

        def _gcn_norm(edge_index, num_nodes):
            loop = jnp.arange(num_nodes, dtype=edge_index.dtype)
            src = jnp.concatenate([edge_index[0], loop])
            dst = jnp.concatenate([edge_index[1], loop])
            deg = jax.ops.segment_sum(jnp.ones_like(dst, dtype=jnp.float32), dst, num_segments=num_nodes)
            dinv = jnp.where(deg > 0, jax.lax.rsqrt(deg), 0.0)
            norm = dinv[src] * dinv[dst]
            return (src, dst, norm)

        def _gcn_conv(x, W, b, src, dst, norm, num_nodes):
            h = x @ W
            msg = h[src] * norm[:, None]
            out = jax.ops.segment_sum(msg, dst, num_segments=num_nodes)
            return out + b

        def _batch_norm(x, gamma, beta):
            mean = jnp.mean(x, axis=0)
            var = jnp.mean((x - mean) ** 2, axis=0)
            return (x - mean) * jax.lax.rsqrt(var + EPS) * gamma + beta
        n = x.shape[0]
        src, dst, norm = _gcn_norm(edge_index, n)
        h = _gcn_conv(x, W1, b1, src, dst, norm, n)
        h = _batch_norm(jax.nn.relu(h), g1, beta1)
        h = _gcn_conv(h, W2, b2, src, dst, norm, n)
        h = _batch_norm(jax.nn.relu(h), g2, beta2)
        h = _gcn_conv(h, W3, b3, src, dst, norm, n)
        return _batch_norm(h, g3, beta3)
    edge_index = jnp.stack([src, dst])
    h = jnp.maximum(_layernorm(x, axis=-1), 0.0)
    x = x + _L0_gnn_ref(h, edge_index, edge_attr_32, L0_gnn_Wq, L0_gnn_Wk, L0_gnn_Wv, L0_gnn_We)
    h = jnp.maximum(_layernorm(x, axis=-1), 0.0)
    x = x + _L1_gnn_ref(h, edge_index, L1_gnn_W1, L1_gnn_b1, L1_gnn_g1, L1_gnn_beta1, L1_gnn_W2, L1_gnn_b2, L1_gnn_g2, L1_gnn_beta2, L1_gnn_W3, L1_gnn_b3, L1_gnn_g3, L1_gnn_beta3)
    return x

_drawn_inputs = setup_inputs


def setup_inputs(seed=0):
    import zlib

    import numpy as np

    out = dict(_drawn_inputs(seed))
    spreads = {'L1_gnn_b1': (0.0, 0.1),
     'L1_gnn_g1': (1.0, 0.2),
     'L1_gnn_beta1': (0.0, 0.1),
     'L1_gnn_b2': (0.0, 0.1),
     'L1_gnn_g2': (1.0, 0.2),
     'L1_gnn_beta2': (0.0, 0.272),
     'L1_gnn_b3': (0.0, 0.8),
     'L1_gnn_g3': (1.0, 0.2),
     'L1_gnn_beta3': (0.0, 0.1)}
    factors = {}
    for name, (base, spread) in spreads.items():
        noise = np.random.default_rng([zlib.crc32(name.encode()), seed]).standard_normal(out[name].shape)
        drawn = base * np.exp(spread * noise) if base else spread * noise
        out[name] = jnp.asarray(drawn.astype(out[name].dtype))
    for name, factor in factors.items():
        out[name] = (out[name] * factor).astype(out[name].dtype)
    return out
```

```python
from contextlib import ExitStack

import concourse.bass as bass
from concourse import mybir

ALU = mybir.AluOpType
ACT = mybir.ActivationFunctionType
AX = mybir.AxisListType
F32 = mybir.dt.float32
BF16 = mybir.dt.bfloat16
I32 = mybir.dt.int32
U32 = mybir.dt.uint32

P = 128
W = 32
G = 4
J = 2
C = G * J
BLOCK = C * P
HEADS = 8
HC = 16
DIM = HEADS * HC
EDIM = 32
CH = 512
SENTINEL = 1 << 20
BIG = float(2 ** 100)
EPS = 1e-5
AUXD = 64
AUXN = 72
AUXROWS = 73
U4 = 4
U2 = 2


class Shapes:

    def __init__(self, n_nodes, n_edges):
        self.N, self.E = n_nodes, n_edges
        self.NS = -(-(n_nodes + W) // 256) * 256
        self.LAST = self.NS - W
        self.BLOCKS = -(-n_edges // (BLOCK * U4)) * U4
        self.GROUPS = self.BLOCKS * G
        self.GP = max(p for p in range(1, P + 1) if self.GROUPS % p == 0)
        self.GF = self.GROUPS // self.GP
        self.TILES = self.NS // P
        self.FULL = n_nodes // CH
        self.CHUNKS = self.FULL + 1
        self.LW = self.NS - self.FULL * CH
        self.LV = n_nodes - self.FULL * CH
        assert self.TILES % U2 == 0 and self.FULL % U2 == 0 and 0 < self.LV <= self.LW <= CH


class Step:

    def __init__(self, n, slot, nth, use, use_in_pass):
        self.n, self.slot, self.nth, self.use, self.use_in_pass = n, slot, nth, use, use_in_pass

    def freed(self, eng, sem, depth):
        if not (isinstance(self.n, int) and self.n < depth):
            eng.wait_ge(sem, self.nth - depth)

    def slot_freed(self, eng, sem, count):
        if not (isinstance(self.n, int) and self.use_in_pass == 0):
            eng.wait_ge(sem, (self.use - 1) * count)


def alone(eng):
    eng.nop(nofuse=True)


def steps(eng, total, slots, stages, pass_=None):
    most = max(lag for lag, _ in stages)
    first = 1 + -(-most // slots)
    full = total // slots

    def step(n, slot, use):
        if pass_ is None:
            return Step(n, slot, n + 1, use + 1, use)
        return Step(n, slot, pass_ * total + n + 1, pass_ * full + use + 1, use)

    def static(i):
        for lag, stage in stages:
            n = i - lag
            if 0 <= n < total:
                stage(step(n, n % slots, n // slots))

    assert pass_ is None or total % slots == 0
    loop = range(first * slots, full * slots) if full > first else range(0)
    head = loop.start if loop else total + most
    for i in range(head):
        static(i)
    if loop:
        with eng.Fori(first, full) as t:
            for k in range(slots):
                for lag, stage in stages:
                    stage(step(t * slots + (k - lag), (k - lag) % slots, t + (k - lag) // slots))
        for i in range(loop.stop, total + most):
            static(i)


def build(nc, sh, x, src_blocks, dst_cols, dst_groups, attr, wqkv, wet, w1, w2, w3, vecs, out):
    ctx = ExitStack()

    def sb(name, shape, dt=F32):
        return ctx.enter_context(nc.sbuf_tensor(name, shape, dt))

    with ctx:
        q_tab = nc.dram_tensor("q_tab", (sh.NS, 3 * DIM), BF16, kind="Internal").ap()
        kv_tab = nc.dram_tensor("kv_tab", (sh.NS, 2 * DIM), F32, kind="Internal").ap()
        x1_tab = nc.dram_tensor("x1_tab", (sh.NS, DIM), F32, kind="Internal").ap()
        g_tabs = [nc.dram_tensor(f"g_tab{i}", (sh.NS, DIM), F32, kind="Internal").ap() for i in range(3)]
        base_tab = nc.dram_tensor("base_tab", (sh.GROUPS,), I32, kind="Internal").ap()

        state = sb("state", [P, sh.NS])
        aux = sb("aux", [P, sh.NS])
        dst_f = sb("dst_f", [P, sh.BLOCKS * C])
        dst_rel = sb("dst_rel", [P, sh.BLOCKS * C])
        base_w = sb("base_w", [P, sh.GROUPS])
        base_i = sb("base_i", [1, sh.GROUPS], I32)
        windows = sb("windows", [1, 1], I32)
        ident = sb("ident", [P, P])
        iota_w = sb("iota_w", [P, W])
        eps_t = sb("eps_t", [P, 1])
        one_t = sb("one_t", [P, 1])
        neg1_t = sb("neg1_t", [P, 1])
        zero_t = sb("zero_t", [P, 1])
        vec_t = sb("vec_t", [P, 12])

        prepare(nc, sh, locals())
        project(nc, sh, locals())
        attend(nc, sh, locals())
        normalise(nc, sh, locals())
        with nc.sbuf_tensor("w1_sb", [P, 2, DIM], F32) as w1_sb, \
                nc.sbuf_tensor("w2_sb", [P, 2, DIM], F32) as w2_sb, \
                nc.sbuf_tensor("w3_sb", [P, DIM], F32) as w3_sb:
            weights = (w1_sb, w2_sb, w3_sb)
            for layer in range(3):
                aggregate(nc, sh, layer, locals())
                transform(nc, sh, layer, locals())


def semaphores(nc, ctx):
    made = []


    def clear():
        nc.clear_and_free_semaphores(made)
        nc.all_engine_barrier()

    ctx.callback(clear)

    def sem(name):
        made.append(nc.alloc_semaphore(name))
        return made[-1]
    return sem


def prepare(nc, sh, env):
    ident, iota_w, windows, base_tab = env["ident"], env["iota_w"], env["windows"], env["base_tab"]
    state, aux, dst_f, base_w, base_i = env["state"], env["aux"], env["dst_f"], env["base_w"], env["base_i"]
    wide = sh.GF * J * P
    with ExitStack() as c:
        def tile(name, shape, dt=F32):
            return c.enter_context(nc.sbuf_tensor(name, shape, dt))

        raw = tile("raw", [P, wide], I32)
        val = tile("val", [P, wide])
        low = tile("low", [P, wide])
        dst_i = tile("dst_i", [P, sh.BLOCKS * C], I32)
        base_n = tile("base_n", [P, sh.GROUPS], I32)
        least = tile("least", [P, sh.GF])
        most = tile("most", [P, sh.GF])
        span = tile("span", [P, sh.GF])
        span1 = tile("span1", [P, 1])
        top = tile("top", [1, 2])
        least_i = tile("least_i", [P, sh.GF], I32)
        turned = c.enter_context(nc.psum_tensor("turned", [P, P], F32))
        new = semaphores(nc, c)
        loaded, cast, lowered, reduced, spanned, widest, topped, base_made, base_out, base_back, cols_in, made = (
            new(s) for s in
            ("loaded", "cast", "lowered", "reduced", "spanned", "widest", "topped", "base_made", "base_out",
             "base_back", "cols_in", "made"))
        block = c.enter_context(nc.Block())

        @block.sync
        def _(sp):
            sp.dma_start(raw[0:sh.GP, :], env["dst_groups"]).then_inc(loaded, 16)
            sp.dma_start(dst_i[:, :], env["dst_cols"]).then_inc(cols_in, 16)
            sp.dma_start(env["vec_t"][:, :], env["vecs"]).then_inc(cols_in, 16)
            sp.wait_ge(base_made, 1)
            sp.dma_start(base_tab.rearrange("(p f) -> p f", p=sh.GP), least_i[0:sh.GP, :]).then_inc(base_out, 16)
            sp.wait_ge(base_out, 16)
            sp.dma_start(base_n[:, :], base_tab.unsqueeze(0).to_broadcast([P, sh.GROUPS])).then_inc(base_back, 16)
            sp.wait_ge(base_back, 16)

        @block.gpsimd
        def _(pool):
            nc.gpsimd.memset(ident[:, :], 0.0).then_inc(made, 1)
            pool.wait_ge(made, 1)
            nc.gpsimd.affine_select(out=ident[:, :], in_=ident[:, :], compare_op=ALU.not_equal, fill=1.0, base=0,
                                    pattern=[[-1, P]], channel_multiplier=1).then_inc(made, 1)
            nc.gpsimd.iota(iota_w[:, :], pattern=[[1, W]], base=0, channel_multiplier=0,
                           allow_small_or_imprecise_dtypes=True)
            nc.gpsimd.memset(env["eps_t"][:, :], EPS)
            nc.gpsimd.memset(env["one_t"][:, :], 1.0)
            nc.gpsimd.memset(env["neg1_t"][:, :], -1.0)
            nc.gpsimd.memset(env["zero_t"][:, :], 0.0)
            nc.gpsimd.memset(state[:, :], 0.0)
            nc.gpsimd.memset(aux[:, :], 0.0).then_inc(made, 1)
            pool.wait_ge(made, 3)
            nc.gpsimd.memset(aux[0:HEADS, :], -BIG).then_inc(made, 1)

        @block.vector
        def _(dve):
            q = slice(0, sh.GP)
            dve.wait_ge(loaded, 16)
            nc.vector.tensor_copy(val[q, :], raw[q, :]).then_inc(cast, 1)
            dve.wait_ge(cast, 1)
            nc.vector.tensor_reduce(least[q, :], val[q, :].rearrange("p (f e) -> p f e", f=sh.GF), AX.X,
                                    ALU.min).then_inc(reduced, 1)
            nc.vector.tensor_scalar(low[q, :], val[q, :], float(SENTINEL), -2.0 * SENTINEL, ALU.is_ge,
                                    ALU.mult).then_inc(lowered, 1)
            dve.wait_ge(lowered, 1)
            nc.vector.tensor_tensor(low[q, :], low[q, :], val[q, :], ALU.add).then_inc(lowered, 1)
            dve.wait_ge(lowered, 2)
            nc.vector.tensor_reduce(most[q, :], low[q, :].rearrange("p (f e) -> p f e", f=sh.GF), AX.X,
                                    ALU.max).then_inc(reduced, 1)
            dve.wait_ge(reduced, 2)
            nc.vector.tensor_tensor(span[q, :], most[q, :], least[q, :], ALU.subtract).then_inc(spanned, 1)
            nc.vector.tensor_scalar(least[q, :], least[q, :], float(sh.LAST), None, ALU.min).then_inc(spanned, 1)
            dve.wait_ge(spanned, 2)
            nc.vector.tensor_copy(least_i[q, :], least[q, :]).then_inc(base_made, 1)
            nc.vector.tensor_reduce(span1[q, :], span[q, :], AX.X, ALU.max).then_inc(spanned, 1)
            dve.wait_ge(widest, 1)
            nc.vector.tensor_reduce(top[:, 0:1], turned[0:1, 0:sh.GP], AX.X, ALU.max).then_inc(topped, 1)
            dve.wait_ge(topped, 1)
            nc.vector.tensor_copy(windows[:, :], top[:, 0:1]).then_inc(topped, 1)
            dve.wait_ge(cols_in, 32)
            nc.vector.tensor_copy(dst_f[:, :], dst_i[:, :])
            dve.wait_ge(base_back, 16)
            nc.vector.tensor_copy(base_w[:, :], base_n[:, :])

        @block.tensor
        def _(pe):
            pe.wait_ge(made, 2)
            pe.wait_ge(spanned, 3)
            nc.tensor.transpose(turned[0:1, 0:sh.GP], span1[0:sh.GP, :], ident[0:sh.GP, 0:sh.GP]).then_inc(widest, 1)


def project(nc, sh, env):
    ident = env["ident"]
    with ExitStack() as c:
        def tile(name, shape, dt=F32):
            return c.enter_context(nc.sbuf_tensor(name, shape, dt))

        def psum(name, shape, dt=F32):
            return c.enter_context(nc.psum_tensor(name, shape, dt))

        sem = semaphores(nc, c)
        w_sb = tile("pj_w", [P, 3 * DIM])
        xt = tile("pj_x", [P, U2, DIM])
        stats = tile("pj_stats", [P, U2, 6])
        mv = tile("pj_mv", [P, U2, 2])
        root = tile("pj_root", [P, U2, 1])
        rstd = tile("pj_rstd", [P, U2, 1])
        hn = tile("pj_hn", [P, U2, DIM])
        ht = tile("pj_ht", [P, U2, DIM])
        kv = tile("pj_kv", [P, U2, 2 * DIM])
        qs = tile("pj_qs", [P, U2, DIM])
        rest = tile("pj_rest", [P, U2, DIM])
        q3 = tile("pj_q3", [P, U2, 3, DIM], BF16)
        h_ps = [psum(f"pj_hps{k}", [P, 512]) for k in range(U2)]
        p_ps = [psum(f"pj_pps{k}", [P, 512]) for k in range(U2)]
        w_in = sem("pj_w_in")
        x_in = [sem(f"pj_x_in{k}") for k in range(U2)]
        stat, aggr, rooted, std, normed, turned, relud, projected, kv_sb, q_sb = (
            sem("pj_" + s) for s in ("stat", "aggr", "rooted", "std", "normed", "turned", "relud", "projected", "kv_sb", "q_sb"))
        split = [sem(f"pj_split{i}") for i in range(5)]
        kv_out = [sem(f"pj_kv_out{k}") for k in range(U2)]
        q_out = [sem(f"pj_q_out{k}") for k in range(U2)]
        block = c.enter_context(nc.Block())

        @block.sync
        def _(sp):
            sp.dma_start(w_sb[:, :], env["wqkv"]).then_inc(w_in, 16)

            def load(s):
                s.freed(sp, normed, U2)
                sp.dma_start(xt[:, s.slot, :], env["x"][bass.ds(s.n * P, P), :]).then_inc(x_in[s.slot], 16)

            def store(s):
                sp.wait_ge(kv_sb, s.nth)
                sp.dma_start(env["kv_tab"][bass.ds(s.n * P, P), :], kv[:, s.slot, :]).then_inc(kv_out[s.slot], 16)
                sp.wait_ge(split[4], s.nth)
                sp.dma_start(env["q_tab"][bass.ds(s.n * P, P), :],
                             q3[:, s.slot, :, :].rearrange("p a d -> p (a d)")).then_inc(q_out[s.slot], 16)

            steps(sp, sh.TILES, U2, [(0, load), (2, store)])
            for k in range(U2):
                sp.wait_ge(kv_out[k], 16 * (sh.TILES // U2))
                sp.wait_ge(q_out[k], 16 * (sh.TILES // U2))

        @block.vector
        def _(dve):
            def norm(s):
                k = s.slot
                dve.wait_ge(x_in[k], 16 * s.use)
                nc.vector.bn_stats(stats[:, k, :], xt[:, k, :]).then_inc(stat, 1)
                dve.wait_ge(stat, s.nth)
                alone(dve)
                nc.vector.bn_aggr(mv[:, k, :], stats[:, k, :]).then_inc(aggr, 1)

            def apply_norm(s):
                k = s.slot
                dve.wait_ge(rooted, s.nth)
                nc.vector.reciprocal(rstd[:, k, :], root[:, k, :]).then_inc(std, 1)
                dve.wait_ge(std, s.nth)
                s.freed(dve, turned, U2)
                nc.vector.tensor_scalar(hn[:, k, :], xt[:, k, :], mv[:, k, 0:1], rstd[:, k, :], ALU.subtract,
                                        ALU.mult).then_inc(normed, 1)

            def split_q(s):
                k = s.slot
                dve.wait_ge(q_sb, s.nth)
                s.slot_freed(dve, q_out[k], 16)
                nc.vector.tensor_copy(q3[:, k, 0, :], qs[:, k, :]).then_inc(split[0], 1)
                dve.wait_ge(split[0], s.nth)
                nc.vector.tensor_tensor(rest[:, k, :], qs[:, k, :], q3[:, k, 0, :], ALU.subtract).then_inc(split[1], 1)
                dve.wait_ge(split[1], s.nth)
                nc.vector.tensor_copy(q3[:, k, 1, :], rest[:, k, :]).then_inc(split[2], 1)
                dve.wait_ge(split[2], s.nth)
                nc.vector.tensor_tensor(rest[:, k, :], rest[:, k, :], q3[:, k, 1, :],
                                        ALU.subtract).then_inc(split[3], 1)
                dve.wait_ge(split[3], s.nth)
                nc.vector.tensor_copy(q3[:, k, 2, :], rest[:, k, :]).then_inc(split[4], 1)

            steps(dve, sh.TILES, U2, [(0, norm), (1, apply_norm), (2, split_q)])

        @block.tensor
        def _(pe):
            pe.wait_ge(w_in, 16)

            def turn(s):
                pe.wait_ge(normed, s.nth)
                nc.tensor.transpose(h_ps[s.slot][:, 0:P], hn[:, s.slot, :], ident[:, :]).then_inc(turned, 1)

            def mul(s):
                pe.wait_ge(relud, s.nth)
                nc.tensor.matmul(p_ps[s.slot][:, 0:3 * DIM], ht[:, s.slot, :], w_sb[:, :], start=True,
                                 stop=True).then_inc(projected, 1)

            steps(pe, sh.TILES, U2, [(1, turn), (1, mul)])

        @block.scalar
        def _(act):
            def relu(s):
                act.wait_ge(turned, s.nth)
                nc.scalar.activation(ht[:, s.slot, :], h_ps[s.slot][:, 0:P], ACT.Relu).then_inc(relud, 1)

            def split_out(s):
                k = s.slot
                act.wait_ge(projected, s.nth)
                s.freed(act, split[1], U2)
                nc.scalar.activation(qs[:, k, :], p_ps[k][:, 0:DIM], ACT.Copy, scale=HC ** -0.5).then_inc(q_sb, 1)
                s.slot_freed(act, kv_out[k], 16)
                nc.scalar.activation(kv[:, k, :], p_ps[k][:, DIM:3 * DIM], ACT.Copy).then_inc(kv_sb, 1)

            def root_var(s):
                act.wait_ge(aggr, s.nth)
                s.freed(act, std, U2)
                nc.scalar.activation(root[:, s.slot, :], mv[:, s.slot, 1:2], ACT.Sqrt, bias=env["eps_t"][:, :]
                                     ).then_inc(rooted, 1)

            steps(act, sh.TILES, U2, [(0, root_var), (1, relu), (1, split_out)])


def start_pass(nc, dve, env, ready, changed):
    nc.vector.tensor_tensor(rel_view(env["dst_rel"]), rel_view(env["dst_f"]), base_view(env["base_w"]),
                            ALU.subtract).then_inc(changed, 1)
    nc.vector.tensor_copy(env["base_i"][:, :], env["base_w"][0:1, :]).then_inc(ready, 1)


def first_pass(nc, dve, env, base_n, base_in, ready, changed):
    dve.wait_ge(base_in, 16)
    nc.vector.tensor_copy(env["base_w"][:, :], base_n[:, :]).then_inc(changed, 1)
    dve.wait_ge(changed, 1)
    start_pass(nc, dve, env, ready, changed)


def next_pass(nc, dve, sh, env, ready, changed, w):
    nc.vector.tensor_scalar(env["base_w"][:, :], env["base_w"][:, :], float(W), float(sh.LAST), ALU.add,
                            ALU.min).then_inc(changed, 1)
    dve.wait_ge(changed, 2 * w + 3)
    start_pass(nc, dve, env, ready, changed)


def rel_view(t):
    return t[:, :].rearrange("p (s j g) -> p s j g", j=J, g=G)


def base_view(t):
    v = t[:, :].rearrange("p (s g) -> p s g", g=G).unsqueeze(2)
    return v.to_broadcast([P, v.shape[1], J, G])


def passes(eng, sh, env):
    widest = eng.value_load(env["windows"][0:1, 0:1], min_val=0, max_val=sh.N)
    return eng.Fori(0, widest // W + 1)


def bases(eng, sh, env, n):
    return [eng.value_load(env["base_i"][0:1, bass.ds(n * G + g, 1)], min_val=0, max_val=sh.LAST) for g in range(G)]


def one_hot(nc, dve, env, dest, n):
    rel = env["dst_rel"][:, bass.ds(n * C, C)].unsqueeze(2).to_broadcast([P, C, W])
    idx = env["iota_w"][:, :].unsqueeze(1).to_broadcast([P, C, W])
    return nc.vector.tensor_tensor(dest, rel, idx, ALU.is_equal)


def attend(nc, sh, env):
    ident, state, aux = env["ident"], env["state"], env["aux"]
    with ExitStack() as c:
        def tile(name, shape, dt=F32):
            return c.enter_context(nc.sbuf_tensor(name, shape, dt))

        def psum(name, shape, dt=F32):
            return c.enter_context(nc.psum_tensor(name, shape, dt))

        new = semaphores(nc, c)

        def sem(name):
            return new("at_" + name)

        identb = tile("at_identb", [P, P], BF16)
        sel_head = tile("at_sel_head", [G * HEADS, HEADS, P])
        sel_feat = tile("at_sel_feat", [HEADS, DIM])
        sel_aux = tile("at_sel_aux", [HEADS + 1, AUXROWS])
        diag = tile("at_diag", [P, G])
        we = tile("at_we", [P, G * HEADS])

        base_n = tile("at_base_n", [P, sh.GROUPS], I32)
        idx = tile("at_idx", [P, U4, C], U32)
        att = tile("at_attr", [P, U4, J, P])
        qd = tile("at_qd", [P, U4, G, 3, DIM], BF16)
        kv = tile("at_kv", [P, U4, C, 2 * DIM])
        hot = tile("at_hot", [P, U4, C, W])
        hot_t = tile("at_hot_t", [P, U4, J, P])
        hot_b = tile("at_hot_b", [P, U4, J, P], BF16)
        miss_b = tile("at_miss_b", [P, U4, J, P], BF16)
        prod = tile("at_prod", [P, C, DIM])
        qk = tile("at_qk", [P, C * HEADS])
        sc = tile("at_sc", [P, U4, J, G * HEADS])
        sct = tile("at_sct", [G * HEADS, U2, J, P])
        ml4 = tile("at_ml4", [P, J, HEADS])
        ml = tile("at_ml", [P, HEADS])
        mnew = tile("at_mnew", [HEADS, G, W])
        drop = tile("at_drop", [HEADS, G, W])
        scale = tile("at_scale", [HEADS + 1, G * W])
        md = tile("at_md", [P, G, HEADS])
        arg = tile("at_arg", [P, C * HEADS])
        ex = tile("at_ex", [P, U2, C, AUXROWS])
        msg = tile("at_msg", [P, U2, C, DIM])

        ps_hot = psum("at_ps_hot", [P, J, P])
        ps_qe = psum("at_ps_qe", [P, C, DIM])
        ps_bc = [psum(f"at_ps_bc{i}", [P, 4, P]) for i in range(2)]
        ps_sum = psum("at_ps_sum", [P, 512])
        ps_low = psum("at_ps_low", [P, 512])
        ps_me = psum("at_ps_me", [P, 512])
        sct_ps = ps_bc[0][0:G * HEADS, 0:J, :]
        mlt_ps = ps_bc[1][0:HEADS, 0, :]
        mt_ps = ps_bc[1][:, 1, 0:HEADS]
        bias_ps = ps_low[:, 0:64]
        sf_ps = ps_low[:, 128:256]
        sa_ps = ps_low[0:AUXROWS, 256:384]
        num_ps = ps_sum[:, 0:128]
        den_ps = ps_sum[0:AUXROWS, 128:256]
        me_ps = ps_me[:, 0:64]

        made, we_in, base_in, tables, changed = (sem(s) for s in ("made", "we_in", "base_in", "tables", "changed"))
        MADE = 17
        idx_in = [sem(f"idx_in{k}") for k in range(U4)]
        attr_in = [sem(f"attr_in{k}") for k in range(U4)]
        q_in = [sem(f"q_in{k}") for k in range(U4)]
        kv_in = [sem(f"kv_in{k}") for k in range(U4)]
        hot_made, hot_turned, hot_copied, bias_made, q_spread, prod_made, qk_made, sc_made = (
            sem(s) for s in ("hot_made", "hot_turned", "hot_copied", "bias_made", "q_spread",
                             "prod_made", "qk_made", "sc_made"))
        sc_turned, sct_made, ml_made, ml_turned, m_turned, md_made, m_spread = (
            sem(s) for s in ("sc_turned", "sct_made", "ml_made", "ml_turned", "m_turned", "md_made", "m_spread"))
        bc_made = [sem(f"bc_made{i}") for i in range(4)]
        bc_read = [sem(f"bc_read{i}") for i in range(4)]
        arg_made, arg_cut, ex_made, scale_made, scale_spread, msg_made, summed = (
            sem(s) for s in ("arg_made", "arg_cut", "ex_made", "scale_made", "scale_spread", "msg_made", "summed"))
        scaled = [sem(f"scaled{g}") for g in range(G)]
        added = [sem(f"added{g}") for g in range(G)]
        m_kept = [sem(f"m_kept{g}") for g in range(G)]
        drop_made = [sem(f"drop_made{g}") for g in range(G)]
        m_up = [sem(f"m_up{g}") for g in range(G)]
        block = c.enter_context(nc.Block())

        @block.sync
        def _(sp):
            sp.dma_start(base_n[:, :], env["base_tab"].unsqueeze(0).to_broadcast([P, sh.GROUPS])
                         ).then_inc(base_in, 16)
            sp.wait_ge(made, 8)
            for g in range(G):
                sp.dma_start(we[EDIM * g:EDIM * (g + 1), HEADS * g:HEADS * (g + 1)], env["wet"]).then_inc(we_in, 16)
            with passes(sp, sh, env) as w:
                sp.wait_ge(tables, w + 1)

                def load(s):
                    k = s.slot
                    s.slot_freed(sp, kv_in[k], 16 * C)
                    sp.dma_start(idx[:, k, :], env["src_blocks"][bass.ds(s.n, 1), :, :].squeeze(0)
                                 ).then_inc(idx_in[k], 16)
                    s.freed(sp, bias_made, U4)
                    sp.dma_start(att[:, k, :, :].rearrange("p j e -> p (j e)"),
                                 env["attr"][bass.ds(s.n, 1), :, :].squeeze(0)).then_inc(attr_in[k], 16)
                    s.freed(sp, q_spread, U4)
                    for g, b in enumerate(bases(sp, sh, env, s.n)):
                        sp.dma_start(qd[W * g:W * (g + 1), k, g, :, :].rearrange("p a d -> p (a d)"),
                                     env["q_tab"][bass.ds(b, W), :]).then_inc(q_in[k], 16)

                steps(sp, sh.BLOCKS, U4, [(0, load)], w)

        @block.gpsimd
        def _(pool):
            nc.gpsimd.memset(we[:, :], 0.0).then_inc(made, 1)
            nc.gpsimd.memset(qd[:, :, :, :, :], 0.0).then_inc(made, 1)
            nc.gpsimd.memset(ex[:, :, :, :], 0.0).then_inc(made, 1)
            nc.gpsimd.memset(sel_head[:, :, :], 0.0).then_inc(made, 1)
            nc.gpsimd.memset(sel_feat[:, :], 1.0).then_inc(made, 1)
            nc.gpsimd.memset(sel_aux[:, :], 0.0).then_inc(made, 1)
            nc.gpsimd.memset(diag[:, :], 1.0).then_inc(made, 1)
            nc.gpsimd.memset(scale[:, :], 1.0).then_inc(made, 1)
            pool.wait_ge(made, 8)
            nc.gpsimd.memset(ex[:, :, :, AUXN:AUXN + 1], 1.0).then_inc(made, 1)
            sv = sel_head[:, :, :].rearrange("p h (g w) -> p h g w", g=G)
            nc.gpsimd.affine_select(out=sv, in_=sv, compare_op=ALU.not_equal, fill=1.0, base=0,
                                    pattern=[[-1, HEADS], [-HEADS, G], [0, W]], channel_multiplier=1
                                    ).then_inc(made, 1)
            nc.gpsimd.affine_select(out=sel_feat[:, :], in_=sel_feat[:, :], compare_op=ALU.is_ge, fill=0.0, base=0,
                                    pattern=[[1, DIM]], channel_multiplier=-HC).then_inc(made, 1)
            nc.gpsimd.affine_select(out=sel_aux[0:HEADS, :], in_=sel_aux[0:HEADS, :], compare_op=ALU.not_equal,
                                    fill=1.0, base=AUXD, pattern=[[-1, AUXROWS]], channel_multiplier=1
                                    ).then_inc(made, 1)
            nc.gpsimd.affine_select(out=diag[:, :], in_=diag[:, :], compare_op=ALU.is_ge, fill=0.0, base=0,
                                    pattern=[[-W, G]], channel_multiplier=1).then_inc(made, 1)
            nc.gpsimd.tensor_scalar(identb[:, :], ident[:, :], BIG, None, ALU.mult).then_inc(made, 1)
            pool.wait_ge(made, 14)
            nc.gpsimd.affine_select(out=sel_feat[:, :], in_=sel_feat[:, :], compare_op=ALU.is_ge, fill=0.0,
                                    base=HC - 1, pattern=[[-1, DIM]], channel_multiplier=HC).then_inc(made, 1)
            nc.gpsimd.affine_select(out=sel_aux[:, :], in_=sel_aux[:, :], compare_op=ALU.not_equal, fill=1.0,
                                    base=AUXN - 1000 * HEADS, pattern=[[-1, AUXROWS]], channel_multiplier=1000
                                    ).then_inc(made, 1)
            nc.gpsimd.affine_select(out=diag[:, :], in_=diag[:, :], compare_op=ALU.is_ge, fill=0.0, base=W - 1,
                                    pattern=[[W, G]], channel_multiplier=-1).then_inc(made, 1)
            pool.wait_ge(made, MADE)
            with passes(pool, sh, env) as w:
                pool.wait_ge(tables, w + 1)

                def gather(s):
                    pool.wait_ge(idx_in[s.slot], 16 * s.use)
                    s.freed(pool, msg_made, U4)
                    alone(pool)
                    for ch in range(C):
                        nc.gpsimd.indirect_dma_start(
                            kv[:, s.slot, ch, :], None, env["kv_tab"],
                            bass.IndirectOffsetOnAxis(ap=idx[:, s.slot, ch:ch + 1], axis=0)
                        ).then_inc(kv_in[s.slot], 16)

                steps(pool, sh.BLOCKS, U4, [(0, gather)], w)

        @block.vector
        def _(dve):
            first_pass(nc, dve, env, base_n, base_in, tables, changed)
            dve.wait_ge(made, MADE)
            with passes(dve, sh, env) as w:
                dve.wait_ge(changed, 2 * w + 2)
                dve.wait_ge(tables, w + 1)

                def head_max(s):
                    for u in range(4):
                        dve.wait_ge(bc_made[u], s.nth)
                        nc.vector.tensor_reduce(ml4[:, u // 2, 4 * (u % 2):4 * (u % 2) + 4], ps_bc[u % 2][:, :, :],
                                                AX.X, ALU.max).then_inc(bc_read[u], 1)
                    for u in range(4):
                        dve.wait_ge(bc_read[u], s.nth)
                    nc.vector.tensor_tensor(ml[:, :], ml4[:, 0, :], ml4[:, 1, :], ALU.max).then_inc(ml_made, 1)

                def messages(s):
                    k = s.slot
                    dve.wait_ge(ex_made, s.nth)
                    e = ex[:, k % 2, :, AUXD:AUXD + HEADS].unsqueeze(3).to_broadcast([P, C, HEADS, HC])
                    v = kv[:, k, :, DIM:2 * DIM].rearrange("p c (h d) -> p c h d", h=HEADS)
                    nc.vector.tensor_tensor(msg[:, k % 2, :, :].rearrange("p c (h d) -> p c h d", h=HEADS), v, e,
                                            ALU.mult).then_inc(msg_made, 1)

                def raise_max(s):
                    dve.wait_ge(ml_turned, s.nth)
                    s.freed(dve, scale_made, 1)
                    alone(dve)
                    for g, b in enumerate(bases(dve, sh, env, s.n)):
                        run = aux[0:HEADS, bass.ds(b, W)]
                        if g:
                            dve.wait_ge(m_kept[g - 1], s.nth)
                        else:
                            s.freed(dve, m_kept[G - 1], 1)
                        nc.vector.tensor_tensor(mnew[:, g, :], run, mlt_ps[:, g * W:(g + 1) * W],
                                                ALU.max).then_inc(m_up[g], 1)
                        dve.wait_ge(m_up[g], s.nth)
                        nc.vector.tensor_tensor(drop[:, g, :], run, mnew[:, g, :], ALU.subtract
                                                ).then_inc(drop_made[g], 1)
                        dve.wait_ge(drop_made[g], s.nth)
                        nc.vector.tensor_tensor(run, run, mnew[:, g, :], ALU.max).then_inc(m_kept[g], 1)

                def hot_one(s):
                    one_hot(nc, dve, env, hot[:, s.slot, :, :], s.n).then_inc(hot_made, 1)

                def score(s):
                    k = s.slot
                    dve.wait_ge(kv_in[k], 16 * C * s.use)
                    dve.wait_ge(q_spread, s.nth)
                    nc.vector.tensor_tensor(prod[:, :, :], ps_qe[:, :, :], kv[:, k, :, 0:DIM],
                                            ALU.mult).then_inc(prod_made, 1)
                    dve.wait_ge(prod_made, s.nth)
                    nc.vector.tensor_reduce(qk[:, :], prod[:, :, :].rearrange("p c (h d) -> p (c h) d", h=HEADS),
                                            AX.X, ALU.add).then_inc(qk_made, 1)
                    dve.wait_ge(qk_made, s.nth)
                    dve.wait_ge(bias_made, s.nth)
                    if not (isinstance(s.n, int) and s.n < 2):
                        dve.wait_ge(scale_spread, s.nth - 2)
                    nc.vector.tensor_tensor(sc[:, k, :, :].rearrange("p j q -> p (j q)"), qk[:, :], bias_ps,
                                            ALU.add).then_inc(sc_made, 1)

                def spread_max(s):
                    dve.wait_ge(m_turned, s.nth)
                    nc.vector.tensor_tensor(md[:, :, :], mt_ps.unsqueeze(1).to_broadcast([P, G, HEADS]),
                                            diag[:, :].unsqueeze(2).to_broadcast([P, G, HEADS]),
                                            ALU.mult).then_inc(md_made, 1)

                def merge(s):
                    dve.wait_ge(summed, s.nth)
                    dve.wait_ge(scale_spread, s.nth)
                    alone(dve)
                    for g, b in enumerate(bases(dve, sh, env, s.n)):
                        q = slice(g * W, (g + 1) * W)
                        num = state[:, bass.ds(b, W)]
                        den = aux[AUXD:AUXROWS, bass.ds(b, W)]
                        if g:
                            dve.wait_ge(added[g - 1], 2 * s.nth)
                        elif not (isinstance(s.n, int) and s.n < 1):
                            dve.wait_ge(added[G - 1], 2 * (s.nth - 1))
                        nc.vector.tensor_tensor(num, num, sf_ps[:, q], ALU.mult).then_inc(scaled[g], 1)
                        nc.vector.tensor_tensor(den, den, sa_ps[AUXD:AUXROWS, q], ALU.mult).then_inc(scaled[g], 1)
                        dve.wait_ge(scaled[g], 2 * s.nth)
                        nc.vector.tensor_tensor(num, num, num_ps[:, q], ALU.add).then_inc(added[g], 1)
                        nc.vector.tensor_tensor(den, den, den_ps[AUXD:AUXROWS, q], ALU.add).then_inc(added[g], 1)

                def below_max(s):
                    dve.wait_ge(m_spread, s.nth)
                    s.freed(dve, ex_made, 1)
                    nc.vector.tensor_tensor(arg[:, :], sc[:, s.slot, :, :].rearrange("p j q -> p (j q)"), me_ps,
                                            ALU.subtract).then_inc(arg_made, 1)
                    dve.wait_ge(arg_made, s.nth)
                    nc.vector.tensor_scalar(arg[:, :], arg[:, :], 0.0, None, ALU.min).then_inc(arg_cut, 1)

                steps(dve, sh.BLOCKS, U4, [(2, head_max), (3, messages), (2, raise_max), (0, hot_one), (1, score),
                                           (2, spread_max), (3, merge), (2, below_max)], w)
                next_pass(nc, dve, sh, env, tables, changed, w)

        @block.tensor
        def _(pe):
            pe.wait_ge(made, MADE)
            pe.wait_ge(we_in, 16 * G)
            with passes(pe, sh, env) as w:
                pe.wait_ge(tables, w + 1)

                def spread_q(s):
                    k = s.slot
                    pe.wait_ge(hot_copied, 3 * s.nth)
                    pe.wait_ge(q_in[k], 16 * G * s.use)
                    s.freed(pe, prod_made, 1)
                    for j in range(J):
                        for part in range(3):
                            last = nc.tensor.matmul(ps_qe[:, G * j:G * (j + 1), :], hot_b[:, k, j, :],
                                                    qd[:, k, :, part, :], start=part == 0, stop=part == 2)
                    last.then_inc(q_spread, 1)

                def spread_scores(s):
                    k = s.slot
                    pe.wait_ge(sct_made, s.nth)
                    for u in range(4):
                        j, half = divmod(u, 2)
                        if u < 2:
                            s.freed(pe, bc_read[u + 2], 1)
                            if u == 1:
                                s.freed(pe, md_made, 1)
                        else:
                            pe.wait_ge(bc_read[u - 2], s.nth)
                        nc.tensor.matmul(ps_bc[u % 2][:, :, :], identb[:, :],
                                         miss_b[:, k, j, :].unsqueeze(1).to_broadcast([P, 4, P]),
                                         start=True, stop=False, skip_group_check=True)
                        for h in range(4):
                            last = nc.tensor.matmul(ps_bc[u % 2][:, h, :], sel_head[:, 4 * half + h, :],
                                                    sct[:, k % 2, j, :], start=False, stop=h == 3,
                                                    skip_group_check=True)
                        last.then_inc(bc_made[u], 1)

                def turn_block_max(s):
                    pe.wait_ge(ml_made, s.nth)
                    nc.tensor.transpose(mlt_ps, ml[:, :], ident[:, :]).then_inc(ml_turned, 1)

                def sum_up(s):
                    k = s.slot
                    pe.wait_ge(msg_made, s.nth)
                    for g in range(G):
                        q = slice(g * W, (g + 1) * W)
                        for j in range(J):
                            nc.tensor.matmul(num_ps[:, q], msg[:, k % 2, j * G + g, :], hot[:, k, j * G + g, :],
                                             start=j == 0, stop=j == J - 1)
                        for j in range(J):
                            last = nc.tensor.matmul(den_ps[:, q], ex[:, k % 2, j * G + g, :],
                                                    hot[:, k, j * G + g, :], start=j == 0, stop=j == J - 1)
                    last.then_inc(summed, 1)

                def turn_max(s):
                    pe.wait_ge(m_kept[G - 1], s.nth)
                    alone(pe)
                    nc.tensor.transpose(mt_ps, mnew[:, :, :].rearrange("h g w -> h (g w)"),
                                        ident[0:HEADS, 0:HEADS]).then_inc(m_turned, 1)

                def turn_hot(s):
                    pe.wait_ge(hot_made, s.nth)
                    if not (isinstance(s.n, int) and s.n < 1):
                        pe.wait_ge(hot_copied, 3 * (s.nth - 1))
                    for j in range(J):
                        last = nc.tensor.transpose(ps_hot[:, j, :], hot[:, s.slot, G * j:G * (j + 1), :].rearrange(
                            "p g w -> p (g w)"), ident[:, :])
                    last.then_inc(hot_turned, 1)

                def turn_scores(s):
                    pe.wait_ge(sc_made, s.nth)
                    s.freed(pe, bc_read[2], 1)
                    for j in range(J):
                        last = nc.tensor.transpose(sct_ps[:, j, :], sc[:, s.slot, j, :], ident[:, :])
                    last.then_inc(sc_turned, 1)

                def bias(s):
                    k = s.slot
                    pe.wait_ge(attr_in[k], 16 * s.use)
                    s.freed(pe, sc_made, 1)
                    if not (isinstance(s.n, int) and s.n < 3):
                        pe.wait_ge(added[G - 1], 2 * (s.nth - 3))
                    for j in range(J):
                        last = nc.tensor.matmul(bias_ps[:, j * 32:(j + 1) * 32], att[:, k, j, :], we[:, :],
                                                start=True, stop=True)
                    last.then_inc(bias_made, 1)

                def spread_m(s):
                    pe.wait_ge(md_made, s.nth)
                    for j in range(J):
                        last = nc.tensor.matmul(me_ps[:, j * 32:(j + 1) * 32], hot_t[:, s.slot, j, :],
                                                md[:, :, :].rearrange("p g h -> p (g h)"), start=True, stop=True)
                    last.then_inc(m_spread, 1)

                def spread_scale(s):
                    pe.wait_ge(scale_made, s.nth)
                    if not (isinstance(s.n, int) and s.n < 1):
                        pe.wait_ge(added[G - 1], 2 * (s.nth - 1))
                    nc.tensor.matmul(sf_ps, sel_feat[:, :], scale[0:HEADS, :], start=True, stop=True)
                    nc.tensor.matmul(sa_ps, sel_aux[:, :], scale[:, :], start=True, stop=True
                                     ).then_inc(scale_spread, 1)

                steps(pe, sh.BLOCKS, U4, [(1, spread_q), (2, spread_scores), (2, turn_block_max), (3, sum_up),
                                          (2, turn_max), (0, turn_hot), (1, turn_scores), (2, spread_m), (0, bias),
                                          (2, spread_scale)], w)

        @block.scalar
        def _(act):
            act.wait_ge(made, MADE)
            with passes(act, sh, env) as w:
                act.wait_ge(tables, w + 1)

                def scale_exp(s):
                    act.wait_ge(drop_made[G - 1], s.nth)
                    s.freed(act, scale_spread, 1)
                    nc.scalar.activation(scale[0:HEADS, :], drop[:, :, :].rearrange("h g w -> h (g w)"), ACT.Exp,
                                         bias=env["zero_t"][0:HEADS, :]).then_inc(scale_made, 1)

                def copy_hot(s):
                    k = s.slot
                    act.wait_ge(hot_turned, s.nth)
                    nc.scalar.activation(hot_b[:, k, :, :], ps_hot[:, :, :], ACT.Copy).then_inc(hot_copied, 1)
                    nc.scalar.activation(hot_t[:, k, :, :], ps_hot[:, :, :], ACT.Copy).then_inc(hot_copied, 1)
                    nc.scalar.activation(miss_b[:, k, :, :], ps_hot[:, :, :], ACT.Identity, bias=env["neg1_t"][:, :]
                                         ).then_inc(hot_copied, 1)

                def copy_scores(s):
                    act.wait_ge(sc_turned, s.nth)
                    s.freed(act, bc_made[3], 2)
                    nc.scalar.activation(sct[:, s.slot % 2, :, :], sct_ps, ACT.Copy).then_inc(sct_made, 1)

                def exp(s):
                    act.wait_ge(arg_cut, s.nth)
                    s.freed(act, summed, 2)
                    nc.scalar.activation(ex[:, s.slot % 2, :, AUXD:AUXD + HEADS],
                                         arg[:, :].rearrange("p (c h) -> p c h", h=HEADS), ACT.Exp,
                                         bias=env["zero_t"][:, :]).then_inc(ex_made, 1)

                steps(act, sh.BLOCKS, U4, [(2, scale_exp), (0, copy_hot), (1, copy_scores), (2, exp)], w)


def normalise(nc, sh, env):
    ident, state, aux = env["ident"], env["state"], env["aux"]
    with ExitStack() as c:
        def tile(name, shape, dt=F32):
            return c.enter_context(nc.sbuf_tensor("nm_" + name, shape, dt))

        def psum(name, shape, dt=F32):
            return c.enter_context(nc.psum_tensor("nm_" + name, shape, dt))

        new = semaphores(nc, c)

        def sem(name):
            return new("nm_" + name)

        T = CH // P
        pick_den = tile("pick_den", [AUXROWS, DIM])
        pick_deg = tile("pick_deg", [AUXROWS, DIM])
        xt = tile("xt", [P, U2, T, DIM])
        inv = tile("inv", [P, U2, CH])
        sq = tile("sq", [P, U2, CH])
        x1 = tile("x1", [P, U2, T, DIM])
        stats = tile("stats", [P, U2, T, 6])
        mv = tile("mv", [P, U2, T, 2])
        root = tile("root", [P, U2, T])
        rstd = tile("rstd", [P, U2, T])
        hn = tile("hn", [P, U2, T, DIM])
        ht = tile("ht", [P, U2, CH])
        gs = tile("gs", [P, U2, CH])
        row = tile("row", [P, U2, T, DIM])
        den_ps, deg_ps, at_ps, ht_ps, row_ps = (psum(s, [P, CH]) for s in ("den", "deg", "at", "ht_ps", "row_ps"))
        (made, state_made, var_rooted, spread, den_cut, inverted, rooted, degd, attd, at_turned, x1_made, stat, aggr, std, normed, h_turned,
         relud, g_made, row_turned, row_made) = (sem(s) for s in (
             "made", "state_made", "var_rooted", "spread", "den_cut", "inverted", "rooted", "degd", "attd", "at_turned", "x1_made", "stat", "aggr",
             "std", "normed", "h_turned", "relud", "g_made", "row_turned", "row_made"))
        x_in = [sem(f"x_in{k}") for k in range(U2)]
        x1_out = [sem(f"x1_out{k}") for k in range(U2)]
        row_out = [sem(f"row_out{k}") for k in range(U2)]
        block = c.enter_context(nc.Block())
        width = chunk_width(sh)

        @block.sync
        def _(sp):
            def load(s):
                cw = width(s.n)
                s.freed(sp, x1_made, U2)
                sp.dma_start(xt[:, s.slot, 0:cw // P, :], rows_of(env["x"], s.n, cw)).then_inc(x_in[s.slot], 16)

            def store(s):
                cw = width(s.n)
                sp.wait_ge(x1_made, s.nth)
                sp.dma_start(rows_of(env["x1_tab"], s.n, cw), x1[:, s.slot, 0:cw // P, :]
                             ).then_inc(x1_out[s.slot], 16)
                sp.wait_ge(row_made, s.nth)
                sp.dma_start(rows_of(env["g_tabs"][0], s.n, cw), row[:, s.slot, 0:cw // P, :]
                             ).then_inc(row_out[s.slot], 16)

            steps(sp, sh.CHUNKS, U2, [(0, load), (2, store)])
            for k in range(U2):
                uses = len(range(k, sh.CHUNKS, U2))
                sp.wait_ge(x1_out[k], 16 * uses)
                sp.wait_ge(row_out[k], 16 * uses)

        @block.gpsimd
        def _(pool):
            nc.gpsimd.memset(pick_den[:, :], 1.0).then_inc(made, 1)
            nc.gpsimd.memset(pick_deg[:, :], 0.0).then_inc(made, 1)
            pool.wait_ge(made, 2)
            nc.gpsimd.affine_select(out=pick_den[:, :], in_=pick_den[:, :], compare_op=ALU.is_ge, fill=0.0,
                                    base=HC * AUXD, pattern=[[1, DIM]], channel_multiplier=-HC).then_inc(made, 1)
            nc.gpsimd.affine_select(out=pick_deg[:, :], in_=pick_deg[:, :], compare_op=ALU.not_equal, fill=1.0,
                                    base=-AUXN, pattern=[[0, DIM]], channel_multiplier=1).then_inc(made, 1)
            pool.wait_ge(made, 4)
            nc.gpsimd.affine_select(out=pick_den[:, :], in_=pick_den[:, :], compare_op=ALU.is_ge, fill=0.0,
                                    base=HC - 1 - HC * AUXD, pattern=[[-1, DIM]], channel_multiplier=HC
                                    ).then_inc(made, 1)

        @block.vector
        def _(dve):
            def attention(s):
                k, cw = s.slot, width(s.n)
                cols = bass.ds(s.n * CH, cw)
                dve.wait_ge(spread, s.nth)
                s.freed(dve, at_turned, U2)
                nc.vector.tensor_scalar(inv[:, k, 0:cw], den_ps[:, 0:cw], 0.5, None, ALU.max).then_inc(den_cut, 1)
                dve.wait_ge(den_cut, s.nth)
                nc.vector.reciprocal(inv[:, k, 0:cw], inv[:, k, 0:cw]).then_inc(inverted, 1)
                dve.wait_ge(inverted, s.nth)
                nc.vector.tensor_tensor(inv[:, k, 0:cw], state[:, cols], inv[:, k, 0:cw], ALU.mult).then_inc(attd, 1)
                dve.wait_ge(rooted, s.nth)
                nc.vector.reciprocal(aux[:, cols], sq[:, k, 0:cw]).then_inc(degd, 1)

            def layernorm(s):
                k, cw = s.slot, width(s.n)
                t = cw // P
                dve.wait_ge(at_turned, s.nth)
                dve.wait_ge(x_in[k], 16 * s.use)
                s.slot_freed(dve, x1_out[k], 16)
                nc.vector.tensor_tensor(x1[:, k, 0:t, :], at_ps[:, 0:cw].rearrange("p (t d) -> p t d", d=DIM),
                                        xt[:, k, 0:t, :], ALU.add).then_inc(x1_made, 1)
                dve.wait_ge(x1_made, s.nth)
                for i in range(t):
                    last = nc.vector.bn_stats(stats[:, k, i, :], x1[:, k, i, :])
                last.then_inc(stat, 1)
                dve.wait_ge(stat, s.nth)
                alone(dve)
                for i in range(t):
                    last = nc.vector.bn_aggr(mv[:, k, i, :], stats[:, k, i, :])
                last.then_inc(aggr, 1)

            def apply_norm(s):
                k = s.slot
                t = width(s.n) // P
                dve.wait_ge(var_rooted, s.nth)
                nc.vector.reciprocal(rstd[:, k, 0:t], root[:, k, 0:t]).then_inc(std, 1)
                dve.wait_ge(std, s.nth)
                s.freed(dve, h_turned, U2)
                for i in range(t):
                    last = nc.vector.tensor_scalar(hn[:, k, i, :], x1[:, k, i, :], mv[:, k, i, 0:1],
                                                   rstd[:, k, i:i + 1], ALU.subtract, ALU.mult)
                last.then_inc(normed, 1)

            def scale_h(s):
                k, cw = s.slot, width(s.n)
                cols = bass.ds(s.n * CH, cw)
                dve.wait_ge(relud, s.nth)
                dve.wait_ge(degd, s.nth)
                s.freed(dve, row_turned, U2)
                s.freed(dve, state_made, U2)
                nc.vector.tensor_tensor(gs[:, k, 0:cw], ht[:, k, 0:cw], aux[:, cols], ALU.mult).then_inc(g_made, 1)

            steps(dve, sh.CHUNKS, U2, [(0, attention), (0, layernorm), (1, apply_norm), (2, scale_h)])

        @block.tensor
        def _(pe):
            pe.wait_ge(made, 5)

            def spread_aux(s):
                cw = width(s.n)
                cols = bass.ds(s.n * CH, cw)
                s.freed(pe, den_cut, 1)
                s.freed(pe, rooted, 1)
                nc.tensor.matmul(den_ps[:, 0:cw], pick_den[:, :], aux[0:AUXROWS, cols], start=True, stop=True)
                nc.tensor.matmul(deg_ps[:, 0:cw], pick_deg[:, :], aux[0:AUXROWS, cols], start=True, stop=True
                                 ).then_inc(spread, 1)

            def turn_att(s):
                cw = width(s.n)
                pe.wait_ge(attd, s.nth)
                s.freed(pe, x1_made, 1)
                for i in range(cw // P):
                    last = nc.tensor.transpose(at_ps[:, i * P:(i + 1) * P], inv[:, s.slot, i * P:(i + 1) * P],
                                               ident[:, :])
                last.then_inc(at_turned, 1)

            def turn_h(s):
                cw = width(s.n)
                pe.wait_ge(normed, s.nth)
                s.freed(pe, relud, 1)
                for i in range(cw // P):
                    last = nc.tensor.transpose(ht_ps[:, i * P:(i + 1) * P], hn[:, s.slot, i, :], ident[:, :])
                last.then_inc(h_turned, 1)

            def turn_row(s):
                cw = width(s.n)
                pe.wait_ge(g_made, s.nth)
                s.freed(pe, row_made, 1)
                for i in range(cw // P):
                    last = nc.tensor.transpose(row_ps[:, i * P:(i + 1) * P], gs[:, s.slot, i * P:(i + 1) * P],
                                               ident[:, :])
                last.then_inc(row_turned, 1)

            steps(pe, sh.CHUNKS, U2, [(0, spread_aux), (0, turn_att), (1, turn_h), (2, turn_row)])

        @block.scalar
        def _(act):
            def root_deg(s):
                k, cw = s.slot, width(s.n)
                act.wait_ge(spread, s.nth)
                s.freed(act, degd, U2)
                nc.scalar.activation(sq[:, k, 0:cw], deg_ps[:, 0:cw], ACT.Sqrt, bias=env["one_t"][:, :]
                                     ).then_inc(rooted, 1)

            def relu(s):
                k, cw = s.slot, width(s.n)
                act.wait_ge(h_turned, s.nth)
                s.freed(act, g_made, U2)
                nc.scalar.activation(ht[:, k, 0:cw], ht_ps[:, 0:cw], ACT.Relu).then_inc(relud, 1)

            def copy_row(s):
                k, cw = s.slot, width(s.n)
                act.wait_ge(row_turned, s.nth)
                s.slot_freed(act, row_out[k], 16)
                nc.scalar.activation(row[:, k, 0:cw // P, :].rearrange("p t d -> p (t d)"), row_ps[:, 0:cw],
                                     ACT.Copy).then_inc(row_made, 1)

            def copy_state(s):
                cw = width(s.n)
                act.wait_ge(g_made, s.nth)
                act.wait_ge(attd, s.nth)
                nc.scalar.activation(state[:, bass.ds(s.n * CH, cw)], gs[:, s.slot, 0:cw], ACT.Copy
                                     ).then_inc(state_made, 1)

            def root_var(s):
                k, t = s.slot, width(s.n) // P
                act.wait_ge(aggr, s.nth)
                s.freed(act, std, U2)
                nc.scalar.activation(root[:, k, 0:t], mv[:, k, 0:t, 1:2].rearrange("p t o -> p (t o)"), ACT.Sqrt,
                                     bias=env["eps_t"][:, :]).then_inc(var_rooted, 1)

            steps(act, sh.CHUNKS, U2, [(0, root_deg), (0, root_var), (1, relu), (2, copy_state), (2, copy_row)])


def chunk_width(sh):
    return lambda n: sh.LW if isinstance(n, int) and n == sh.CHUNKS - 1 else CH


def rows_of(tab, n, cw):
    return tab[bass.ds(n * CH, cw), :].rearrange("(t p) d -> p t d", p=P)


def aggregate(nc, sh, layer, env):
    state = env["state"]
    with ExitStack() as c:
        def tile(name, shape, dt=F32):
            return c.enter_context(nc.sbuf_tensor(f"ag{layer}_{name}", shape, dt))

        new = semaphores(nc, c)

        def sem(name):
            return new(f"ag{layer}_{name}")

        idx = tile("idx", [P, U4, C], U32)
        rows = tile("rows", [P, U4, C, DIM])
        hot = tile("hot", [P, U4, C, W])
        base_n = tile("base_n", [P, sh.GROUPS], I32)
        sum_ps = [c.enter_context(nc.psum_tensor(f"ag{layer}_sum{k}", [P, 512], F32)) for k in range(2)]
        base_in, tables, changed, hot_made, summed = (sem(s) for s in (
            "base_in", "tables", "changed", "hot_made", "summed"))
        idx_in = [sem(f"idx_in{k}") for k in range(U4)]
        rows_in = [sem(f"rows_in{k}") for k in range(U4)]
        added = [sem(f"added{g}") for g in range(G)]
        block = c.enter_context(nc.Block())

        @block.sync
        def _(sp):
            sp.dma_start(base_n[:, :], env["base_tab"].unsqueeze(0).to_broadcast([P, sh.GROUPS])
                         ).then_inc(base_in, 16)
            with passes(sp, sh, env) as w:
                sp.wait_ge(tables, w + 1)

                def load(s):
                    s.slot_freed(sp, rows_in[s.slot], 16 * C)
                    sp.dma_start(idx[:, s.slot, :], env["src_blocks"][bass.ds(s.n, 1), :, :].squeeze(0)
                                 ).then_inc(idx_in[s.slot], 16)

                steps(sp, sh.BLOCKS, U4, [(0, load)], w)

        @block.gpsimd
        def _(pool):
            with passes(pool, sh, env) as w:
                pool.wait_ge(tables, w + 1)

                def gather(s):
                    pool.wait_ge(idx_in[s.slot], 16 * s.use)
                    s.freed(pool, summed, U4)
                    alone(pool)
                    for ch in range(C):
                        nc.gpsimd.indirect_dma_start(
                            rows[:, s.slot, ch, :], None, env["g_tabs"][layer],
                            bass.IndirectOffsetOnAxis(ap=idx[:, s.slot, ch:ch + 1], axis=0)
                        ).then_inc(rows_in[s.slot], 16)

                steps(pool, sh.BLOCKS, U4, [(0, gather)], w)

        @block.vector
        def _(dve):
            first_pass(nc, dve, env, base_n, base_in, tables, changed)
            with passes(dve, sh, env) as w:
                dve.wait_ge(changed, 2 * w + 2)
                dve.wait_ge(tables, w + 1)

                def hot_one(s):
                    s.freed(dve, summed, U4)
                    one_hot(nc, dve, env, hot[:, s.slot, :, :], s.n).then_inc(hot_made, 1)

                def merge(s):
                    dve.wait_ge(summed, s.nth)
                    alone(dve)
                    for g, b in enumerate(bases(dve, sh, env, s.n)):
                        into = state[:, bass.ds(b, W)]
                        if g:
                            dve.wait_ge(added[g - 1], s.nth)
                        else:
                            s.freed(dve, added[G - 1], 1)
                        nc.vector.tensor_tensor(into, into, sum_ps[s.slot % 2][:, g * W:(g + 1) * W],
                                                ALU.add).then_inc(added[g], 1)

                steps(dve, sh.BLOCKS, U4, [(0, hot_one), (1, merge)], w)
                next_pass(nc, dve, sh, env, tables, changed, w)

        @block.tensor
        def _(pe):
            with passes(pe, sh, env) as w:
                pe.wait_ge(tables, w + 1)

                def sum_up(s):
                    k = s.slot
                    pe.wait_ge(rows_in[k], 16 * C * s.use)
                    pe.wait_ge(hot_made, s.nth)
                    s.freed(pe, added[G - 1], 2)
                    for g in range(G):
                        for j in range(J):
                            last = nc.tensor.matmul(sum_ps[k % 2][:, g * W:(g + 1) * W], rows[:, k, j * G + g, :],
                                                    hot[:, k, j * G + g, :], start=j == 0, stop=j == J - 1)
                    last.then_inc(summed, 1)

                steps(pe, sh.BLOCKS, U4, [(0, sum_up)], w)


def transform(nc, sh, layer, env):
    ident, state, dinv, vec = env["ident"], env["state"], env["aux"], env["vec_t"]
    w1, w2, w3 = env["weights"]
    with ExitStack() as c:
        def tile(name, shape, dt=F32):
            return c.enter_context(nc.sbuf_tensor(f"tr{layer}_{name}", shape, dt))

        new = semaphores(nc, c)

        def sem(name):
            return new(f"tr{layer}_{name}")

        T = CH // P
        halves = 2 if layer == 0 else 1
        at = (0, 6, 9)[layer]
        act_fn = ACT.Identity if layer == 2 else ACT.Relu
        r = tile("r", [P, U2, 2, CH]) if layer == 0 else None
        gs = tile("gs", [P, U2, CH])
        hb = tile("hb", [P, U2, halves, CH])
        stats = tile("stats", [P, 2, sh.CHUNKS, 6])
        mv = tile("mv", [P, 2, 2])
        root = tile("root", [P, 2])
        gain = tile("gain", [P, 2])
        shift = tile("shift", [P, 2])
        row = tile("row", [P, U2, T, DIM])
        x1 = tile("x1", [P, U2, T, DIM])
        z_ps = [[c.enter_context(nc.psum_tensor(f"tr{layer}_z{k}{h}", [P, CH], F32)) for h in range(2)]
                for k in range(2)] if layer == 0 else None
        o_ps = c.enter_context(nc.psum_tensor(f"tr{layer}_o", [P, CH], F32))
        row_ps = c.enter_context(nc.psum_tensor(f"tr{layer}_rowps", [P, CH], F32))
        (w_in, scaled, z_made, r_made, stat, aggr, std, gained, shifting, shifted, z2_made, r2_made, h_made, o_made,
         g_made, row_turned, row_made, rooted, state_made) = (sem(s) for s in (
             "w_in", "scaled", "z_made", "r_made", "stat", "aggr", "std", "gained", "shifting", "shifted", "z2_made",
             "r2_made", "h_made", "o_made", "g_made", "row_turned", "row_made", "rooted",
             "state_made"))
        x_in = [sem(f"x_in{k}") for k in range(U2)]
        row_out = [sem(f"row_out{k}") for k in range(U2)]
        block = c.enter_context(nc.Block())
        width = chunk_width(sh)
        dest = env["out"] if layer == 2 else env["g_tabs"][layer + 1]

        def cols_of(s):
            return bass.ds(s.n * CH, width(s.n))

        @block.sync
        def _(sp):
            if layer == 0:
                sp.dma_start(w1[:, :, :].rearrange("p a d -> p (a d)"), env["w1"]).then_inc(w_in, 16)
                sp.dma_start(w2[:, :, :], env["w2"].rearrange("(a p) d -> p a d", p=P)).then_inc(w_in, 16)
                sp.dma_start(w3[:, :], env["w3"]).then_inc(w_in, 16)

            def load(s):
                if layer == 2:
                    s.freed(sp, row_made, U2)
                    sp.dma_start(x1[:, s.slot, 0:width(s.n) // P, :], rows_of(env["x1_tab"], s.n, width(s.n))
                                 ).then_inc(x_in[s.slot], 16)

            def store(s):
                sp.wait_ge(row_made, s.nth)
                sp.dma_start(rows_of(dest, s.n, width(s.n)), row[:, s.slot, 0:width(s.n) // P, :]
                             ).then_inc(row_out[s.slot], 16)

            steps(sp, sh.CHUNKS, U2, [(0, load), (1, store)])
            for k in range(U2):
                sp.wait_ge(row_out[k], 16 * len(range(k, sh.CHUNKS, U2)))

        @block.vector
        def _(dve):
            def scale(s):
                nc.vector.tensor_tensor(state[:, cols_of(s)], state[:, cols_of(s)], dinv[:, cols_of(s)],
                                        ALU.mult).then_inc(scaled, 1)

            def statistics(s):
                cv = sh.LV if width(s.n) != CH or (isinstance(s.n, int) and s.n == sh.CHUNKS - 1) else CH
                dve.wait_ge(r_made, halves * s.nth)
                for h in range(halves):
                    src = r[:, s.slot, h, 0:cv] if layer == 0 else state[:, bass.ds(s.n * CH, cv)]
                    last = nc.vector.bn_stats(stats[:, h, bass.ds(s.n, 1), :].rearrange("p a b -> p (a b)"), src)
                last.then_inc(stat, 1)

            steps(dve, sh.CHUNKS, U2, [(0, scale), (1, statistics)])
            dve.wait_ge(stat, sh.CHUNKS)
            for h in range(halves):
                nc.vector.bn_aggr(mv[:, h, :], stats[:, h, :, :].rearrange("p a b -> p (a b)")).then_inc(aggr, 1)
            dve.wait_ge(aggr, halves)
            hs = slice(0, halves)
            dve.wait_ge(rooted, 1)
            nc.vector.reciprocal(gain[:, hs], root[:, hs]).then_inc(std, 1)
            dve.wait_ge(std, 1)
            nc.vector.tensor_tensor(gain[:, hs], gain[:, hs], vec[:, at + halves:at + 2 * halves],
                                    ALU.mult).then_inc(gained, 1)
            dve.wait_ge(gained, 1)
            nc.vector.tensor_tensor(shift[:, hs], mv[:, hs, 0:1].rearrange("p h o -> p (h o)"), gain[:, hs],
                                    ALU.mult).then_inc(shifting, 1)
            dve.wait_ge(shifting, 1)
            nc.vector.tensor_tensor(shift[:, hs], vec[:, at + 2 * halves:at + 3 * halves], shift[:, hs],
                                    ALU.subtract).then_inc(shifted, 1)
            dve.wait_ge(shifted, 1)

            def normed(s):
                cw = width(s.n)
                if layer == 0:
                    dve.wait_ge(r2_made, 2 * s.nth)
                s.freed(dve, o_made if layer < 2 else row_turned, U2)
                for h in range(halves):
                    src = r[:, s.slot, h, 0:cw] if layer == 0 else state[:, cols_of(s)]
                    last = nc.vector.tensor_scalar(hb[:, s.slot, h, 0:cw], src, gain[:, h:h + 1], shift[:, h:h + 1],
                                                   ALU.mult, ALU.add)
                last.then_inc(h_made, 1)

            def table(s):
                k, cw = s.slot, width(s.n)
                if layer < 2:
                    dve.wait_ge(o_made, s.nth)
                    s.freed(dve, row_turned, U2)
                    s.freed(dve, state_made, U2)
                    nc.vector.tensor_tensor(gs[:, k, 0:cw], o_ps[:, 0:cw], dinv[:, cols_of(s)],
                                            ALU.mult).then_inc(g_made, 1)
                else:
                    dve.wait_ge(row_turned, s.nth)
                    dve.wait_ge(x_in[k], 16 * s.use)
                    s.slot_freed(dve, row_out[k], 16)
                    nc.vector.tensor_tensor(row[:, k, 0:cw // P, :].rearrange("p t d -> p (t d)"), row_ps[:, 0:cw],
                                            x1[:, k, 0:cw // P, :].rearrange("p t d -> p (t d)"),
                                            ALU.add).then_inc(row_made, 1)

            steps(dve, sh.CHUNKS, U2, [(0, normed), (1, table)])

        @block.tensor
        def _(pe):
            def before(freed_by, made):
                def run(s):
                    cw = width(s.n)
                    pe.wait_ge(scaled, s.nth)
                    if not (isinstance(s.n, int) and s.n < U2):
                        pe.wait_ge(freed_by, 2 * (s.nth - U2))
                    for h in range(2):
                        last = nc.tensor.matmul(z_ps[s.slot][h][:, 0:cw], w1[:, h, :], state[:, cols_of(s)],
                                                start=True, stop=True)
                    last.then_inc(made, 1)
                return run

            def after(s):
                k, cw = s.slot, width(s.n)
                pe.wait_ge(h_made, s.nth)
                s.freed(pe, g_made, 1)
                for h in range(halves):
                    last = nc.tensor.matmul(o_ps[:, 0:cw], w2[:, h, :] if layer == 0 else w3[:, :],
                                            hb[:, k, h, 0:cw], start=h == 0, stop=h == halves - 1)
                last.then_inc(o_made, 1)

            def turn(s):
                cw = width(s.n)
                pe.wait_ge(g_made if layer < 2 else h_made, s.nth)
                s.freed(pe, row_made, 1)
                for i in range(cw // P):
                    src = gs[:, s.slot, i * P:(i + 1) * P] if layer < 2 else hb[:, s.slot, 0, i * P:(i + 1) * P]
                    last = nc.tensor.transpose(row_ps[:, i * P:(i + 1) * P], src, ident[:, :])
                last.then_inc(row_turned, 1)

            if layer == 0:
                pe.wait_ge(w_in, 48)
                steps(pe, sh.CHUNKS, U2, [(0, before(r_made, z_made))])
                pe.wait_ge(r_made, 2 * sh.CHUNKS)
                steps(pe, sh.CHUNKS, U2, [(0, before(r2_made, z2_made)), (0, after), (1, turn)])
            elif layer == 1:
                steps(pe, sh.CHUNKS, U2, [(0, after), (1, turn)])
            else:
                steps(pe, sh.CHUNKS, U2, [(0, turn)])

        @block.scalar
        def _(act):
            def nonlinear(made_by, made, used_by):
                def run(s):
                    k, cw = s.slot, width(s.n)
                    act.wait_ge(made_by, s.nth)
                    if layer == 0:
                        s.freed(act, used_by, U2)
                    for h in range(halves):
                        src = z_ps[k][h][:, 0:cw] if layer == 0 else state[:, cols_of(s)]
                        to = r[:, k, h, 0:cw] if layer == 0 else state[:, cols_of(s)]
                        nc.scalar.activation(to, src, act_fn, bias=vec[:, at + h:at + h + 1]).then_inc(made, 1)
                return run

            def copy_row(s):
                k, cw = s.slot, width(s.n)
                act.wait_ge(row_turned, s.nth)
                s.slot_freed(act, row_out[k], 16)
                nc.scalar.activation(row[:, k, 0:cw // P, :].rearrange("p t d -> p (t d)"), row_ps[:, 0:cw],
                                     ACT.Copy).then_inc(row_made, 1)

            def copy_state(s):
                act.wait_ge(g_made, s.nth)
                nc.scalar.activation(state[:, cols_of(s)], gs[:, s.slot, 0:width(s.n)], ACT.Copy
                                     ).then_inc(state_made, 1)

            steps(act, sh.CHUNKS, U2, [(0, nonlinear(z_made if layer == 0 else scaled, r_made, stat))])
            act.wait_ge(aggr, halves)
            nc.scalar.activation(root[:, 0:halves], mv[:, 0:halves, 1:2].rearrange("p h o -> p (h o)"), ACT.Sqrt,
                                 bias=env["eps_t"][:, :]).then_inc(rooted, 1)
            if layer == 0:
                steps(act, sh.CHUNKS, U2, [(0, nonlinear(z2_made, r2_made, h_made)), (1, copy_state), (1, copy_row)])
            elif layer == 1:
                steps(act, sh.CHUNKS, U2, [(0, copy_state), (0, copy_row)])


def kernel(**inputs):
    import numpy as np
    import concourse.bacc as bacc
    from concourse.bass_utils import run_bass_kernel_spmd

    a = {k: np.asarray(v) for k, v in inputs.items()}
    n_nodes, n_edges = a["x"].shape[0], a["src"].shape[0]
    sh = Shapes(n_nodes, n_edges)
    pad = sh.BLOCKS * BLOCK - n_edges

    def by_chunk(v, fill):
        v = np.concatenate([v, np.full(pad, fill, v.dtype)]).reshape(sh.BLOCKS, G, J, P)
        return v.transpose(3, 0, 2, 1).reshape(P, sh.BLOCKS, C)

    dst = np.concatenate([a["dst"], np.full(pad, SENTINEL, a["dst"].dtype)])
    attr = np.concatenate([a["edge_attr_32"], np.zeros((pad, EDIM), a["edge_attr_32"].dtype)])
    attr = attr.reshape(sh.BLOCKS, G, J, P, EDIM).transpose(0, 1, 4, 2, 3).reshape(sh.BLOCKS, P, J * P)

    def halves(name):
        return a[name].reshape(-1, P).T

    arrays = {
        "x": np.concatenate([a["x"], np.zeros((sh.NS - n_nodes, DIM), a["x"].dtype)]),
        "src_blocks": by_chunk(a["src"], 0).transpose(1, 0, 2).view(np.uint32),
        "dst_cols": by_chunk(a["dst"], SENTINEL).reshape(P, -1),
        "dst_groups": dst.reshape(sh.GP, -1),
        "attr": attr,
        "wqkv": np.concatenate([a["L0_gnn_Wq"].T, a["L0_gnn_Wk"].T, a["L0_gnn_Wv"].T], 1),
        "wet": a["L0_gnn_We"].T,
        "w1": a["L1_gnn_W1"], "w2": a["L1_gnn_W2"], "w3": a["L1_gnn_W3"],
        "vecs": np.concatenate([halves(f"L1_gnn_{v}{i}") for i in (1, 2, 3) for v in ("b", "g", "beta")], 1),
    }
    arrays = {k: np.ascontiguousarray(v) for k, v in arrays.items()}
    nc = bacc.Bacc("TRN2", target_bir_lowering=False, num_devices=1)
    args = [nc.dram_tensor(k, v.shape, mybir.dt.from_np(v.dtype), kind="ExternalInput").ap()
            for k, v in arrays.items()]
    out = nc.dram_tensor("out", (sh.NS, DIM), F32, kind="ExternalOutput").ap()
    build(nc, sh, *args, out)
    result = run_bass_kernel_spmd(nc, [arrays], core_ids=[0])
    return result.results[0]["out"][:n_nodes]
```

```python
from contextlib import ExitStack

import concourse.bass as bass
from concourse import mybir

ALU = mybir.AluOpType
ACT = mybir.ActivationFunctionType
AX = mybir.AxisListType
F32 = mybir.dt.float32
BF16 = mybir.dt.bfloat16
I32 = mybir.dt.int32
U32 = mybir.dt.uint32

P = 128
W = 32
G = 4
J = 2
C = G * J
BLOCK = C * P
HEADS = 8
HC = 16
DIM = HEADS * HC
EDIM = 32
CH = 512
SENTINEL = 1 << 20
BIG = float(2 ** 100)
EPS = 1e-5
AUXD = 64
AUXN = 72
AUXROWS = 73
MSG = DIM + HEADS + 1
U4 = 4



class Shapes:

    def __init__(self, n_nodes, n_edges):
        self.N, self.E = n_nodes, n_edges
        self.NS = -(-(n_nodes + W) // 256) * 256
        self.LAST = self.NS - W
        self.BLOCKS = -(-n_edges // (BLOCK * U4)) * U4
        self.GROUPS = self.BLOCKS * G
        self.GP = max(p for p in range(1, P + 1) if self.GROUPS % p == 0)
        self.GF = self.GROUPS // self.GP
        self.TILES = self.NS // P
        self.FULL = n_nodes // CH
        self.CHUNKS = self.FULL + 1
        self.LW = self.NS - self.FULL * CH
        self.LV = n_nodes - self.FULL * CH
        assert 0 < self.LV <= self.LW <= CH


class Step:

    def __init__(self, n, slot, nth, use, use_in_pass):
        self.n, self.slot, self.nth, self.use, self.use_in_pass = n, slot, nth, use, use_in_pass

    def freed(self, eng, sem, depth):
        if not (isinstance(self.n, int) and self.n < depth):
            eng.wait_ge(sem, self.nth - depth)

    def slot_freed(self, eng, sem, count):
        if not (isinstance(self.n, int) and self.use_in_pass == 0):
            eng.wait_ge(sem, (self.use - 1) * count)


def alone(eng):
    eng.nop(nofuse=True)


def steps(eng, total, slots, stages, pass_=None):
    most = max(lag for lag, _ in stages)
    first = 1 + -(-most // slots)
    full = total // slots

    def step(n, slot, use):
        if pass_ is None:
            return Step(n, slot, n + 1, use + 1, use)
        return Step(n, slot, pass_ * total + n + 1, pass_ * full + use + 1, use)

    def static(i):
        for lag, stage in stages:
            n = i - lag
            if 0 <= n < total:
                stage(step(n, n % slots, n // slots))

    assert pass_ is None or total % slots == 0
    loop = range(first * slots, full * slots) if full > first else range(0)
    head = loop.start if loop else total + most
    for i in range(head):
        static(i)
    if loop:
        with eng.Fori(first, full) as t:
            for k in range(slots):
                for lag, stage in stages:
                    stage(step(t * slots + (k - lag), (k - lag) % slots, t + (k - lag) // slots))
        for i in range(loop.stop, total + most):
            static(i)


def build(nc, sh, x, src_blocks, dst_cols, dst_groups, attr, wqkv, wet, w1, w2, w3, vecs, out):
    ctx = ExitStack()

    def sb(name, shape, dt=F32):
        return ctx.enter_context(nc.sbuf_tensor(name, shape, dt))

    with ctx:
        q_tab = nc.dram_tensor("q_tab", (sh.NS, 3 * DIM), BF16, kind="Internal").ap()
        kv_tab = nc.dram_tensor("kv_tab", (sh.NS, 2 * DIM), F32, kind="Internal").ap()
        x1_tab = nc.dram_tensor("x1_tab", (sh.NS, DIM), F32, kind="Internal").ap()
        g_tabs = [nc.dram_tensor(f"g_tab{i}", (sh.NS, DIM), F32, kind="Internal").ap() for i in range(3)]
        base_tab = nc.dram_tensor("base_tab", (sh.GROUPS,), I32, kind="Internal").ap()

        state = sb("state", [P, sh.NS])
        aux = sb("aux", [P, sh.NS])
        dst_f = sb("dst_f", [P, sh.BLOCKS * C])
        dst_rel = sb("dst_rel", [P, sh.BLOCKS * C])
        base_w = sb("base_w", [P, sh.GROUPS])
        base_i = sb("base_i", [1, sh.GROUPS], I32)
        windows = sb("windows", [1, 1], I32)
        ident = sb("ident", [P, P])
        iota_w = sb("iota_w", [P, W])
        eps_t = sb("eps_t", [P, 1])
        one_t = sb("one_t", [P, 1])
        neg1_t = sb("neg1_t", [P, 1])
        zero_t = sb("zero_t", [P, 1])
        vec_t = sb("vec_t", [P, 12])

        prepare(nc, sh, locals())
        project(nc, sh, locals())
        attend(nc, sh, locals())
        normalise(nc, sh, locals())
        with nc.sbuf_tensor("w1_sb", [P, 2, DIM], F32) as w1_sb, \
                nc.sbuf_tensor("w2_sb", [P, 2, DIM], F32) as w2_sb, \
                nc.sbuf_tensor("w3_sb", [P, DIM], F32) as w3_sb:
            weights = (w1_sb, w2_sb, w3_sb)
            for layer in range(3):
                aggregate(nc, sh, layer, locals())
                transform(nc, sh, layer, locals())


def semaphores(nc, ctx):
    made = []


    def clear():
        nc.clear_and_free_semaphores(made)
        nc.all_engine_barrier()

    ctx.callback(clear)

    def sem(name):
        made.append(nc.alloc_semaphore(name))
        return made[-1]
    return sem


def prepare(nc, sh, env):
    ident, iota_w, windows, base_tab = env["ident"], env["iota_w"], env["windows"], env["base_tab"]
    state, aux, dst_f, base_w, base_i = env["state"], env["aux"], env["dst_f"], env["base_w"], env["base_i"]
    wide = sh.GF * J * P
    with ExitStack() as c:
        def tile(name, shape, dt=F32):
            return c.enter_context(nc.sbuf_tensor(name, shape, dt))

        raw = tile("raw", [P, wide], I32)
        val = tile("val", [P, wide])
        low = tile("low", [P, wide])
        dst_i = tile("dst_i", [P, sh.BLOCKS * C], I32)
        base_n = tile("base_n", [P, sh.GROUPS], I32)
        least = tile("least", [P, sh.GF])
        most = tile("most", [P, sh.GF])
        span = tile("span", [P, sh.GF])
        span1 = tile("span1", [P, 1])
        top = tile("top", [1, 2])
        least_i = tile("least_i", [P, sh.GF], I32)
        turned = c.enter_context(nc.psum_tensor("turned", [P, P], F32))
        new = semaphores(nc, c)
        loaded, cast, lowered, reduced, spanned, widest, topped, base_made, base_out, base_back, cols_in, made = (
            new(s) for s in
            ("loaded", "cast", "lowered", "reduced", "spanned", "widest", "topped", "base_made", "base_out",
             "base_back", "cols_in", "made"))
        block = c.enter_context(nc.Block())

        @block.sync
        def _(sp):
            sp.dma_start(raw[0:sh.GP, :], env["dst_groups"]).then_inc(loaded, 16)
            sp.dma_start(dst_i[:, :], env["dst_cols"]).then_inc(cols_in, 16)
            sp.dma_start(env["vec_t"][:, :], env["vecs"]).then_inc(cols_in, 16)
            sp.wait_ge(base_made, 1)
            sp.dma_start(base_tab.rearrange("(p f) -> p f", p=sh.GP), least_i[0:sh.GP, :]).then_inc(base_out, 16)
            sp.wait_ge(base_out, 16)
            sp.dma_start(base_n[:, :], base_tab.unsqueeze(0).to_broadcast([P, sh.GROUPS])).then_inc(base_back, 16)
            sp.wait_ge(base_back, 16)

        @block.gpsimd
        def _(pool):
            nc.gpsimd.memset(ident[:, :], 0.0).then_inc(made, 1)
            pool.wait_ge(made, 1)
            nc.gpsimd.affine_select(out=ident[:, :], in_=ident[:, :], compare_op=ALU.not_equal, fill=1.0, base=0,
                                    pattern=[[-1, P]], channel_multiplier=1).then_inc(made, 1)
            nc.gpsimd.iota(iota_w[:, :], pattern=[[1, W]], base=0, channel_multiplier=0,
                           allow_small_or_imprecise_dtypes=True)
            nc.gpsimd.memset(env["eps_t"][:, :], EPS)
            nc.gpsimd.memset(env["one_t"][:, :], 1.0)
            nc.gpsimd.memset(env["neg1_t"][:, :], -1.0)
            nc.gpsimd.memset(env["zero_t"][:, :], 0.0)
            nc.gpsimd.memset(state[:, :], 0.0)
            nc.gpsimd.memset(aux[:, :], 0.0).then_inc(made, 1)
            pool.wait_ge(made, 3)
            nc.gpsimd.memset(aux[0:HEADS, :], -BIG).then_inc(made, 1)

        @block.vector
        def _(dve):
            q = slice(0, sh.GP)
            dve.wait_ge(loaded, 16)
            nc.vector.tensor_copy(val[q, :], raw[q, :]).then_inc(cast, 1)
            dve.wait_ge(cast, 1)
            nc.vector.tensor_reduce(least[q, :], val[q, :].rearrange("p (f e) -> p f e", f=sh.GF), AX.X,
                                    ALU.min).then_inc(reduced, 1)
            nc.vector.tensor_scalar(low[q, :], val[q, :], float(SENTINEL), -2.0 * SENTINEL, ALU.is_ge,
                                    ALU.mult).then_inc(lowered, 1)
            dve.wait_ge(lowered, 1)
            nc.vector.tensor_tensor(low[q, :], low[q, :], val[q, :], ALU.add).then_inc(lowered, 1)
            dve.wait_ge(lowered, 2)
            nc.vector.tensor_reduce(most[q, :], low[q, :].rearrange("p (f e) -> p f e", f=sh.GF), AX.X,
                                    ALU.max).then_inc(reduced, 1)
            dve.wait_ge(reduced, 2)
            nc.vector.tensor_tensor(span[q, :], most[q, :], least[q, :], ALU.subtract).then_inc(spanned, 1)
            nc.vector.tensor_scalar(least[q, :], least[q, :], float(sh.LAST), None, ALU.min).then_inc(spanned, 1)
            dve.wait_ge(spanned, 2)
            nc.vector.tensor_copy(least_i[q, :], least[q, :]).then_inc(base_made, 1)
            nc.vector.tensor_reduce(span1[q, :], span[q, :], AX.X, ALU.max).then_inc(spanned, 1)
            dve.wait_ge(widest, 1)
            nc.vector.tensor_reduce(top[:, 0:1], turned[0:1, 0:sh.GP], AX.X, ALU.max).then_inc(topped, 1)
            dve.wait_ge(topped, 1)
            nc.vector.tensor_copy(windows[:, :], top[:, 0:1]).then_inc(topped, 1)
            dve.wait_ge(cols_in, 32)
            nc.vector.tensor_copy(dst_f[:, :], dst_i[:, :])
            dve.wait_ge(base_back, 16)
            nc.vector.tensor_copy(base_w[:, :], base_n[:, :])

        @block.tensor
        def _(pe):
            pe.wait_ge(made, 2)
            pe.wait_ge(spanned, 3)
            nc.tensor.transpose(turned[0:1, 0:sh.GP], span1[0:sh.GP, :], ident[0:sh.GP, 0:sh.GP]).then_inc(widest, 1)


def project(nc, sh, env):
    ident = env["ident"]
    with ExitStack() as c:
        def tile(name, shape, dt=F32):
            return c.enter_context(nc.sbuf_tensor("pj_" + name, shape, dt))

        new = semaphores(nc, c)

        def sem(name):
            return new("pj_" + name)

        T = CH // P
        w_sb = tile("w", [P, 3 * DIM])
        xt = tile("x", [P, U4, T, DIM])
        stats = tile("stats", [P, U4, T, 6])
        mv = tile("mv", [P, U4, T, 2])
        root = tile("root", [P, U4, T])
        rstd = tile("rstd", [P, U4, T])
        hn = tile("hn", [P, U4, T, DIM])
        ht = tile("ht", [P, U4, CH])
        kv = tile("kv", [P, U4, T, 2 * DIM])
        qs = tile("qs", [P, U4, T, DIM])
        q3 = tile("q3", [P, U4, T, 3, DIM], BF16)
        h_ps = [c.enter_context(nc.psum_tensor(f"pj_hps{k}", [P, CH], F32)) for k in range(2)]
        p_ps = [c.enter_context(nc.psum_tensor(f"pj_pps{t}", [P, 512], F32)) for t in range(T)]
        w_in, stat, aggr, rooted, std, normed, turned, relud, q_sb = (sem(s) for s in (
            "w_in", "stat", "aggr", "rooted", "std", "normed", "turned", "relud", "q_sb"))
        split = [sem(f"split{i}") for i in range(5)]
        projected = [sem(f"projected{t}") for t in range(T)]
        read = [sem(f"read{t}") for t in range(T)]
        x_in = [sem(f"x_in{k}") for k in range(U4)]
        kv_out = [sem(f"kv_out{k}") for k in range(U4)]
        q_out = [sem(f"q_out{k}") for k in range(U4)]
        block = c.enter_context(nc.Block())
        width = chunk_width(sh)

        def tiles(s):
            return width(s.n) // P

        @block.sync
        def _(sp):
            sp.dma_start(w_sb[:, :], env["wqkv"]).then_inc(w_in, 16)

            def load(s):
                s.freed(sp, normed, U4)
                sp.dma_start(xt[:, s.slot, 0:tiles(s), :], rows_of(env["x"], s.n, width(s.n))
                             ).then_inc(x_in[s.slot], 16)

            def store(s):
                k, t = s.slot, tiles(s)
                sp.wait_ge(read[t - 1], s.nth)
                sp.dma_start(rows_of(env["kv_tab"], s.n, width(s.n)), kv[:, k, 0:t, :]).then_inc(kv_out[k], 16)
                sp.wait_ge(split[4], s.nth)
                sp.dma_start(rows_of(env["q_tab"], s.n, width(s.n)),
                             q3[:, k, 0:t, :, :].rearrange("p t a d -> p t (a d)")).then_inc(q_out[k], 16)

            steps(sp, sh.CHUNKS, U4, [(0, load), (3, store)])
            for k in range(U4):
                uses = len(range(k, sh.CHUNKS, U4))
                sp.wait_ge(kv_out[k], 16 * uses)
                sp.wait_ge(q_out[k], 16 * uses)

        @block.vector
        def _(dve):
            def statistics(s):
                k = s.slot
                dve.wait_ge(x_in[k], 16 * s.use)
                for i in range(tiles(s)):
                    last = nc.vector.bn_stats(stats[:, k, i, :], xt[:, k, i, :])
                last.then_inc(stat, 1)
                dve.wait_ge(stat, s.nth)
                alone(dve)
                for i in range(tiles(s)):
                    last = nc.vector.bn_aggr(mv[:, k, i, :], stats[:, k, i, :])
                last.then_inc(aggr, 1)

            def apply_norm(s):
                k, t = s.slot, tiles(s)
                dve.wait_ge(rooted, s.nth)
                nc.vector.reciprocal(rstd[:, k, 0:t], root[:, k, 0:t]).then_inc(std, 1)
                dve.wait_ge(std, s.nth)
                s.freed(dve, turned, U4)
                for i in range(t):
                    last = nc.vector.tensor_scalar(hn[:, k, i, :], xt[:, k, i, :], mv[:, k, i, 0:1],
                                                   rstd[:, k, i:i + 1], ALU.subtract, ALU.mult)
                last.then_inc(normed, 1)

            def split_q(s):
                k, t = s.slot, tiles(s)
                dve.wait_ge(q_sb, s.nth)
                s.slot_freed(dve, q_out[k], 16)
                q = qs[:, k, 0:t, :]
                nc.vector.tensor_copy(q3[:, k, 0:t, 0, :], q).then_inc(split[0], 1)
                for part in range(2):
                    dve.wait_ge(split[2 * part], s.nth)
                    nc.vector.tensor_tensor(q, q, q3[:, k, 0:t, part, :], ALU.subtract).then_inc(split[2 * part + 1], 1)
                    dve.wait_ge(split[2 * part + 1], s.nth)
                    nc.vector.tensor_copy(q3[:, k, 0:t, part + 1, :], q).then_inc(split[2 * part + 2], 1)

            steps(dve, sh.CHUNKS, U4, [(3, split_q), (1, apply_norm), (0, statistics)])

        @block.tensor
        def _(pe):
            pe.wait_ge(w_in, 16)

            def turn(s):
                pe.wait_ge(normed, s.nth)
                s.freed(pe, relud, 2)
                for i in range(tiles(s)):
                    last = nc.tensor.transpose(h_ps[s.slot % 2][:, i * P:(i + 1) * P], hn[:, s.slot, i, :], ident[:, :])
                last.then_inc(turned, 1)

            def mul(s):
                pe.wait_ge(relud, s.nth)
                for i in range(T):
                    if i < tiles(s):
                        s.freed(pe, read[i], 1)
                        nc.tensor.matmul(p_ps[i][:, 0:3 * DIM], ht[:, s.slot, i * P:(i + 1) * P], w_sb[:, :],
                                         start=True, stop=True).then_inc(projected[i], 1)

            steps(pe, sh.CHUNKS, U4, [(2, mul), (1, turn)])

        @block.scalar
        def _(act):
            def root_var(s):
                k, t = s.slot, tiles(s)
                act.wait_ge(aggr, s.nth)
                s.freed(act, std, U4)
                nc.scalar.activation(root[:, k, 0:t], mv[:, k, 0:t, 1:2].rearrange("p t o -> p (t o)"), ACT.Sqrt,
                                     bias=env["eps_t"][:, :]).then_inc(rooted, 1)

            def relu(s):
                k, cw = s.slot, width(s.n)
                act.wait_ge(turned, s.nth)
                s.freed(act, projected[0], U4)
                nc.scalar.activation(ht[:, k, 0:cw], h_ps[k % 2][:, 0:cw], ACT.Relu).then_inc(relud, 1)

            def split_out(s):
                k, t = s.slot, tiles(s)
                s.freed(act, split[4], U4)
                s.slot_freed(act, kv_out[k], 16)
                for i in range(t):
                    act.wait_ge(projected[i], s.nth)
                    q = nc.scalar.activation(qs[:, k, i, :], p_ps[i][:, 0:DIM], ACT.Copy, scale=HC ** -0.5)
                    v = nc.scalar.activation(kv[:, k, i, :], p_ps[i][:, DIM:3 * DIM], ACT.Copy).then_inc(read[i], 1)
                    if i == t - 1:
                        q.then_inc(q_sb, 1)

            steps(act, sh.CHUNKS, U4, [(2, split_out), (1, relu), (0, root_var)])


def start_pass(nc, dve, env, ready, changed):
    nc.vector.tensor_tensor(rel_view(env["dst_rel"]), rel_view(env["dst_f"]), base_view(env["base_w"]),
                            ALU.subtract).then_inc(changed, 1)
    nc.vector.tensor_copy(env["base_i"][:, :], env["base_w"][0:1, :]).then_inc(ready, 1)


def first_pass(nc, dve, env, base_n, base_in, ready, changed):
    dve.wait_ge(base_in, 16)
    nc.vector.tensor_copy(env["base_w"][:, :], base_n[:, :]).then_inc(changed, 1)
    dve.wait_ge(changed, 1)
    start_pass(nc, dve, env, ready, changed)


def next_pass(nc, dve, sh, env, ready, changed, w):
    nc.vector.tensor_scalar(env["base_w"][:, :], env["base_w"][:, :], float(W), float(sh.LAST), ALU.add,
                            ALU.min).then_inc(changed, 1)
    dve.wait_ge(changed, 2 * w + 3)
    start_pass(nc, dve, env, ready, changed)


def rel_view(t):
    return t[:, :].rearrange("p (s j g) -> p s j g", j=J, g=G)


def base_view(t):
    v = t[:, :].rearrange("p (s g) -> p s g", g=G).unsqueeze(2)
    return v.to_broadcast([P, v.shape[1], J, G])


def passes(eng, sh, env):
    widest = eng.value_load(env["windows"][0:1, 0:1], min_val=0, max_val=sh.N)
    return eng.Fori(0, widest // W + 1)


def eng_loads(nc, eng, row, most):
    _, values = nc.values_load_multi_w_load_instructions(
        row, engines=[eng.engine], min_val=0, max_val=most,
        skip_runtime_bounds_check_because="prepare and next_pass bound each base by the last window's")
    return values


def bases(eng, sh, env, n, blocks=1):
    return eng_loads(env["nc"], eng, env["base_i"][0:1, bass.ds(n * G, blocks * G)], sh.LAST)


def one_hot(nc, dve, env, dest, n):
    rel = env["dst_rel"][:, bass.ds(n * C, C)].unsqueeze(2).to_broadcast([P, C, W])
    idx = env["iota_w"][:, :].unsqueeze(1).to_broadcast([P, C, W])
    return nc.vector.tensor_tensor(dest, rel, idx, ALU.is_equal)


def attend(nc, sh, env):
    ident, state, aux = env["ident"], env["state"], env["aux"]
    with ExitStack() as c:
        def tile(name, shape, dt=F32):
            return c.enter_context(nc.sbuf_tensor(name, shape, dt))

        def psum(name, shape, dt=F32):
            return c.enter_context(nc.psum_tensor(name, shape, dt))

        new = semaphores(nc, c)

        def sem(name):
            return new("at_" + name)

        identb = tile("at_identb", [P, P], BF16)
        ident16 = tile("at_ident16", [P, P], BF16)
        sel_head = tile("at_sel_head", [3 * G * HEADS, HEADS, P], BF16)
        sel_feat = tile("at_sel_feat", [HEADS, DIM])
        sel_aux = tile("at_sel_aux", [HEADS + 1, AUXROWS])
        diag = tile("at_diag", [P, G])
        we = tile("at_we", [P, G * HEADS])

        base_n = tile("at_base_n", [P, sh.GROUPS], I32)
        idx = tile("at_idx", [P, U4, C], U32)
        att = tile("at_attr", [P, U4, J, P])
        qd = tile("at_qd", [P, U4, G, 3, DIM], BF16)
        kv = tile("at_kv", [P, U4, C, 2 * DIM])
        hot = tile("at_hot", [P, U4, C, W])
        hot_t = tile("at_hot_t", [P, U4, J, P])
        hot_b = tile("at_hot_b", [P, U4, J, P], BF16)
        miss_b = tile("at_miss_b", [P, U4, J, P], BF16)
        prod = tile("at_prod", [P, C, DIM])
        qk = tile("at_qk", [P, C * HEADS])
        sc = tile("at_sc", [P, U4, J, G * HEADS])
        parts = tile("at_parts", [P, J, 3, G * HEADS], BF16)
        rest = tile("at_rest", [P, J, G * HEADS])
        sct = tile("at_sct", [3 * G * HEADS, 2, J, P], BF16)
        ml4 = tile("at_ml4", [P, J, HEADS])
        ml = tile("at_ml", [P, HEADS])
        mnew = tile("at_mnew", [HEADS, G, W])
        drop = tile("at_drop", [HEADS, G, W])
        fall = tile("at_fall", [HEADS, G * W])
        scale = tile("at_scale", [HEADS + 1, G * W])
        md = tile("at_md", [P, G, HEADS])
        above = tile("at_above", [P, C * HEADS])
        below = tile("at_below", [P, C * HEADS])
        msg = tile("at_msg", [P, 2, C, MSG])
        nodes = tile("at_nodes", [P, 2, DIM + AUXROWS])

        ps_in = psum("at_ps_in", [P, 512])
        ps_qe = psum("at_ps_qe", [P, C, DIM])
        ps_bc = [psum(f"at_ps_bc{i}", [P, 4, P]) for i in range(2)]
        ps_sum = psum("at_ps_sum", [P, 512])
        ps_low = psum("at_ps_low", [P, 512])
        ps_me = psum("at_ps_me", [P, 512])
        ps_hot = ps_in[:, 0:J * P].rearrange("p (j e) -> p j e", j=J)
        node_ps = ps_in[:, J * P:J * P + MSG]
        sct_ps = ps_bc[0][0:3 * G * HEADS, 0:J, :]
        mlt_ps = ps_me[0:HEADS, 128:256]
        mt_ps = ps_me[:, 256:256 + HEADS]
        bias_ps = ps_low[:, 0:64]
        sf_ps = ps_low[:, 128:256]
        sa_ps = ps_low[0:AUXROWS, 256:384]
        num_ps = ps_sum[:, 0:128]
        den_ps = ps_sum[0:AUXROWS, 128:256]
        me_ps = ps_me[:, 0:64]

        made, we_in, base_in, tables, changed = (sem(s) for s in ("made", "we_in", "base_in", "tables", "changed"))
        MADE = 20
        idx_in = [sem(f"idx_in{k}") for k in range(U4)]
        attr_in = [sem(f"attr_in{k}") for k in range(U4)]
        q_in = [sem(f"q_in{k}") for k in range(U4)]
        kv_in = [sem(f"kv_in{k}") for k in range(U4)]
        hot_made, hot_turned, hot_copied, bias_made, q_spread, prod_made, qk_made, sc_made = (
            sem(s) for s in ("hot_made", "hot_turned", "hot_copied", "bias_made", "q_spread",
                             "prod_made", "qk_made", "sc_made"))
        sc_turned, sct_made, ml_made, ml_turned, fall_made, m_turned, md_made, m_spread = (
            sem(s) for s in ("sc_turned", "sct_made", "ml_made", "ml_turned", "fall_made", "m_turned", "md_made",
                             "m_spread"))
        split = [sem(f"split{i}") for i in range(4)]
        bc_made = [sem(f"bc_made{i}") for i in range(4)]
        bc_read = [sem(f"bc_read{i}") for i in range(4)]
        above_made, below_made, ex_made, scale_made, scale_spread, msg_made, summed = (
            sem(s) for s in ("above_made", "below_made", "ex_made", "scale_made", "scale_spread", "msg_made", "summed"))
        node_summed, nodes_copied = sem("node_summed"), sem("nodes_copied")
        scaled = [sem(f"scaled{g}") for g in range(G)]
        added = [sem(f"added{g}") for g in range(G)]
        m_kept = [sem(f"m_kept{g}") for g in range(G)]
        m_read = [sem(f"m_read{g}") for g in range(G)]
        block = c.enter_context(nc.Block())

        @block.sync
        def _(sp):
            sp.dma_start(base_n[:, :], env["base_tab"].unsqueeze(0).to_broadcast([P, sh.GROUPS])
                         ).then_inc(base_in, 16)
            sp.wait_ge(made, 8)
            for g in range(G):
                sp.dma_start(we[EDIM * g:EDIM * (g + 1), HEADS * g:HEADS * (g + 1)], env["wet"]).then_inc(we_in, 16)
            with passes(sp, sh, env) as w:
                sp.wait_ge(tables, w + 1)

                def load(s):
                    k = s.slot
                    s.slot_freed(sp, kv_in[k], 16 * C)
                    sp.dma_start(idx[:, k, :], env["src_blocks"][bass.ds(s.n, 1), :, :].squeeze(0)
                                 ).then_inc(idx_in[k], 16)
                    s.freed(sp, bias_made, U4)
                    sp.dma_start(att[:, k, :, :].rearrange("p j e -> p (j e)"),
                                 env["attr"][bass.ds(s.n, 1), :, :].squeeze(0)).then_inc(attr_in[k], 16)
                    s.freed(sp, q_spread, U4)
                    for g, b in enumerate(bases(sp, sh, env, s.n)):
                        sp.dma_start(qd[W * g:W * (g + 1), k, g, :, :].rearrange("p a d -> p (a d)"),
                                     env["q_tab"][bass.ds(b, W), :]).then_inc(q_in[k], 16)

                steps(sp, sh.BLOCKS, U4, [(0, load)], w)

        @block.gpsimd
        def _(pool):
            nc.gpsimd.memset(we[:, :], 0.0).then_inc(made, 1)
            nc.gpsimd.memset(qd[:, :, :, :, :], 0.0).then_inc(made, 1)
            nc.gpsimd.memset(nodes[:, :, :], 0.0).then_inc(made, 1)
            nc.gpsimd.memset(sel_head[:, :, :], 0.0).then_inc(made, 1)
            nc.gpsimd.memset(sel_feat[:, :], 1.0).then_inc(made, 1)
            nc.gpsimd.memset(sel_aux[:, :], 0.0).then_inc(made, 1)
            nc.gpsimd.memset(diag[:, :], 1.0).then_inc(made, 1)
            nc.gpsimd.memset(scale[:, :], 1.0).then_inc(made, 1)
            pool.wait_ge(made, 8)
            nc.gpsimd.memset(msg[:, :, :, MSG - 1:MSG], 1.0).then_inc(made, 1)

            def select_head(part):
                sv = sel_head[:, :, :].rearrange("p h (g w) -> p h g w", g=G)
                nc.gpsimd.affine_select(out=sv, in_=sv, compare_op=ALU.not_equal, fill=1.0,
                                        base=-part * G * HEADS, pattern=[[-1, HEADS], [-HEADS, G], [0, W]],
                                        channel_multiplier=1).then_inc(made, 1)

            select_head(0)
            nc.gpsimd.affine_select(out=sel_feat[:, :], in_=sel_feat[:, :], compare_op=ALU.is_ge, fill=0.0, base=0,
                                    pattern=[[1, DIM]], channel_multiplier=-HC).then_inc(made, 1)
            nc.gpsimd.affine_select(out=sel_aux[0:HEADS, :], in_=sel_aux[0:HEADS, :], compare_op=ALU.not_equal,
                                    fill=1.0, base=AUXD, pattern=[[-1, AUXROWS]], channel_multiplier=1
                                    ).then_inc(made, 1)
            nc.gpsimd.affine_select(out=diag[:, :], in_=diag[:, :], compare_op=ALU.is_ge, fill=0.0, base=0,
                                    pattern=[[-W, G]], channel_multiplier=1).then_inc(made, 1)
            nc.gpsimd.tensor_scalar(identb[:, :], ident[:, :], BIG, None, ALU.mult).then_inc(made, 1)
            nc.gpsimd.tensor_scalar(ident16[:, :], ident[:, :], 1.0, None, ALU.mult).then_inc(made, 1)
            pool.wait_ge(made, 15)
            select_head(1)
            nc.gpsimd.affine_select(out=sel_feat[:, :], in_=sel_feat[:, :], compare_op=ALU.is_ge, fill=0.0,
                                    base=HC - 1, pattern=[[-1, DIM]], channel_multiplier=HC).then_inc(made, 1)
            nc.gpsimd.affine_select(out=sel_aux[:, :], in_=sel_aux[:, :], compare_op=ALU.not_equal, fill=1.0,
                                    base=AUXN - 1000 * HEADS, pattern=[[-1, AUXROWS]], channel_multiplier=1000
                                    ).then_inc(made, 1)
            nc.gpsimd.affine_select(out=diag[:, :], in_=diag[:, :], compare_op=ALU.is_ge, fill=0.0, base=W - 1,
                                    pattern=[[W, G]], channel_multiplier=-1).then_inc(made, 1)
            pool.wait_ge(made, MADE - 1)
            select_head(2)
            pool.wait_ge(made, MADE)
            with passes(pool, sh, env) as w:
                pool.wait_ge(tables, w + 1)

                def gather(s):
                    pool.wait_ge(idx_in[s.slot], 16 * s.use)
                    s.freed(pool, msg_made, U4)
                    alone(pool)
                    for ch in range(C):
                        nc.gpsimd.indirect_dma_start(
                            kv[:, s.slot, ch, :], None, env["kv_tab"],
                            bass.IndirectOffsetOnAxis(ap=idx[:, s.slot, ch:ch + 1], axis=0)
                        ).then_inc(kv_in[s.slot], 16)

                steps(pool, sh.BLOCKS, U4, [(0, gather)], w)

        @block.vector
        def _(dve):
            first_pass(nc, dve, env, base_n, base_in, tables, changed)
            dve.wait_ge(made, MADE)
            with passes(dve, sh, env) as w:
                dve.wait_ge(changed, 2 * w + 2)
                dve.wait_ge(tables, w + 1)

                def head_max(units):
                    def run(s):
                        for u in units:
                            dve.wait_ge(bc_made[u], s.nth)
                            nc.vector.tensor_reduce(ml4[:, u // 2, 4 * (u % 2):4 * (u % 2) + 4],
                                                    ps_bc[u % 2][:, :, :], AX.X, ALU.max).then_inc(bc_read[u], 1)
                    return run

                b_sum, b_max = [None] * G, [None] * G

                def block_max(s):
                    for u in range(4):
                        dve.wait_ge(bc_read[u], s.nth)
                    nc.vector.tensor_tensor(ml[:, :], ml4[:, 0, :], ml4[:, 1, :], ALU.max).then_inc(ml_made, 1)

                def messages(s):
                    k = s.slot
                    dve.wait_ge(ex_made, s.nth)
                    e = msg[:, k % 2, :, DIM:DIM + HEADS].unsqueeze(3).to_broadcast([P, C, HEADS, HC])
                    v = kv[:, k, :, DIM:2 * DIM].rearrange("p c (h d) -> p c h d", h=HEADS)
                    nc.vector.tensor_tensor(msg[:, k % 2, :, 0:DIM].rearrange("p c (h d) -> p c h d", h=HEADS), v, e,
                                            ALU.mult).then_inc(msg_made, 1)

                def update(groups, raised=True):
                    def run(s):
                        merged = not (isinstance(s.n, int) and s.n == 0)
                        before = s.nth - 1
                        if groups[0] == 0:
                            if raised and merged:
                                b = bases(dve, sh, env, s.n - 1, 2)
                                b_sum[:], b_max[:] = b[:G], b[G:]
                            elif raised:
                                b_max[:] = bases(dve, sh, env, s.n)
                            else:
                                b_sum[:] = bases(dve, sh, env, s.n - 1)
                            if raised:
                                dve.wait_ge(ml_turned, s.nth)
                                s.freed(dve, fall_made, 1)
                            if merged:
                                dve.wait_ge(summed, before)
                                dve.wait_ge(scale_spread, before)
                            alone(dve)
                        for g in groups:
                            q = slice(g * W, (g + 1) * W)
                            if raised:
                                top = aux[0:HEADS, bass.ds(b_max[g], W)]
                                if g:
                                    dve.wait_ge(m_kept[g - 1], s.nth)
                                else:
                                    s.freed(dve, m_kept[G - 1], 1)
                                nc.vector.tensor_tensor(mnew[:, g, :], top, mlt_ps[:, q], ALU.max
                                                        ).then_inc(m_read[g], 1)
                                nc.vector.tensor_tensor(drop[:, g, :], top, mlt_ps[:, q], ALU.subtract
                                                        ).then_inc(m_read[g], 1)
                            if merged:
                                num = state[:, bass.ds(b_sum[g], W)]
                                den = aux[AUXD:AUXROWS, bass.ds(b_sum[g], W)]
                                if g:
                                    dve.wait_ge(added[g - 1], 2 * before)
                                elif not (isinstance(s.n, int) and s.n == 1):
                                    dve.wait_ge(added[G - 1], 2 * (before - 1))
                                nc.vector.tensor_tensor(num, num, sf_ps[:, q], ALU.mult).then_inc(scaled[g], 1)
                                nc.vector.tensor_tensor(den, den, sa_ps[AUXD:AUXROWS, q], ALU.mult
                                                        ).then_inc(scaled[g], 1)
                            if raised:
                                dve.wait_ge(m_read[g], 2 * s.nth)
                                nc.vector.tensor_tensor(top, top, mnew[:, g, :], ALU.max).then_inc(m_kept[g], 1)
                            if merged:
                                dve.wait_ge(scaled[g], 2 * before)
                                nc.vector.tensor_tensor(num, num, num_ps[:, q], ALU.add).then_inc(added[g], 1)
                                nc.vector.tensor_tensor(den, den, den_ps[AUXD:AUXROWS, q], ALU.add
                                                        ).then_inc(added[g], 1)
                    return run

                def hot_one(s):
                    one_hot(nc, dve, env, hot[:, s.slot, :, :], s.n).then_inc(hot_made, 1)

                def score(s):
                    k = s.slot
                    dve.wait_ge(kv_in[k], 16 * C * s.use)
                    dve.wait_ge(q_spread, s.nth)
                    nc.vector.tensor_tensor(prod[:, :, :], ps_qe[:, :, :], kv[:, k, :, 0:DIM],
                                            ALU.mult).then_inc(prod_made, 1)
                    dve.wait_ge(prod_made, s.nth)
                    nc.vector.tensor_reduce(qk[:, :], prod[:, :, :].rearrange("p c (h d) -> p (c h) d", h=HEADS),
                                            AX.X, ALU.add).then_inc(qk_made, 1)
                    dve.wait_ge(qk_made, s.nth)
                    dve.wait_ge(bias_made, s.nth)
                    nc.vector.tensor_tensor(sc[:, k, :, :].rearrange("p j q -> p (j q)"), qk[:, :], bias_ps,
                                            ALU.add).then_inc(sc_made, 1)

                def first_rest(s):
                    dve.wait_ge(split[0], s.nth)
                    nc.vector.tensor_tensor(rest[:, :, :], sc[:, s.slot, :, :], parts[:, :, 0, :], ALU.subtract
                                            ).then_inc(split[1], 1)

                def last_rest(s):
                    dve.wait_ge(split[2], s.nth)
                    nc.vector.tensor_tensor(parts[:, :, 2, :], rest[:, :, :], parts[:, :, 1, :], ALU.subtract
                                            ).then_inc(split[3], 1)

                def spread_max(s):
                    dve.wait_ge(m_turned, s.nth)
                    nc.vector.tensor_tensor(md[:, :, :], mt_ps.unsqueeze(1).to_broadcast([P, G, HEADS]),
                                            diag[:, :].unsqueeze(2).to_broadcast([P, G, HEADS]),
                                            ALU.mult).then_inc(md_made, 1)

                def above_score(s):
                    dve.wait_ge(m_spread, s.nth)
                    s.freed(dve, below_made, 1)
                    nc.vector.tensor_tensor(above[:, :], sc[:, s.slot, :, :].rearrange("p j q -> p (j q)"), me_ps,
                                            ALU.subtract).then_inc(above_made, 1)

                steps(dve, sh.BLOCKS, U4, [(1, score), (0, hot_one), (1, first_rest), (2, update((0,))),
                                           (1, last_rest), (2, update((1, 2, 3))), (1, head_max((0,))),
                                           (2, spread_max), (1, head_max((1, 2))), (2, above_score),
                                           (1, head_max((3,))), (2, messages),
                                           (1, block_max)], w)
                update(range(G), raised=False)(Step(sh.BLOCKS, 0, (w + 1) * sh.BLOCKS + 1, 0, 0))
                next_pass(nc, dve, sh, env, tables, changed, w)

        @block.tensor
        def _(pe):
            pe.wait_ge(made, MADE)
            pe.wait_ge(we_in, 16 * G)
            with passes(pe, sh, env) as w:
                pe.wait_ge(tables, w + 1)

                def spread_q(j):
                    def run(s):
                        k = s.slot
                        if j == 0:
                            pe.wait_ge(hot_copied, 3 * (s.nth - 1) + 1)
                            pe.wait_ge(q_in[k], 16 * G * s.use)
                            s.freed(pe, prod_made, 1)
                        for part in range(3):
                            last = nc.tensor.matmul(ps_qe[:, G * j:G * (j + 1), :], hot_b[:, k, j, :],
                                                    qd[:, k, :, part, :], start=part == 0, stop=part == 2)
                        if j == J - 1:
                            last.then_inc(q_spread, 1)
                    return run

                def spread_scores(units):
                    def run(s):
                        k = s.slot
                        for u in units:
                            j, half = divmod(u, 2)
                            if u < 2:
                                pe.wait_ge(sct_made, s.nth)
                                s.freed(pe, bc_read[u + 2], 1)
                            else:
                                pe.wait_ge(bc_read[u - 2], s.nth)
                            nc.tensor.matmul(ps_bc[u % 2][:, :, :], identb[:, :],
                                             miss_b[:, k, j, :].unsqueeze(1).to_broadcast([P, 4, P]),
                                             start=True, stop=False, skip_group_check=True)
                            for h in range(4):
                                last = nc.tensor.matmul(ps_bc[u % 2][:, h, :], sel_head[:, 4 * half + h, :],
                                                        sct[:, k % 2, j, :], start=False, stop=h == 3,
                                                        skip_group_check=True)
                            last.then_inc(bc_made[u], 1)
                    return run

                def turn_block_max(s):
                    pe.wait_ge(ml_made, s.nth)
                    nc.tensor.transpose(mlt_ps, ml[:, :], ident[:, :]).then_inc(ml_turned, 1)

                def sum_up(s):
                    k = s.slot
                    pe.wait_ge(msg_made, s.nth)
                    ahead = min(2, sh.BLOCKS - 1 - s.n) if isinstance(s.n, int) else 2
                    pe.wait_ge(hot_copied, 3 * (s.nth + ahead))
                    for g in range(G):
                        for j in range(J):
                            last = nc.tensor.matmul(node_ps[g * W:(g + 1) * W, :], hot[:, k, j * G + g, :],
                                                    msg[:, k % 2, j * G + g, :], start=j == 0, stop=j == J - 1,
                                                    tile_position=(0, g * W))
                    last.then_inc(node_summed, 1)

                def turn_sums(s):
                    pe.wait_ge(nodes_copied, 2 * s.nth)
                    if not (isinstance(s.n, int) and s.n < 1):
                        pe.wait_ge(added[G - 1], 2 * (s.nth - 1))
                    nc.tensor.transpose(num_ps, nodes[:, s.slot % 2, 0:DIM], ident[:, :])
                    nc.tensor.transpose(den_ps, nodes[:, s.slot % 2, DIM:DIM + AUXROWS], ident[:, :]
                                        ).then_inc(summed, 1)

                def turn_max(s):
                    pe.wait_ge(m_kept[G - 1], s.nth)
                    alone(pe)
                    nc.tensor.transpose(mt_ps, mnew[:, :, :].rearrange("h g w -> h (g w)"),
                                        ident[0:HEADS, 0:HEADS]).then_inc(m_turned, 1)

                def turn_hot(s):
                    pe.wait_ge(hot_made, s.nth)
                    if not (isinstance(s.n, int) and s.n < 1):
                        pe.wait_ge(hot_copied, 3 * (s.nth - 1))
                    for j in range(J):
                        last = nc.tensor.transpose(ps_hot[:, j, :], hot[:, s.slot, G * j:G * (j + 1), :].rearrange(
                            "p g w -> p (g w)"), ident[:, :])
                    last.then_inc(hot_turned, 1)

                def turn_scores(s):
                    pe.wait_ge(split[3], s.nth)
                    s.freed(pe, bc_read[2], 1)
                    for j in range(J):
                        last = nc.tensor.matmul(sct_ps[:, j, :], parts[:, j, :, :].rearrange("p a q -> p (a q)"),
                                                ident16[:, :], start=True, stop=True)
                    last.then_inc(sc_turned, 1)

                def bias(s):
                    k = s.slot
                    pe.wait_ge(attr_in[k], 16 * s.use)
                    s.freed(pe, sc_made, 1)
                    if not (isinstance(s.n, int) and s.n < 3):
                        pe.wait_ge(added[G - 1], 2 * (s.nth - 3))
                    for j in range(J):
                        last = nc.tensor.matmul(bias_ps[:, j * 32:(j + 1) * 32], att[:, k, j, :], we[:, :],
                                                start=True, stop=True)
                    last.then_inc(bias_made, 1)

                def spread_m(s):
                    pe.wait_ge(md_made, s.nth)
                    for j in range(J):
                        last = nc.tensor.matmul(me_ps[:, j * 32:(j + 1) * 32], hot_t[:, s.slot, j, :],
                                                md[:, :, :].rearrange("p g h -> p (g h)"), start=True, stop=True)
                    last.then_inc(m_spread, 1)

                def spread_scale(s):
                    pe.wait_ge(scale_made, s.nth)
                    if not (isinstance(s.n, int) and s.n < 1):
                        pe.wait_ge(added[G - 1], 2 * (s.nth - 1))
                    nc.tensor.matmul(sf_ps, sel_feat[:, :], scale[0:HEADS, :], start=True, stop=True)
                    nc.tensor.matmul(sa_ps, sel_aux[:, :], scale[:, :], start=True, stop=True
                                     ).then_inc(scale_spread, 1)

                steps(pe, sh.BLOCKS, U4, [(3, sum_up), (3, turn_sums), (0, turn_hot), (0, spread_q(0)),
                                          (1, turn_scores), (1, spread_scores((0, 1))), (2, turn_max),
                                          (1, spread_scores((2,))), (2, spread_m), (1, spread_scores((3,))),
                                          (0, spread_q(1)), (2, spread_scale), (0, bias), (1, turn_block_max)], w)

        @block.scalar
        def _(act):
            act.wait_ge(made, MADE)
            with passes(act, sh, env) as w:
                act.wait_ge(tables, w + 1)

                def scale_exp(s):
                    act.wait_ge(m_read[G - 1], 2 * s.nth)
                    nc.scalar.activation(fall[:, :], drop[:, :, :].rearrange("h g w -> h (g w)"), ACT.Relu,
                                         scale=-1.0).then_inc(fall_made, 1)
                    act.wait_ge(fall_made, s.nth)
                    s.freed(act, scale_spread, 1)
                    nc.scalar.activation(scale[0:HEADS, :], fall[:, :], ACT.Exp, bias=env["zero_t"][0:HEADS, :],
                                         scale=-1.0).then_inc(scale_made, 1)

                def high_part(s):
                    act.wait_ge(sc_made, s.nth)
                    nc.scalar.activation(parts[:, :, 0, :], sc[:, s.slot, :, :], ACT.Copy).then_inc(split[0], 1)

                def middle_part(s):
                    act.wait_ge(split[1], s.nth)
                    nc.scalar.activation(parts[:, :, 1, :], rest[:, :, :], ACT.Copy).then_inc(split[2], 1)

                def copy_hot(s):
                    k = s.slot
                    act.wait_ge(hot_turned, s.nth)
                    nc.scalar.activation(hot_b[:, k, :, :], ps_hot[:, :, :], ACT.Copy).then_inc(hot_copied, 1)
                    nc.scalar.activation(hot_t[:, k, :, :], ps_hot[:, :, :], ACT.Copy).then_inc(hot_copied, 1)
                    nc.scalar.activation(miss_b[:, k, :, :], ps_hot[:, :, :], ACT.Identity, bias=env["neg1_t"][:, :]
                                         ).then_inc(hot_copied, 1)

                def copy_scores(s):
                    act.wait_ge(sc_turned, s.nth)
                    s.freed(act, bc_made[3], 2)
                    nc.scalar.activation(sct[:, s.slot % 2, :, :], sct_ps, ACT.Copy).then_inc(sct_made, 1)

                def exp(s):
                    act.wait_ge(above_made, s.nth)
                    nc.scalar.activation(below[:, :], above[:, :], ACT.Relu, scale=-1.0).then_inc(below_made, 1)
                    act.wait_ge(below_made, s.nth)
                    s.freed(act, node_summed, 2)
                    nc.scalar.activation(msg[:, s.slot % 2, :, DIM:DIM + HEADS],
                                         below[:, :].rearrange("p (c h) -> p c h", h=HEADS), ACT.Exp,
                                         bias=env["zero_t"][:, :], scale=-1.0).then_inc(ex_made, 1)

                def copy_nodes(s):
                    act.wait_ge(node_summed, s.nth)
                    s.freed(act, summed, 2)
                    to = nodes[:, s.slot % 2, :]
                    nc.scalar.activation(to[:, 0:DIM], node_ps[:, 0:DIM], ACT.Copy).then_inc(nodes_copied, 1)
                    nc.scalar.activation(to[:, DIM + AUXD:DIM + AUXROWS], node_ps[:, DIM:MSG], ACT.Copy
                                         ).then_inc(nodes_copied, 1)

                steps(act, sh.BLOCKS, U4, [(3, copy_nodes), (1, high_part), (1, middle_part), (0, copy_hot),
                                           (1, copy_scores), (2, scale_exp),
                                           (2, exp)], w)


def normalise(nc, sh, env):
    ident, state, aux = env["ident"], env["state"], env["aux"]
    with ExitStack() as c:
        def tile(name, shape, dt=F32):
            return c.enter_context(nc.sbuf_tensor("nm_" + name, shape, dt))

        def psum(name, shape, dt=F32):
            return c.enter_context(nc.psum_tensor("nm_" + name, shape, dt))

        new = semaphores(nc, c)

        def sem(name):
            return new("nm_" + name)

        T = CH // P
        pick_den = tile("pick_den", [AUXROWS, DIM])
        pick_deg = tile("pick_deg", [AUXROWS, DIM])
        xt = tile("xt", [P, U4, T, DIM])
        inv = tile("inv", [P, U4, CH])
        sq = tile("sq", [P, U4, CH])
        x1 = tile("x1", [P, U4, T, DIM])
        stats = tile("stats", [P, U4, T, 6])
        mv = tile("mv", [P, U4, T, 2])
        root = tile("root", [P, U4, T])
        rstd = tile("rstd", [P, U4, T])
        hn = tile("hn", [P, U4, T, DIM])
        ht = tile("ht", [P, U4, CH])
        gs = tile("gs", [P, U4, CH])
        row = tile("row", [P, U4, T, DIM])
        den_ps, deg_ps, at_ps, ht_ps, row_ps = (psum(s, [P, CH]) for s in ("den", "deg", "at", "ht_ps", "row_ps"))
        (made, state_made, var_rooted, spread, den_cut, inverted, rooted, degd, attd, at_turned, x1_made, stat, aggr, std, normed, h_turned,
         relud, g_made, row_turned, row_made) = (sem(s) for s in (
             "made", "state_made", "var_rooted", "spread", "den_cut", "inverted", "rooted", "degd", "attd", "at_turned", "x1_made", "stat", "aggr",
             "std", "normed", "h_turned", "relud", "g_made", "row_turned", "row_made"))
        x_in = [sem(f"x_in{k}") for k in range(U4)]
        x1_out = [sem(f"x1_out{k}") for k in range(U4)]
        row_out = [sem(f"row_out{k}") for k in range(U4)]
        block = c.enter_context(nc.Block())
        width = chunk_width(sh)

        @block.sync
        def _(sp):
            def load(s):
                cw = width(s.n)
                s.freed(sp, x1_made, U4)
                sp.dma_start(xt[:, s.slot, 0:cw // P, :], rows_of(env["x"], s.n, cw)).then_inc(x_in[s.slot], 16)

            def store(s):
                cw = width(s.n)
                sp.wait_ge(x1_made, s.nth)
                sp.dma_start(rows_of(env["x1_tab"], s.n, cw), x1[:, s.slot, 0:cw // P, :]
                             ).then_inc(x1_out[s.slot], 16)
                sp.wait_ge(row_made, s.nth)
                sp.dma_start(rows_of(env["g_tabs"][0], s.n, cw), row[:, s.slot, 0:cw // P, :]
                             ).then_inc(row_out[s.slot], 16)

            steps(sp, sh.CHUNKS, U4, [(0, load), (4, store)])
            for k in range(U4):
                uses = len(range(k, sh.CHUNKS, U4))
                sp.wait_ge(x1_out[k], 16 * uses)
                sp.wait_ge(row_out[k], 16 * uses)

        @block.gpsimd
        def _(pool):
            nc.gpsimd.memset(pick_den[:, :], 1.0).then_inc(made, 1)
            nc.gpsimd.memset(pick_deg[:, :], 0.0).then_inc(made, 1)
            pool.wait_ge(made, 2)
            nc.gpsimd.affine_select(out=pick_den[:, :], in_=pick_den[:, :], compare_op=ALU.is_ge, fill=0.0,
                                    base=HC * AUXD, pattern=[[1, DIM]], channel_multiplier=-HC).then_inc(made, 1)
            nc.gpsimd.affine_select(out=pick_deg[:, :], in_=pick_deg[:, :], compare_op=ALU.not_equal, fill=1.0,
                                    base=-AUXN, pattern=[[0, DIM]], channel_multiplier=1).then_inc(made, 1)
            pool.wait_ge(made, 4)
            nc.gpsimd.affine_select(out=pick_den[:, :], in_=pick_den[:, :], compare_op=ALU.is_ge, fill=0.0,
                                    base=HC - 1 - HC * AUXD, pattern=[[-1, DIM]], channel_multiplier=HC
                                    ).then_inc(made, 1)

        @block.vector
        def _(dve):
            def attention(s):
                k, cw = s.slot, width(s.n)
                cols = bass.ds(s.n * CH, cw)
                dve.wait_ge(spread, s.nth)
                s.freed(dve, at_turned, U4)
                nc.vector.tensor_scalar(inv[:, k, 0:cw], den_ps[:, 0:cw], 0.5, None, ALU.max).then_inc(den_cut, 1)
                dve.wait_ge(den_cut, s.nth)
                nc.vector.reciprocal(inv[:, k, 0:cw], inv[:, k, 0:cw]).then_inc(inverted, 1)
                dve.wait_ge(inverted, s.nth)
                nc.vector.tensor_tensor(inv[:, k, 0:cw], state[:, cols], inv[:, k, 0:cw], ALU.mult).then_inc(attd, 1)
                dve.wait_ge(rooted, s.nth)
                nc.vector.reciprocal(aux[:, cols], sq[:, k, 0:cw]).then_inc(degd, 1)

            def layernorm(s):
                k, cw = s.slot, width(s.n)
                t = cw // P
                dve.wait_ge(at_turned, s.nth)
                dve.wait_ge(x_in[k], 16 * s.use)
                s.slot_freed(dve, x1_out[k], 16)
                nc.vector.tensor_tensor(x1[:, k, 0:t, :], at_ps[:, 0:cw].rearrange("p (t d) -> p t d", d=DIM),
                                        xt[:, k, 0:t, :], ALU.add).then_inc(x1_made, 1)
                dve.wait_ge(x1_made, s.nth)
                for i in range(t):
                    last = nc.vector.bn_stats(stats[:, k, i, :], x1[:, k, i, :])
                last.then_inc(stat, 1)
                dve.wait_ge(stat, s.nth)
                alone(dve)
                for i in range(t):
                    last = nc.vector.bn_aggr(mv[:, k, i, :], stats[:, k, i, :])
                last.then_inc(aggr, 1)

            def apply_norm(s):
                k = s.slot
                t = width(s.n) // P
                dve.wait_ge(var_rooted, s.nth)
                nc.vector.reciprocal(rstd[:, k, 0:t], root[:, k, 0:t]).then_inc(std, 1)
                dve.wait_ge(std, s.nth)
                s.freed(dve, h_turned, U4)
                for i in range(t):
                    last = nc.vector.tensor_scalar(hn[:, k, i, :], x1[:, k, i, :], mv[:, k, i, 0:1],
                                                   rstd[:, k, i:i + 1], ALU.subtract, ALU.mult)
                last.then_inc(normed, 1)

            def scale_h(s):
                k, cw = s.slot, width(s.n)
                cols = bass.ds(s.n * CH, cw)
                dve.wait_ge(relud, s.nth)
                dve.wait_ge(degd, s.nth)
                s.freed(dve, row_turned, U4)
                s.freed(dve, state_made, U4)
                nc.vector.tensor_tensor(gs[:, k, 0:cw], ht[:, k, 0:cw], aux[:, cols], ALU.mult).then_inc(g_made, 1)

            steps(dve, sh.CHUNKS, U4, [(4, scale_h), (3, apply_norm), (2, layernorm), (1, attention)])

        @block.tensor
        def _(pe):
            pe.wait_ge(made, 5)

            def spread_aux(s):
                cw = width(s.n)
                cols = bass.ds(s.n * CH, cw)
                s.freed(pe, den_cut, 1)
                s.freed(pe, rooted, 1)
                nc.tensor.matmul(den_ps[:, 0:cw], pick_den[:, :], aux[0:AUXROWS, cols], start=True, stop=True)
                nc.tensor.matmul(deg_ps[:, 0:cw], pick_deg[:, :], aux[0:AUXROWS, cols], start=True, stop=True
                                 ).then_inc(spread, 1)

            def turn_att(s):
                cw = width(s.n)
                pe.wait_ge(attd, s.nth)
                s.freed(pe, x1_made, 1)
                for i in range(cw // P):
                    last = nc.tensor.transpose(at_ps[:, i * P:(i + 1) * P], inv[:, s.slot, i * P:(i + 1) * P],
                                               ident[:, :])
                last.then_inc(at_turned, 1)

            def turn_h(s):
                cw = width(s.n)
                pe.wait_ge(normed, s.nth)
                s.freed(pe, relud, 1)
                for i in range(cw // P):
                    last = nc.tensor.transpose(ht_ps[:, i * P:(i + 1) * P], hn[:, s.slot, i, :], ident[:, :])
                last.then_inc(h_turned, 1)

            def turn_row(s):
                cw = width(s.n)
                pe.wait_ge(g_made, s.nth)
                s.freed(pe, row_made, 1)
                for i in range(cw // P):
                    last = nc.tensor.transpose(row_ps[:, i * P:(i + 1) * P], gs[:, s.slot, i * P:(i + 1) * P],
                                               ident[:, :])
                last.then_inc(row_turned, 1)

            steps(pe, sh.CHUNKS, U4, [(4, turn_row), (3, turn_h), (1, turn_att), (0, spread_aux)])

        @block.scalar
        def _(act):
            def root_deg(s):
                k, cw = s.slot, width(s.n)
                act.wait_ge(spread, s.nth)
                s.freed(act, degd, U4)
                nc.scalar.activation(sq[:, k, 0:cw], deg_ps[:, 0:cw], ACT.Sqrt, bias=env["one_t"][:, :]
                                     ).then_inc(rooted, 1)

            def relu(s):
                k, cw = s.slot, width(s.n)
                act.wait_ge(h_turned, s.nth)
                s.freed(act, g_made, U4)
                nc.scalar.activation(ht[:, k, 0:cw], ht_ps[:, 0:cw], ACT.Relu).then_inc(relud, 1)

            def copy_row(s):
                k, cw = s.slot, width(s.n)
                act.wait_ge(row_turned, s.nth)
                s.slot_freed(act, row_out[k], 16)
                nc.scalar.activation(row[:, k, 0:cw // P, :].rearrange("p t d -> p (t d)"), row_ps[:, 0:cw],
                                     ACT.Copy).then_inc(row_made, 1)

            def copy_state(s):
                cw = width(s.n)
                act.wait_ge(g_made, s.nth)
                act.wait_ge(attd, s.nth)
                nc.scalar.activation(state[:, bass.ds(s.n * CH, cw)], gs[:, s.slot, 0:cw], ACT.Copy
                                     ).then_inc(state_made, 1)

            def root_var(s):
                k, t = s.slot, width(s.n) // P
                act.wait_ge(aggr, s.nth)
                s.freed(act, std, U4)
                nc.scalar.activation(root[:, k, 0:t], mv[:, k, 0:t, 1:2].rearrange("p t o -> p (t o)"), ACT.Sqrt,
                                     bias=env["eps_t"][:, :]).then_inc(var_rooted, 1)

            steps(act, sh.CHUNKS, U4, [(4, copy_state), (4, copy_row), (2, root_var), (3, relu), (0, root_deg)])


def chunk_width(sh):
    return lambda n: sh.LW if isinstance(n, int) and n == sh.CHUNKS - 1 else CH


def rows_of(tab, n, cw):
    return tab[bass.ds(n * CH, cw), :].rearrange("(t p) d -> p t d", p=P)


def aggregate(nc, sh, layer, env):
    state = env["state"]
    with ExitStack() as c:
        def tile(name, shape, dt=F32):
            return c.enter_context(nc.sbuf_tensor(f"ag{layer}_{name}", shape, dt))

        new = semaphores(nc, c)

        def sem(name):
            return new(f"ag{layer}_{name}")

        idx = tile("idx", [P, U4, C], U32)
        rows = tile("rows", [P, U4, C, DIM])
        hot = tile("hot", [P, U4, C, W])
        base_n = tile("base_n", [P, sh.GROUPS], I32)
        sum_ps = [c.enter_context(nc.psum_tensor(f"ag{layer}_sum{k}", [P, 512], F32)) for k in range(2)]
        base_in, tables, changed, hot_made, summed = (sem(s) for s in (
            "base_in", "tables", "changed", "hot_made", "summed"))
        idx_in = [sem(f"idx_in{k}") for k in range(U4)]
        rows_in = [sem(f"rows_in{k}") for k in range(U4)]
        added = [sem(f"added{g}") for g in range(G)]
        block = c.enter_context(nc.Block())

        @block.sync
        def _(sp):
            sp.dma_start(base_n[:, :], env["base_tab"].unsqueeze(0).to_broadcast([P, sh.GROUPS])
                         ).then_inc(base_in, 16)
            with passes(sp, sh, env) as w:
                sp.wait_ge(tables, w + 1)

                def load(s):
                    s.slot_freed(sp, rows_in[s.slot], 16 * C)
                    sp.dma_start(idx[:, s.slot, :], env["src_blocks"][bass.ds(s.n, 1), :, :].squeeze(0)
                                 ).then_inc(idx_in[s.slot], 16)

                steps(sp, sh.BLOCKS, U4, [(0, load)], w)

        @block.gpsimd
        def _(pool):
            with passes(pool, sh, env) as w:
                pool.wait_ge(tables, w + 1)

                def gather(s):
                    pool.wait_ge(idx_in[s.slot], 16 * s.use)
                    s.freed(pool, summed, U4)
                    alone(pool)
                    for ch in range(C):
                        nc.gpsimd.indirect_dma_start(
                            rows[:, s.slot, ch, :], None, env["g_tabs"][layer],
                            bass.IndirectOffsetOnAxis(ap=idx[:, s.slot, ch:ch + 1], axis=0)
                        ).then_inc(rows_in[s.slot], 16)

                steps(pool, sh.BLOCKS, U4, [(0, gather)], w)

        @block.vector
        def _(dve):
            first_pass(nc, dve, env, base_n, base_in, tables, changed)
            with passes(dve, sh, env) as w:
                dve.wait_ge(changed, 2 * w + 2)
                dve.wait_ge(tables, w + 1)

                def hot_one(s):
                    s.freed(dve, summed, U4)
                    one_hot(nc, dve, env, hot[:, s.slot, :, :], s.n).then_inc(hot_made, 1)

                def merge(s):
                    dve.wait_ge(summed, s.nth)
                    alone(dve)
                    for g, b in enumerate(bases(dve, sh, env, s.n)):
                        into = state[:, bass.ds(b, W)]
                        if g:
                            dve.wait_ge(added[g - 1], s.nth)
                        else:
                            s.freed(dve, added[G - 1], 1)
                        nc.vector.tensor_tensor(into, into, sum_ps[s.slot % 2][:, g * W:(g + 1) * W],
                                                ALU.add).then_inc(added[g], 1)

                steps(dve, sh.BLOCKS, U4, [(0, hot_one), (1, merge)], w)
                next_pass(nc, dve, sh, env, tables, changed, w)

        @block.tensor
        def _(pe):
            with passes(pe, sh, env) as w:
                pe.wait_ge(tables, w + 1)

                def sum_up(s):
                    k = s.slot
                    pe.wait_ge(rows_in[k], 16 * C * s.use)
                    pe.wait_ge(hot_made, s.nth)
                    s.freed(pe, added[G - 1], 2)
                    for g in range(G):
                        for j in range(J):
                            last = nc.tensor.matmul(sum_ps[k % 2][:, g * W:(g + 1) * W], rows[:, k, j * G + g, :],
                                                    hot[:, k, j * G + g, :], start=j == 0, stop=j == J - 1)
                    last.then_inc(summed, 1)

                steps(pe, sh.BLOCKS, U4, [(0, sum_up)], w)


def transform(nc, sh, layer, env):
    ident, state, dinv, vec = env["ident"], env["state"], env["aux"], env["vec_t"]
    w1, w2, w3 = env["weights"]
    with ExitStack() as c:
        def tile(name, shape, dt=F32):
            return c.enter_context(nc.sbuf_tensor(f"tr{layer}_{name}", shape, dt))

        new = semaphores(nc, c)

        def sem(name):
            return new(f"tr{layer}_{name}")

        T = CH // P
        halves = 2 if layer == 0 else 1
        lag = 1 if layer == 0 else 0
        at = (0, 6, 9)[layer]
        act_fn = ACT.Identity if layer == 2 else ACT.Relu
        r = tile("r", [P, U4, 2, CH]) if layer == 0 else None
        gs = tile("gs", [P, U4, CH])
        hb = tile("hb", [P, U4, halves, CH])
        stats = tile("stats", [P, 2, sh.CHUNKS, 6])
        mv = tile("mv", [P, 2, 2])
        root = tile("root", [P, 2])
        gain = tile("gain", [P, 2])
        shift = tile("shift", [P, 2])
        row = tile("row", [P, U4, T, DIM])
        x1 = tile("x1", [P, U4, T, DIM])
        z_ps = [[c.enter_context(nc.psum_tensor(f"tr{layer}_z{k}{h}", [P, CH], F32)) for h in range(2)]
                for k in range(2)] if layer == 0 else None
        o_ps = c.enter_context(nc.psum_tensor(f"tr{layer}_o", [P, CH], F32))
        row_ps = c.enter_context(nc.psum_tensor(f"tr{layer}_rowps", [P, CH], F32))
        (w_in, scaled, z_made, r_made, stat, aggr, std, gained, shifting, shifted, z2_made, r2_made, h_made, o_made,
         g_made, row_turned, row_made, rooted, state_made) = (sem(s) for s in (
             "w_in", "scaled", "z_made", "r_made", "stat", "aggr", "std", "gained", "shifting", "shifted", "z2_made",
             "r2_made", "h_made", "o_made", "g_made", "row_turned", "row_made", "rooted",
             "state_made"))
        x_in = [sem(f"x_in{k}") for k in range(U4)]
        row_out = [sem(f"row_out{k}") for k in range(U4)]
        block = c.enter_context(nc.Block())
        width = chunk_width(sh)
        dest = env["out"] if layer == 2 else env["g_tabs"][layer + 1]

        def cols_of(s):
            return bass.ds(s.n * CH, width(s.n))

        @block.sync
        def _(sp):
            if layer == 0:
                sp.dma_start(w1[:, :, :].rearrange("p a d -> p (a d)"), env["w1"]).then_inc(w_in, 16)
                sp.dma_start(w2[:, :, :], env["w2"].rearrange("(a p) d -> p a d", p=P)).then_inc(w_in, 16)
                sp.dma_start(w3[:, :], env["w3"]).then_inc(w_in, 16)

            def load(s):
                if layer == 2:
                    s.freed(sp, row_made, U4)
                    sp.dma_start(x1[:, s.slot, 0:width(s.n) // P, :], rows_of(env["x1_tab"], s.n, width(s.n))
                                 ).then_inc(x_in[s.slot], 16)

            def store(s):
                sp.wait_ge(row_made, s.nth)
                sp.dma_start(rows_of(dest, s.n, width(s.n)), row[:, s.slot, 0:width(s.n) // P, :]
                             ).then_inc(row_out[s.slot], 16)

            steps(sp, sh.CHUNKS, U4, [(0, load), (lag + 2, store)])
            for k in range(U4):
                sp.wait_ge(row_out[k], 16 * len(range(k, sh.CHUNKS, U4)))

        @block.vector
        def _(dve):
            def scale(s):
                nc.vector.tensor_tensor(state[:, cols_of(s)], state[:, cols_of(s)], dinv[:, cols_of(s)],
                                        ALU.mult).then_inc(scaled, 1)

            def statistics(s):
                cv = sh.LV if width(s.n) != CH or (isinstance(s.n, int) and s.n == sh.CHUNKS - 1) else CH
                dve.wait_ge(r_made, halves * s.nth)
                for h in range(halves):
                    src = r[:, s.slot, h, 0:cv] if layer == 0 else state[:, bass.ds(s.n * CH, cv)]
                    last = nc.vector.bn_stats(stats[:, h, bass.ds(s.n, 1), :].rearrange("p a b -> p (a b)"), src)
                last.then_inc(stat, 1)

            steps(dve, sh.CHUNKS, U4, [(2, statistics), (0, scale)])
            dve.wait_ge(stat, sh.CHUNKS)
            for h in range(halves):
                nc.vector.bn_aggr(mv[:, h, :], stats[:, h, :, :].rearrange("p a b -> p (a b)")).then_inc(aggr, 1)
            dve.wait_ge(aggr, halves)
            hs = slice(0, halves)
            dve.wait_ge(rooted, 1)
            nc.vector.reciprocal(gain[:, hs], root[:, hs]).then_inc(std, 1)
            dve.wait_ge(std, 1)
            nc.vector.tensor_tensor(gain[:, hs], gain[:, hs], vec[:, at + halves:at + 2 * halves],
                                    ALU.mult).then_inc(gained, 1)
            dve.wait_ge(gained, 1)
            nc.vector.tensor_tensor(shift[:, hs], mv[:, hs, 0:1].rearrange("p h o -> p (h o)"), gain[:, hs],
                                    ALU.mult).then_inc(shifting, 1)
            dve.wait_ge(shifting, 1)
            nc.vector.tensor_tensor(shift[:, hs], vec[:, at + 2 * halves:at + 3 * halves], shift[:, hs],
                                    ALU.subtract).then_inc(shifted, 1)
            dve.wait_ge(shifted, 1)

            def normed(s):
                cw = width(s.n)
                if layer == 0:
                    dve.wait_ge(r2_made, 2 * s.nth)
                s.freed(dve, o_made if layer < 2 else row_turned, U4)
                for h in range(halves):
                    src = r[:, s.slot, h, 0:cw] if layer == 0 else state[:, cols_of(s)]
                    last = nc.vector.tensor_scalar(hb[:, s.slot, h, 0:cw], src, gain[:, h:h + 1], shift[:, h:h + 1],
                                                   ALU.mult, ALU.add)
                last.then_inc(h_made, 1)

            def table(s):
                k, cw = s.slot, width(s.n)
                if layer < 2:
                    dve.wait_ge(o_made, s.nth)
                    s.freed(dve, row_turned, U4)
                    s.freed(dve, state_made, U4)
                    nc.vector.tensor_tensor(gs[:, k, 0:cw], o_ps[:, 0:cw], dinv[:, cols_of(s)],
                                            ALU.mult).then_inc(g_made, 1)
                else:
                    dve.wait_ge(row_turned, s.nth)
                    dve.wait_ge(x_in[k], 16 * s.use)
                    s.slot_freed(dve, row_out[k], 16)
                    nc.vector.tensor_tensor(row[:, k, 0:cw // P, :].rearrange("p t d -> p (t d)"), row_ps[:, 0:cw],
                                            x1[:, k, 0:cw // P, :].rearrange("p t d -> p (t d)"),
                                            ALU.add).then_inc(row_made, 1)

            steps(dve, sh.CHUNKS, U4, [(lag + 1, table), (lag, normed)])

        @block.tensor
        def _(pe):
            def before(freed_by, made):
                def run(s):
                    cw = width(s.n)
                    pe.wait_ge(scaled, s.nth)
                    if not (isinstance(s.n, int) and s.n < 2):
                        pe.wait_ge(freed_by, 2 * (s.nth - 2))
                    for h in range(2):
                        last = nc.tensor.matmul(z_ps[s.slot % 2][h][:, 0:cw], w1[:, h, :], state[:, cols_of(s)],
                                                start=True, stop=True)
                    last.then_inc(made, 1)
                return run

            def after(s):
                k, cw = s.slot, width(s.n)
                pe.wait_ge(h_made, s.nth)
                s.freed(pe, g_made, 1)
                for h in range(halves):
                    last = nc.tensor.matmul(o_ps[:, 0:cw], w2[:, h, :] if layer == 0 else w3[:, :],
                                            hb[:, k, h, 0:cw], start=h == 0, stop=h == halves - 1)
                last.then_inc(o_made, 1)

            def turn(s):
                cw = width(s.n)
                pe.wait_ge(g_made if layer < 2 else h_made, s.nth)
                s.freed(pe, row_made, 1)
                for i in range(cw // P):
                    src = gs[:, s.slot, i * P:(i + 1) * P] if layer < 2 else hb[:, s.slot, 0, i * P:(i + 1) * P]
                    last = nc.tensor.transpose(row_ps[:, i * P:(i + 1) * P], src, ident[:, :])
                last.then_inc(row_turned, 1)

            if layer == 0:
                pe.wait_ge(w_in, 48)
                steps(pe, sh.CHUNKS, U4, [(0, before(r_made, z_made))])
                pe.wait_ge(r_made, 2 * sh.CHUNKS)
                steps(pe, sh.CHUNKS, U4, [(lag + 2, turn), (lag + 1, after), (0, before(r2_made, z2_made))])
            elif layer == 1:
                steps(pe, sh.CHUNKS, U4, [(lag + 2, turn), (lag + 1, after)])
            else:
                steps(pe, sh.CHUNKS, U4, [(lag, turn)])

        @block.scalar
        def _(act):
            def nonlinear(made_by, made, used_by):
                def run(s):
                    k, cw = s.slot, width(s.n)
                    act.wait_ge(made_by, s.nth)
                    if layer == 0:
                        s.freed(act, used_by, U4)
                    for h in range(halves):
                        src = z_ps[k % 2][h][:, 0:cw] if layer == 0 else state[:, cols_of(s)]
                        to = r[:, k, h, 0:cw] if layer == 0 else state[:, cols_of(s)]
                        nc.scalar.activation(to, src, act_fn, bias=vec[:, at + h:at + h + 1]).then_inc(made, 1)
                return run

            def copy_row(s):
                k, cw = s.slot, width(s.n)
                act.wait_ge(row_turned, s.nth)
                s.slot_freed(act, row_out[k], 16)
                nc.scalar.activation(row[:, k, 0:cw // P, :].rearrange("p t d -> p (t d)"), row_ps[:, 0:cw],
                                     ACT.Copy).then_inc(row_made, 1)

            def copy_state(s):
                act.wait_ge(g_made, s.nth)
                nc.scalar.activation(state[:, cols_of(s)], gs[:, s.slot, 0:width(s.n)], ACT.Copy
                                     ).then_inc(state_made, 1)

            steps(act, sh.CHUNKS, U4, [(0, nonlinear(z_made if layer == 0 else scaled, r_made, stat))])
            act.wait_ge(aggr, halves)
            nc.scalar.activation(root[:, 0:halves], mv[:, 0:halves, 1:2].rearrange("p h o -> p (h o)"), ACT.Sqrt,
                                 bias=env["eps_t"][:, :]).then_inc(rooted, 1)
            if layer == 0:
                steps(act, sh.CHUNKS, U4, [(lag + 2, copy_state), (lag + 2, copy_row),
                                            (0, nonlinear(z2_made, r2_made, h_made))])
            elif layer == 1:
                steps(act, sh.CHUNKS, U4, [(lag + 2, copy_state), (lag + 2, copy_row)])


def kernel(**inputs):
    import numpy as np
    import concourse.bacc as bacc
    from concourse.bass_utils import run_bass_kernel_spmd

    a = {k: np.asarray(v) for k, v in inputs.items()}
    n_nodes, n_edges = a["x"].shape[0], a["src"].shape[0]
    sh = Shapes(n_nodes, n_edges)
    pad = sh.BLOCKS * BLOCK - n_edges

    def by_chunk(v, fill):
        v = np.concatenate([v, np.full(pad, fill, v.dtype)]).reshape(sh.BLOCKS, G, J, P)
        return v.transpose(3, 0, 2, 1).reshape(P, sh.BLOCKS, C)

    dst = np.concatenate([a["dst"], np.full(pad, SENTINEL, a["dst"].dtype)])
    attr = np.concatenate([a["edge_attr_32"], np.zeros((pad, EDIM), a["edge_attr_32"].dtype)])
    attr = attr.reshape(sh.BLOCKS, G, J, P, EDIM).transpose(0, 1, 4, 2, 3).reshape(sh.BLOCKS, P, J * P)

    def halves(name):
        return a[name].reshape(-1, P).T

    arrays = {
        "x": np.concatenate([a["x"], np.zeros((sh.NS - n_nodes, DIM), a["x"].dtype)]),
        "src_blocks": by_chunk(a["src"], 0).transpose(1, 0, 2).view(np.uint32),
        "dst_cols": by_chunk(a["dst"], SENTINEL).reshape(P, -1),
        "dst_groups": dst.reshape(sh.GP, -1),
        "attr": attr,
        "wqkv": np.concatenate([a["L0_gnn_Wq"].T, a["L0_gnn_Wk"].T, a["L0_gnn_Wv"].T], 1),
        "wet": a["L0_gnn_We"].T,
        "w1": a["L1_gnn_W1"], "w2": a["L1_gnn_W2"], "w3": a["L1_gnn_W3"],
        "vecs": np.concatenate([halves(f"L1_gnn_{v}{i}") for i in (1, 2, 3) for v in ("b", "g", "beta")], 1),
    }
    arrays = {k: np.ascontiguousarray(v) for k, v in arrays.items()}
    nc = bacc.Bacc("TRN2", target_bir_lowering=False, num_devices=1)
    args = [nc.dram_tensor(k, v.shape, mybir.dt.from_np(v.dtype), kind="ExternalInput").ap()
            for k, v in arrays.items()]
    out = nc.dram_tensor("out", (sh.NS, DIM), F32, kind="ExternalOutput").ap()
    build(nc, sh, *args, out)
    result = run_bass_kernel_spmd(nc, [arrays], core_ids=[0])
    return result.results[0]["out"][:n_nodes]
```

```python
from contextlib import ExitStack

import concourse.bass as bass
from concourse import mybir

ALU = mybir.AluOpType
ACT = mybir.ActivationFunctionType
AX = mybir.AxisListType
F32 = mybir.dt.float32
BF16 = mybir.dt.bfloat16
I32 = mybir.dt.int32
U32 = mybir.dt.uint32

P = 128
W = 32
G = 4
J = 2
C = G * J
BLOCK = C * P
HEADS = 8
HC = 16
DIM = HEADS * HC
EDIM = 32
CH = 512
SENTINEL = 1 << 20
BIG = float(2 ** 100)
EPS = 1e-5
AUXD = 64
AUXN = 72
AUXROWS = 73
MSG = DIM + HEADS + 1
SLOTS = 4


class Shapes:

    def __init__(self, n_nodes, n_edges):
        self.N, self.E = n_nodes, n_edges
        self.NS = -(-(n_nodes + W) // 256) * 256
        self.LAST = self.NS - W
        self.BLOCKS = -(-n_edges // (BLOCK * SLOTS)) * SLOTS
        self.GROUPS = self.BLOCKS * G
        self.GP = max(p for p in range(1, P + 1) if self.GROUPS % p == 0)
        self.GF = self.GROUPS // self.GP
        self.TILES = self.NS // P
        self.FULL = n_nodes // CH
        self.CHUNKS = self.FULL + 1
        self.LW = self.NS - self.FULL * CH
        self.LV = n_nodes - self.FULL * CH
        assert 0 < self.LV <= self.LW <= CH


class Step:

    def __init__(self, n, slot, nth, use, use_in_pass):
        self.n, self.slot, self.nth, self.use, self.use_in_pass = n, slot, nth, use, use_in_pass

    def freed(self, eng, sem, depth):
        if not (isinstance(self.n, int) and self.n < depth):
            eng.wait_ge(sem, self.nth - depth)

    def slot_freed(self, eng, sem, count):
        if not (isinstance(self.n, int) and self.use_in_pass == 0):
            eng.wait_ge(sem, (self.use - 1) * count)


def alone(eng):
    eng.nop(nofuse=True)


def steps(eng, total, slots, stages, pass_=None):
    most = max(lag for lag, _ in stages)
    first = 1 + -(-most // slots)
    full = total // slots

    def step(n, slot, use):
        if pass_ is None:
            return Step(n, slot, n + 1, use + 1, use)
        return Step(n, slot, pass_ * total + n + 1, pass_ * full + use + 1, use)

    def static(i):
        for lag, stage in stages:
            n = i - lag
            if 0 <= n < total:
                stage(step(n, n % slots, n // slots))

    assert pass_ is None or total % slots == 0
    loop = range(first * slots, full * slots) if full > first else range(0)
    head = loop.start if loop else total + most
    for i in range(head):
        static(i)
    if loop:
        with eng.Fori(first, full) as t:
            for k in range(slots):
                for lag, stage in stages:
                    stage(step(t * slots + (k - lag), (k - lag) % slots, t + (k - lag) // slots))
        for i in range(loop.stop, total + most):
            static(i)


def build(nc, sh, x, src_blocks, dst_cols, dst_groups, attr, wqkv, wet, w1, w2, w3, vecs, out):
    ctx = ExitStack()

    def sb(name, shape, dt=F32):
        return ctx.enter_context(nc.sbuf_tensor(name, shape, dt))

    with ctx:
        q_tab = nc.dram_tensor("q_tab", (sh.NS, 3 * DIM), BF16, kind="Internal").ap()
        kv_tab = nc.dram_tensor("kv_tab", (sh.NS, 2 * DIM), F32, kind="Internal").ap()
        x1_tab = nc.dram_tensor("x1_tab", (sh.NS, DIM), F32, kind="Internal").ap()
        g_tabs = [nc.dram_tensor(f"g_tab{i}", (sh.NS, DIM), F32, kind="Internal").ap() for i in range(3)]
        base_tab = nc.dram_tensor("base_tab", (sh.GROUPS,), I32, kind="Internal").ap()

        state = sb("state", [P, sh.NS])
        aux = sb("aux", [P, sh.NS])
        dst_f = sb("dst_f", [P, sh.BLOCKS * C])
        dst_rel = sb("dst_rel", [P, sh.BLOCKS * C])
        base_w = sb("base_w", [P, sh.GROUPS])
        base_i = sb("base_i", [1, sh.GROUPS], I32)
        windows = sb("windows", [1, 1], I32)
        ident = sb("ident", [P, P])
        iota_w = sb("iota_w", [P, W])
        eps_t = sb("eps_t", [P, 1])
        one_t = sb("one_t", [P, 1])
        neg1_t = sb("neg1_t", [P, 1])
        zero_t = sb("zero_t", [P, 1])
        vec_t = sb("vec_t", [P, 12])

        prepare(nc, sh, locals())
        project(nc, sh, locals())
        attend(nc, sh, locals())
        normalise(nc, sh, locals())
        with nc.sbuf_tensor("w1_sb", [P, 2, DIM], F32) as w1_sb, \
                nc.sbuf_tensor("w2_sb", [P, 2, DIM], F32) as w2_sb, \
                nc.sbuf_tensor("w3_sb", [P, DIM], F32) as w3_sb:
            weights = (w1_sb, w2_sb, w3_sb)
            for layer in range(3):
                aggregate(nc, sh, layer, locals())
                transform(nc, sh, layer, locals())


def semaphores(nc, ctx):
    made = []

    def clear():
        nc.clear_and_free_semaphores(made)
        nc.all_engine_barrier()

    ctx.callback(clear)

    def sem(name):
        made.append(nc.alloc_semaphore(name))
        return made[-1]
    return sem


def prepare(nc, sh, env):
    ident, iota_w, windows, base_tab = env["ident"], env["iota_w"], env["windows"], env["base_tab"]
    state, aux, dst_f, base_w, base_i = env["state"], env["aux"], env["dst_f"], env["base_w"], env["base_i"]
    wide = sh.GF * J * P
    with ExitStack() as c:
        def tile(name, shape, dt=F32):
            return c.enter_context(nc.sbuf_tensor(name, shape, dt))

        raw = tile("raw", [P, wide], I32)
        val = tile("val", [P, wide])
        low = tile("low", [P, wide])
        dst_i = tile("dst_i", [P, sh.BLOCKS * C], I32)
        base_n = tile("base_n", [P, sh.GROUPS], I32)
        least = tile("least", [P, sh.GF])
        most = tile("most", [P, sh.GF])
        span = tile("span", [P, sh.GF])
        span1 = tile("span1", [P, 1])
        top = tile("top", [1, 2])
        least_i = tile("least_i", [P, sh.GF], I32)
        turned = c.enter_context(nc.psum_tensor("turned", [P, P], F32))
        new = semaphores(nc, c)
        loaded, cast, lowered, reduced, spanned, widest, topped, base_made, base_out, base_back, cols_in, made = (
            new(s) for s in
            ("loaded", "cast", "lowered", "reduced", "spanned", "widest", "topped", "base_made", "base_out",
             "base_back", "cols_in", "made"))
        block = c.enter_context(nc.Block())

        @block.sync
        def _(sp):
            sp.dma_start(raw[0:sh.GP, :], env["dst_groups"]).then_inc(loaded, 16)
            sp.dma_start(dst_i[:, :], env["dst_cols"]).then_inc(cols_in, 16)
            sp.dma_start(env["vec_t"][:, :], env["vecs"]).then_inc(cols_in, 16)
            sp.wait_ge(base_made, 1)
            sp.dma_start(base_tab.rearrange("(p f) -> p f", p=sh.GP), least_i[0:sh.GP, :]).then_inc(base_out, 16)
            sp.wait_ge(base_out, 16)
            sp.dma_start(base_n[:, :], base_tab.unsqueeze(0).to_broadcast([P, sh.GROUPS])).then_inc(base_back, 16)
            sp.wait_ge(base_back, 16)

        @block.gpsimd
        def _(pool):
            nc.gpsimd.memset(ident[:, :], 0.0).then_inc(made, 1)
            pool.wait_ge(made, 1)
            nc.gpsimd.affine_select(out=ident[:, :], in_=ident[:, :], compare_op=ALU.not_equal, fill=1.0, base=0,
                                    pattern=[[-1, P]], channel_multiplier=1).then_inc(made, 1)
            nc.gpsimd.iota(iota_w[:, :], pattern=[[1, W]], base=0, channel_multiplier=0,
                           allow_small_or_imprecise_dtypes=True)
            nc.gpsimd.memset(env["eps_t"][:, :], EPS)
            nc.gpsimd.memset(env["one_t"][:, :], 1.0)
            nc.gpsimd.memset(env["neg1_t"][:, :], -1.0)
            nc.gpsimd.memset(env["zero_t"][:, :], 0.0)
            nc.gpsimd.memset(state[:, :], 0.0)
            nc.gpsimd.memset(aux[:, :], 0.0).then_inc(made, 1)
            pool.wait_ge(made, 3)
            nc.gpsimd.memset(aux[0:HEADS, :], -BIG).then_inc(made, 1)

        @block.vector
        def _(dve):
            q = slice(0, sh.GP)
            dve.wait_ge(loaded, 16)
            nc.vector.tensor_copy(val[q, :], raw[q, :]).then_inc(cast, 1)
            dve.wait_ge(cast, 1)
            nc.vector.tensor_reduce(least[q, :], val[q, :].rearrange("p (f e) -> p f e", f=sh.GF), AX.X,
                                    ALU.min).then_inc(reduced, 1)
            nc.vector.tensor_scalar(low[q, :], val[q, :], float(SENTINEL), -2.0 * SENTINEL, ALU.is_ge,
                                    ALU.mult).then_inc(lowered, 1)
            dve.wait_ge(lowered, 1)
            nc.vector.tensor_tensor(low[q, :], low[q, :], val[q, :], ALU.add).then_inc(lowered, 1)
            dve.wait_ge(lowered, 2)
            nc.vector.tensor_reduce(most[q, :], low[q, :].rearrange("p (f e) -> p f e", f=sh.GF), AX.X,
                                    ALU.max).then_inc(reduced, 1)
            dve.wait_ge(reduced, 2)
            nc.vector.tensor_tensor(span[q, :], most[q, :], least[q, :], ALU.subtract).then_inc(spanned, 1)
            nc.vector.tensor_scalar(least[q, :], least[q, :], float(sh.LAST), None, ALU.min).then_inc(spanned, 1)
            dve.wait_ge(spanned, 2)
            nc.vector.tensor_copy(least_i[q, :], least[q, :]).then_inc(base_made, 1)
            nc.vector.tensor_reduce(span1[q, :], span[q, :], AX.X, ALU.max).then_inc(spanned, 1)
            dve.wait_ge(widest, 1)
            nc.vector.tensor_reduce(top[:, 0:1], turned[0:1, 0:sh.GP], AX.X, ALU.max).then_inc(topped, 1)
            dve.wait_ge(topped, 1)
            nc.vector.tensor_copy(windows[:, :], top[:, 0:1]).then_inc(topped, 1)
            dve.wait_ge(cols_in, 32)
            nc.vector.tensor_copy(dst_f[:, :], dst_i[:, :])
            dve.wait_ge(base_back, 16)
            nc.vector.tensor_copy(base_w[:, :], base_n[:, :])

        @block.tensor
        def _(pe):
            pe.wait_ge(made, 2)
            pe.wait_ge(spanned, 3)
            nc.tensor.transpose(turned[0:1, 0:sh.GP], span1[0:sh.GP, :], ident[0:sh.GP, 0:sh.GP]).then_inc(widest, 1)


def project(nc, sh, env):
    ident = env["ident"]
    with ExitStack() as c:
        def tile(name, shape, dt=F32):
            return c.enter_context(nc.sbuf_tensor("pj_" + name, shape, dt))

        new = semaphores(nc, c)

        def sem(name):
            return new("pj_" + name)

        T = CH // P
        w_sb = tile("w", [P, 3 * DIM])
        xt = tile("x", [P, SLOTS, T, DIM])
        stats = tile("stats", [P, SLOTS, T, 6])
        mv = tile("mv", [P, SLOTS, T, 2])
        root = tile("root", [P, SLOTS, T])
        rstd = tile("rstd", [P, SLOTS, T])
        hn = tile("hn", [P, SLOTS, T, DIM])
        ht = tile("ht", [P, SLOTS, CH])
        kv = tile("kv", [P, SLOTS, T, 2 * DIM])
        qs = tile("qs", [P, SLOTS, T, DIM])
        q3 = tile("q3", [P, SLOTS, T, 3, DIM], BF16)
        h_ps = [c.enter_context(nc.psum_tensor(f"pj_hps{k}", [P, CH], F32)) for k in range(2)]
        p_ps = [c.enter_context(nc.psum_tensor(f"pj_pps{t}", [P, 512], F32)) for t in range(T)]
        w_in, stat, aggr, rooted, std, normed, turned, relud, q_sb = (sem(s) for s in (
            "w_in", "stat", "aggr", "rooted", "std", "normed", "turned", "relud", "q_sb"))
        rested = [sem(f"rested{i}") for i in range(2)]
        split = [sem(f"split{i}") for i in range(2)]
        projected = [sem(f"projected{t}") for t in range(T)]
        read = [sem(f"read{t}") for t in range(T)]
        x_in = [sem(f"x_in{k}") for k in range(SLOTS)]
        kv_out = [sem(f"kv_out{k}") for k in range(SLOTS)]
        q_out = [sem(f"q_out{k}") for k in range(SLOTS)]
        block = c.enter_context(nc.Block())
        width = chunk_width(sh)

        def tiles(s):
            return width(s.n) // P

        @block.sync
        def _(sp):
            sp.dma_start(w_sb[:, :], env["wqkv"]).then_inc(w_in, 16)

            def load(s):
                s.freed(sp, normed, SLOTS)
                sp.dma_start(xt[:, s.slot, 0:tiles(s), :], rows_of(env["x"], s.n, width(s.n))
                             ).then_inc(x_in[s.slot], 16)

            def store(s):
                k, t = s.slot, tiles(s)
                sp.wait_ge(read[t - 1], s.nth)
                sp.dma_start(rows_of(env["kv_tab"], s.n, width(s.n)), kv[:, k, 0:t, :]).then_inc(kv_out[k], 16)
                sp.wait_ge(split[1], s.nth)
                sp.dma_start(rows_of(env["q_tab"], s.n, width(s.n)),
                             q3[:, k, 0:t, :, :].rearrange("p t a d -> p t (a d)")).then_inc(q_out[k], 16)

            steps(sp, sh.CHUNKS, SLOTS, [(0, load), (3, store)])
            for k in range(SLOTS):
                uses = len(range(k, sh.CHUNKS, SLOTS))
                sp.wait_ge(kv_out[k], 16 * uses)
                sp.wait_ge(q_out[k], 16 * uses)

        @block.vector
        def _(dve):
            def statistics(s):
                k = s.slot
                dve.wait_ge(x_in[k], 16 * s.use)
                for i in range(tiles(s)):
                    last = nc.vector.bn_stats(stats[:, k, i, :], xt[:, k, i, :])
                last.then_inc(stat, 1)

            def moments(s):
                dve.wait_ge(stat, s.nth)
                alone(dve)
                for i in range(tiles(s)):
                    last = nc.vector.bn_aggr(mv[:, s.slot, i, :], stats[:, s.slot, i, :])
                last.then_inc(aggr, 1)

            def invert(s):
                k, t = s.slot, tiles(s)
                dve.wait_ge(rooted, s.nth)
                nc.vector.reciprocal(rstd[:, k, 0:t], root[:, k, 0:t]).then_inc(std, 1)

            def apply_norm(s):
                k = s.slot
                dve.wait_ge(std, s.nth)
                s.freed(dve, turned, SLOTS)
                for i in range(tiles(s)):
                    last = nc.vector.tensor_scalar(hn[:, k, i, :], xt[:, k, i, :], mv[:, k, i, 0:1],
                                                   rstd[:, k, i:i + 1], ALU.subtract, ALU.mult)
                last.then_inc(normed, 1)

            def rest(part):
                def run(s):
                    k, t = s.slot, tiles(s)
                    dve.wait_ge(split[part - 1] if part else q_sb, s.nth)
                    nc.vector.tensor_tensor(qs[:, k, 0:t, :], qs[:, k, 0:t, :], q3[:, k, 0:t, part, :],
                                            ALU.subtract).then_inc(rested[part], 1)
                return run

            def next_part(part):
                def run(s):
                    k, t = s.slot, tiles(s)
                    dve.wait_ge(rested[part - 1], s.nth)
                    nc.vector.tensor_copy(q3[:, k, 0:t, part, :], qs[:, k, 0:t, :]).then_inc(split[part - 1], 1)
                return run

            steps(dve, sh.CHUNKS, SLOTS, [(3, rest(0)), (1, invert), (3, next_part(1)), (1, apply_norm),
                                          (3, rest(1)), (0, statistics), (3, next_part(2)), (0, moments)])

        @block.tensor
        def _(pe):
            pe.wait_ge(w_in, 16)

            def turn(s):
                pe.wait_ge(normed, s.nth)
                s.freed(pe, relud, 2)
                for i in range(tiles(s)):
                    last = nc.tensor.transpose(h_ps[s.slot % 2][:, i * P:(i + 1) * P], hn[:, s.slot, i, :],
                                               ident[:, :])
                last.then_inc(turned, 1)

            def mul(s):
                pe.wait_ge(relud, s.nth)
                for i in range(T):
                    if i < tiles(s):
                        s.freed(pe, read[i], 1)
                        nc.tensor.matmul(p_ps[i][:, 0:3 * DIM], ht[:, s.slot, i * P:(i + 1) * P], w_sb[:, :],
                                         start=True, stop=True).then_inc(projected[i], 1)

            steps(pe, sh.CHUNKS, SLOTS, [(2, mul), (1, turn)])

        @block.scalar
        def _(act):
            def root_var(s):
                k, t = s.slot, tiles(s)
                act.wait_ge(aggr, s.nth)
                s.freed(act, std, SLOTS)
                nc.scalar.activation(root[:, k, 0:t], mv[:, k, 0:t, 1:2].rearrange("p t o -> p (t o)"), ACT.Sqrt,
                                     bias=env["eps_t"][:, :]).then_inc(rooted, 1)

            def relu(s):
                k, cw = s.slot, width(s.n)
                act.wait_ge(turned, s.nth)
                s.freed(act, projected[0], SLOTS)
                nc.scalar.activation(ht[:, k, 0:cw], h_ps[k % 2][:, 0:cw], ACT.Relu).then_inc(relud, 1)

            def split_out(s):
                k, t = s.slot, tiles(s)
                s.freed(act, split[1], SLOTS)
                s.slot_freed(act, q_out[k], 16)
                s.slot_freed(act, kv_out[k], 16)
                for i in range(t):
                    act.wait_ge(projected[i], s.nth)
                    nc.scalar.activation(qs[:, k, i, :], p_ps[i][:, 0:DIM], ACT.Copy, scale=HC ** -0.5)
                    high = nc.scalar.activation(q3[:, k, i, 0, :], p_ps[i][:, 0:DIM], ACT.Copy, scale=HC ** -0.5)
                    nc.scalar.activation(kv[:, k, i, :], p_ps[i][:, DIM:3 * DIM], ACT.Copy).then_inc(read[i], 1)
                    if i == t - 1:
                        high.then_inc(q_sb, 1)

            steps(act, sh.CHUNKS, SLOTS, [(2, split_out), (1, relu), (0, root_var)])


def start_pass(nc, dve, env, ready, changed):
    nc.vector.tensor_tensor(rel_view(env["dst_rel"]), rel_view(env["dst_f"]), base_view(env["base_w"]),
                            ALU.subtract).then_inc(changed, 1)
    nc.vector.tensor_copy(env["base_i"][:, :], env["base_w"][0:1, :]).then_inc(ready, 1)


def first_pass(nc, dve, env, base_n, base_in, ready, changed):
    dve.wait_ge(base_in, 16)
    nc.vector.tensor_copy(env["base_w"][:, :], base_n[:, :]).then_inc(changed, 1)
    dve.wait_ge(changed, 1)
    start_pass(nc, dve, env, ready, changed)


def next_pass(nc, dve, sh, env, ready, changed, w):
    nc.vector.tensor_scalar(env["base_w"][:, :], env["base_w"][:, :], float(W), float(sh.LAST), ALU.add,
                            ALU.min).then_inc(changed, 1)
    dve.wait_ge(changed, 2 * w + 3)
    start_pass(nc, dve, env, ready, changed)


def rel_view(t):
    return t[:, :].rearrange("p (s j g) -> p s j g", j=J, g=G)


def base_view(t):
    v = t[:, :].rearrange("p (s g) -> p s g", g=G).unsqueeze(2)
    return v.to_broadcast([P, v.shape[1], J, G])


def passes(eng, sh, env):
    widest = eng.value_load(env["windows"][0:1, 0:1], min_val=0, max_val=sh.N)
    return eng.Fori(0, widest // W + 1)


def eng_loads(nc, eng, row, most):
    _, values = nc.values_load_multi_w_load_instructions(
        row, engines=[eng.engine], min_val=0, max_val=most,
        skip_runtime_bounds_check_because="prepare and next_pass bound each base by the last window's")
    return values


def bases(eng, sh, env, n, blocks=1):
    return eng_loads(env["nc"], eng, env["base_i"][0:1, bass.ds(n * G, blocks * G)], sh.LAST)


def one_hot(nc, dve, env, dest, n):
    rel = env["dst_rel"][:, bass.ds(n * C, C)].unsqueeze(2).to_broadcast([P, C, W])
    idx = env["iota_w"][:, :].unsqueeze(1).to_broadcast([P, C, W])
    return nc.vector.tensor_tensor(dest, rel, idx, ALU.is_equal)


def attend(nc, sh, env):
    ident, state, aux = env["ident"], env["state"], env["aux"]
    with ExitStack() as c:
        def tile(name, shape, dt=F32):
            return c.enter_context(nc.sbuf_tensor(name, shape, dt))

        def psum(name, shape, dt=F32):
            return c.enter_context(nc.psum_tensor(name, shape, dt))

        new = semaphores(nc, c)

        def sem(name):
            return new("at_" + name)

        identb = tile("at_identb", [P, P], BF16)
        ident16 = tile("at_ident16", [P, P], BF16)
        sel_head = tile("at_sel_head", [3 * G * HEADS, HEADS, P], BF16)
        sel_feat = tile("at_sel_feat", [HEADS, DIM])
        sel_aux = tile("at_sel_aux", [HEADS + 1, AUXROWS])
        diag = tile("at_diag", [P, G])
        we = tile("at_we", [P, G * HEADS])

        base_n = tile("at_base_n", [P, sh.GROUPS], I32)
        idx = tile("at_idx", [P, SLOTS, C], U32)
        att = tile("at_attr", [P, SLOTS, J, P])
        qd = tile("at_qd", [P, SLOTS, G, 3, DIM], BF16)
        kv = tile("at_kv", [P, SLOTS, C, 2 * DIM])
        hot = tile("at_hot", [P, SLOTS, C, W])
        hot_t = tile("at_hot_t", [P, SLOTS, J, P])
        hot_b = tile("at_hot_b", [P, SLOTS, J, P], BF16)
        miss_b = tile("at_miss_b", [P, SLOTS, J, P], BF16)
        prod = tile("at_prod", [P, C, DIM])
        qk = tile("at_qk", [P, C * HEADS])
        sc = tile("at_sc", [P, SLOTS, J, G * HEADS])
        parts = tile("at_parts", [P, J, 3, G * HEADS], BF16)
        rest = tile("at_rest", [P, J, G * HEADS])
        sct = tile("at_sct", [3 * G * HEADS, 2, J, P], BF16)
        ml4 = tile("at_ml4", [P, J, HEADS])
        ml = tile("at_ml", [P, HEADS])
        mnew = tile("at_mnew", [HEADS, G, W])
        drop = tile("at_drop", [HEADS, G, W])
        fall = tile("at_fall", [HEADS, G * W])
        scale = tile("at_scale", [HEADS + 1, G * W])
        md = tile("at_md", [P, G, HEADS])
        above = tile("at_above", [P, C * HEADS])
        below = tile("at_below", [P, C * HEADS])
        msg = tile("at_msg", [P, 2, C, MSG])
        nodes = tile("at_nodes", [P, 2, DIM + AUXROWS])

        ps_in = psum("at_ps_in", [P, 512])
        ps_qe = psum("at_ps_qe", [P, C, DIM])
        ps_bc = [psum(f"at_ps_bc{i}", [P, 4, P]) for i in range(2)]
        ps_sum = psum("at_ps_sum", [P, 512])
        ps_scale = psum("at_ps_scale", [P, 512])
        ps_me = psum("at_ps_me", [P, 512])
        ps_hot = ps_in[:, 0:J * P].rearrange("p (j e) -> p j e", j=J)
        node_ps = ps_in[:, J * P:J * P + MSG]
        sct_ps = ps_hot[0:3 * G * HEADS, :, :]
        mlt_ps = ps_me[0:HEADS, 128:256]
        mt_ps = ps_me[:, 256:256 + HEADS]
        bias_ps = ps_in[:, J * P + MSG:J * P + MSG + C * HEADS]
        sf_ps = ps_scale[:, 128:256]
        sa_ps = ps_scale[0:AUXROWS, 256:384]
        num_ps = ps_sum[:, 0:128]
        den_ps = ps_sum[0:AUXROWS, 128:256]
        me_ps = ps_me[:, 0:64]

        made, we_in, base_in, tables, changed = (sem(s) for s in ("made", "we_in", "base_in", "tables", "changed"))
        MADE = 20
        idx_in = [sem(f"idx_in{k}") for k in range(SLOTS)]
        attr_in = [sem(f"attr_in{k}") for k in range(SLOTS)]
        q_in = [sem(f"q_in{k}") for k in range(SLOTS)]
        kv_in = [sem(f"kv_in{k}") for k in range(SLOTS)]
        hot_made, hot_turned, hot_copied, bias_made, q_spread, prod_made, qk_made, sc_made = (
            sem(s) for s in ("hot_made", "hot_turned", "hot_copied", "bias_made", "q_spread",
                             "prod_made", "qk_made", "sc_made"))
        sc_turned, sct_made, ml_made, ml_turned, fall_made, m_turned, md_made, m_spread = (
            sem(s) for s in ("sc_turned", "sct_made", "ml_made", "ml_turned", "fall_made", "m_turned", "md_made",
                             "m_spread"))
        split = [sem(f"split{i}") for i in range(4)]
        bc_made = [sem(f"bc_made{i}") for i in range(4)]
        bc_read = [sem(f"bc_read{i}") for i in range(4)]
        above_made, below_made, ex_made, scale_made, scale_spread, msg_made, summed = (
            sem(s) for s in ("above_made", "below_made", "ex_made", "scale_made", "scale_spread", "msg_made",
                             "summed"))
        node_summed, nodes_copied = sem("node_summed"), sem("nodes_copied")
        scaled = [sem(f"scaled{g}") for g in range(G)]
        added = [sem(f"added{g}") for g in range(G)]
        m_kept = [sem(f"m_kept{g}") for g in range(G)]
        m_read = [sem(f"m_read{g}") for g in range(G)]
        block = c.enter_context(nc.Block())

        @block.sync
        def _(sp):
            sp.dma_start(base_n[:, :], env["base_tab"].unsqueeze(0).to_broadcast([P, sh.GROUPS])
                         ).then_inc(base_in, 16)
            sp.wait_ge(made, 8)
            for g in range(G):
                sp.dma_start(we[EDIM * g:EDIM * (g + 1), HEADS * g:HEADS * (g + 1)], env["wet"]).then_inc(we_in, 16)
            with passes(sp, sh, env) as w:
                sp.wait_ge(tables, w + 1)

                def load(s):
                    k = s.slot
                    s.slot_freed(sp, kv_in[k], 16 * C)
                    sp.dma_start(idx[:, k, :], env["src_blocks"][bass.ds(s.n, 1), :, :].squeeze(0)
                                 ).then_inc(idx_in[k], 16)
                    s.freed(sp, bias_made, SLOTS)
                    sp.dma_start(att[:, k, :, :].rearrange("p j e -> p (j e)"),
                                 env["attr"][bass.ds(s.n, 1), :, :].squeeze(0)).then_inc(attr_in[k], 16)
                    s.freed(sp, q_spread, SLOTS)
                    for g, b in enumerate(bases(sp, sh, env, s.n)):
                        sp.dma_start(qd[W * g:W * (g + 1), k, g, :, :].rearrange("p a d -> p (a d)"),
                                     env["q_tab"][bass.ds(b, W), :]).then_inc(q_in[k], 16)

                steps(sp, sh.BLOCKS, SLOTS, [(0, load)], w)

        @block.gpsimd
        def _(pool):
            nc.gpsimd.memset(we[:, :], 0.0).then_inc(made, 1)
            nc.gpsimd.memset(qd[:, :, :, :, :], 0.0).then_inc(made, 1)
            nc.gpsimd.memset(nodes[:, :, :], 0.0).then_inc(made, 1)
            nc.gpsimd.memset(sel_head[:, :, :], 0.0).then_inc(made, 1)
            nc.gpsimd.memset(sel_feat[:, :], 1.0).then_inc(made, 1)
            nc.gpsimd.memset(sel_aux[:, :], 0.0).then_inc(made, 1)
            nc.gpsimd.memset(diag[:, :], 1.0).then_inc(made, 1)
            nc.gpsimd.memset(scale[:, :], 1.0).then_inc(made, 1)
            pool.wait_ge(made, 8)
            nc.gpsimd.memset(msg[:, :, :, MSG - 1:MSG], 1.0).then_inc(made, 1)

            def select_head(part):
                sv = sel_head[:, :, :].rearrange("p h (g w) -> p h g w", g=G)
                nc.gpsimd.affine_select(out=sv, in_=sv, compare_op=ALU.not_equal, fill=1.0,
                                        base=-part * G * HEADS, pattern=[[-1, HEADS], [-HEADS, G], [0, W]],
                                        channel_multiplier=1).then_inc(made, 1)

            select_head(0)
            nc.gpsimd.affine_select(out=sel_feat[:, :], in_=sel_feat[:, :], compare_op=ALU.is_ge, fill=0.0, base=0,
                                    pattern=[[1, DIM]], channel_multiplier=-HC).then_inc(made, 1)
            nc.gpsimd.affine_select(out=sel_aux[0:HEADS, :], in_=sel_aux[0:HEADS, :], compare_op=ALU.not_equal,
                                    fill=1.0, base=AUXD, pattern=[[-1, AUXROWS]], channel_multiplier=1
                                    ).then_inc(made, 1)
            nc.gpsimd.affine_select(out=diag[:, :], in_=diag[:, :], compare_op=ALU.is_ge, fill=0.0, base=0,
                                    pattern=[[-W, G]], channel_multiplier=1).then_inc(made, 1)
            nc.gpsimd.tensor_scalar(identb[:, :], ident[:, :], BIG, None, ALU.mult).then_inc(made, 1)
            nc.gpsimd.tensor_scalar(ident16[:, :], ident[:, :], 1.0, None, ALU.mult).then_inc(made, 1)
            pool.wait_ge(made, 15)
            select_head(1)
            nc.gpsimd.affine_select(out=sel_feat[:, :], in_=sel_feat[:, :], compare_op=ALU.is_ge, fill=0.0,
                                    base=HC - 1, pattern=[[-1, DIM]], channel_multiplier=HC).then_inc(made, 1)
            nc.gpsimd.affine_select(out=sel_aux[:, :], in_=sel_aux[:, :], compare_op=ALU.not_equal, fill=1.0,
                                    base=AUXN - 1000 * HEADS, pattern=[[-1, AUXROWS]], channel_multiplier=1000
                                    ).then_inc(made, 1)
            nc.gpsimd.affine_select(out=diag[:, :], in_=diag[:, :], compare_op=ALU.is_ge, fill=0.0, base=W - 1,
                                    pattern=[[W, G]], channel_multiplier=-1).then_inc(made, 1)
            pool.wait_ge(made, MADE - 1)
            select_head(2)
            pool.wait_ge(made, MADE)
            with passes(pool, sh, env) as w:
                pool.wait_ge(tables, w + 1)

                def gather(s):
                    pool.wait_ge(idx_in[s.slot], 16 * s.use)
                    s.freed(pool, msg_made, SLOTS)
                    alone(pool)
                    for ch in range(C):
                        nc.gpsimd.indirect_dma_start(
                            kv[:, s.slot, ch, :], None, env["kv_tab"],
                            bass.IndirectOffsetOnAxis(ap=idx[:, s.slot, ch:ch + 1], axis=0)
                        ).then_inc(kv_in[s.slot], 16)

                steps(pool, sh.BLOCKS, SLOTS, [(0, gather)], w)

        @block.vector
        def _(dve):
            first_pass(nc, dve, env, base_n, base_in, tables, changed)
            dve.wait_ge(made, MADE)
            with passes(dve, sh, env) as w:
                dve.wait_ge(changed, 2 * w + 2)
                dve.wait_ge(tables, w + 1)

                def head_max(units):
                    def run(s):
                        for u in units:
                            dve.wait_ge(bc_made[u], s.nth)
                            nc.vector.tensor_reduce(ml4[:, u // 2, 4 * (u % 2):4 * (u % 2) + 4],
                                                    ps_bc[u % 2][:, :, :], AX.X, ALU.max).then_inc(bc_read[u], 1)
                    return run

                b_sum, b_max = [None] * G, [None] * G

                def block_max(s):
                    for u in range(4):
                        dve.wait_ge(bc_read[u], s.nth)
                    nc.vector.tensor_tensor(ml[:, :], ml4[:, 0, :], ml4[:, 1, :], ALU.max).then_inc(ml_made, 1)

                def messages(s):
                    k = s.slot
                    dve.wait_ge(ex_made, s.nth)
                    e = msg[:, k % 2, :, DIM:DIM + HEADS].unsqueeze(3).to_broadcast([P, C, HEADS, HC])
                    v = kv[:, k, :, DIM:2 * DIM].rearrange("p c (h d) -> p c h d", h=HEADS)
                    nc.vector.tensor_tensor(msg[:, k % 2, :, 0:DIM].rearrange("p c (h d) -> p c h d", h=HEADS), v, e,
                                            ALU.mult).then_inc(msg_made, 1)

                def load_bases(s, raised=True):
                    if isinstance(s.n, int) and s.n == 0:
                        b_max[:] = bases(dve, sh, env, s.n)
                    elif raised:
                        b = bases(dve, sh, env, s.n - 1, 2)
                        b_sum[:], b_max[:] = b[:G], b[G:]
                    else:
                        b_sum[:] = bases(dve, sh, env, s.n - 1)

                def update(groups, raised=True):
                    def run(s):
                        merged = not (isinstance(s.n, int) and s.n == 0)
                        before = s.nth - 1
                        if groups[0] == 0:
                            if raised:
                                dve.wait_ge(ml_turned, s.nth)
                                s.freed(dve, fall_made, 1)
                            alone(dve)
                        for g in groups:
                            q = slice(g * W, (g + 1) * W)
                            if raised:
                                top = aux[0:HEADS, bass.ds(b_max[g], W)]
                                if g:
                                    dve.wait_ge(m_kept[g - 1], s.nth)
                                else:
                                    s.freed(dve, m_kept[G - 1], 1)
                                nc.vector.tensor_tensor(mnew[:, g, :], top, mlt_ps[:, q], ALU.max
                                                        ).then_inc(m_read[g], 1)
                                nc.vector.tensor_tensor(drop[:, g, :], top, mlt_ps[:, q], ALU.subtract
                                                        ).then_inc(m_read[g], 1)
                            if merged and g == 0:
                                dve.wait_ge(summed, before)
                                dve.wait_ge(scale_spread, before)
                                alone(dve)
                            if merged:
                                num = state[:, bass.ds(b_sum[g], W)]
                                den = aux[AUXD:AUXROWS, bass.ds(b_sum[g], W)]
                                if g:
                                    dve.wait_ge(added[g - 1], 2 * before)
                                elif not (isinstance(s.n, int) and s.n == 1):
                                    dve.wait_ge(added[G - 1], 2 * (before - 1))
                                nc.vector.tensor_tensor(num, num, sf_ps[:, q], ALU.mult).then_inc(scaled[g], 1)
                                nc.vector.tensor_tensor(den, den, sa_ps[AUXD:AUXROWS, q], ALU.mult
                                                        ).then_inc(scaled[g], 1)
                            if raised:
                                dve.wait_ge(m_read[g], 2 * s.nth)
                                nc.vector.tensor_tensor(top, top, mnew[:, g, :], ALU.max).then_inc(m_kept[g], 1)
                            if merged:
                                dve.wait_ge(scaled[g], 2 * before)
                                nc.vector.tensor_tensor(num, num, num_ps[:, q], ALU.add).then_inc(added[g], 1)
                                nc.vector.tensor_tensor(den, den, den_ps[AUXD:AUXROWS, q], ALU.add
                                                        ).then_inc(added[g], 1)
                    return run

                def hot_one(s):
                    s.freed(dve, node_summed, SLOTS)
                    one_hot(nc, dve, env, hot[:, s.slot, :, :], s.n).then_inc(hot_made, 1)

                def score(s):
                    k = s.slot
                    dve.wait_ge(kv_in[k], 16 * C * s.use)
                    dve.wait_ge(q_spread, s.nth)
                    nc.vector.tensor_tensor(prod[:, :, :], ps_qe[:, :, :], kv[:, k, :, 0:DIM],
                                            ALU.mult).then_inc(prod_made, 1)
                    dve.wait_ge(prod_made, s.nth)
                    nc.vector.tensor_reduce(qk[:, :], prod[:, :, :].rearrange("p c (h d) -> p (c h) d", h=HEADS),
                                            AX.X, ALU.add).then_inc(qk_made, 1)
                    dve.wait_ge(qk_made, s.nth)
                    dve.wait_ge(bias_made, s.nth)
                    if not (isinstance(s.n, int) and s.n < 2):
                        dve.wait_ge(nodes_copied, 2 * (s.nth - 2))
                    else:
                        dve.wait_ge(hot_copied, 3 * (s.nth + min(1, sh.BLOCKS - 1 - s.n)))
                    nc.vector.tensor_tensor(sc[:, k, :, :].rearrange("p j q -> p (j q)"), qk[:, :], bias_ps,
                                            ALU.add).then_inc(sc_made, 1)

                def first_rest(s):
                    dve.wait_ge(split[0], s.nth)
                    nc.vector.tensor_tensor(rest[:, :, :], sc[:, s.slot, :, :], parts[:, :, 0, :], ALU.subtract
                                            ).then_inc(split[1], 1)

                def last_rest(s):
                    dve.wait_ge(split[2], s.nth)
                    nc.vector.tensor_tensor(parts[:, :, 2, :], rest[:, :, :], parts[:, :, 1, :], ALU.subtract
                                            ).then_inc(split[3], 1)

                def spread_max(s):
                    dve.wait_ge(m_turned, s.nth)
                    nc.vector.tensor_tensor(md[:, :, :], mt_ps.unsqueeze(1).to_broadcast([P, G, HEADS]),
                                            diag[:, :].unsqueeze(2).to_broadcast([P, G, HEADS]),
                                            ALU.mult).then_inc(md_made, 1)

                def above_score(s):
                    dve.wait_ge(m_spread, s.nth)
                    s.freed(dve, below_made, 1)
                    nc.vector.tensor_tensor(above[:, :], sc[:, s.slot, :, :].rearrange("p j q -> p (j q)"), me_ps,
                                            ALU.subtract).then_inc(above_made, 1)

                steps(dve, sh.BLOCKS, SLOTS, [(3, load_bases), (2, score), (3, update((0,))), (2, first_rest),
                                           (3, update((1,))), (2, last_rest), (3, update((2, 3))),
                                           (2, head_max((1,))), (3, spread_max), (2, head_max((0, 3))),
                                           (3, above_score), (0, hot_one), (2, head_max((2,))), (3, messages),
                                           (2, block_max)], w)
                last = Step(sh.BLOCKS, 0, (w + 1) * sh.BLOCKS + 1, 0, 0)
                load_bases(last, raised=False)
                update(range(G), raised=False)(last)
                next_pass(nc, dve, sh, env, tables, changed, w)

        @block.tensor
        def _(pe):
            pe.wait_ge(made, MADE)
            pe.wait_ge(we_in, 16 * G)
            with passes(pe, sh, env) as w:
                pe.wait_ge(tables, w + 1)

                def spread_q(j):
                    def run(s):
                        k = s.slot
                        if j == 0:
                            pe.wait_ge(hot_copied, 3 * (s.nth - 1) + 1)
                            pe.wait_ge(q_in[k], 16 * G * s.use)
                            s.freed(pe, prod_made, 1)
                        for part in range(3):
                            last = nc.tensor.matmul(ps_qe[:, G * j:G * (j + 1), :], hot_b[:, k, j, :],
                                                    qd[:, k, :, part, :], start=part == 0, stop=part == 2)
                        if j == J - 1:
                            last.then_inc(q_spread, 1)
                    return run

                def mask(u):
                    def run(s):
                        s.freed(pe, bc_read[u + 2], 1) if u < 2 else pe.wait_ge(bc_read[u - 2], s.nth)
                        nc.tensor.matmul(ps_bc[u % 2][:, :, :], identb[:, :],
                                         miss_b[:, s.slot, u // 2, :].unsqueeze(1).to_broadcast([P, 4, P]),
                                         start=True, stop=False, skip_group_check=True)
                    return run

                def spread_scores(u):
                    def run(s):
                        pe.wait_ge(sct_made, s.nth)
                        for h in range(4):
                            last = nc.tensor.matmul(ps_bc[u % 2][:, h, :], sel_head[:, 4 * (u % 2) + h, :],
                                                    sct[:, s.slot % 2, u // 2, :], start=False, stop=h == 3,
                                                    skip_group_check=True)
                        last.then_inc(bc_made[u], 1)
                    return run

                def turn_block_max(s):
                    pe.wait_ge(ml_made, s.nth)
                    nc.tensor.transpose(mlt_ps, ml[:, :], ident[:, :]).then_inc(ml_turned, 1)

                def sum_up(s):
                    k = s.slot
                    pe.wait_ge(msg_made, s.nth)
                    ahead = min(3, sh.BLOCKS - 1 - s.n) if isinstance(s.n, int) else 3
                    pe.wait_ge(hot_copied, 3 * (s.nth + ahead))
                    for g in range(G):
                        for j in range(J):
                            last = nc.tensor.matmul(node_ps[g * W:(g + 1) * W, :], hot[:, k, j * G + g, :],
                                                    msg[:, k % 2, j * G + g, :], start=j == 0, stop=j == J - 1,
                                                    tile_position=(0, g * W))
                    last.then_inc(node_summed, 1)

                def turn_sums(s):
                    pe.wait_ge(nodes_copied, 2 * s.nth)
                    if not (isinstance(s.n, int) and s.n < 1):
                        pe.wait_ge(added[G - 1], 2 * (s.nth - 1))
                    nc.tensor.transpose(num_ps, nodes[:, s.slot % 2, 0:DIM], ident[:, :])
                    nc.tensor.transpose(den_ps, nodes[:, s.slot % 2, DIM:DIM + AUXROWS], ident[:, :]
                                        ).then_inc(summed, 1)

                def turn_max(s):
                    pe.wait_ge(m_kept[G - 1], s.nth)
                    alone(pe)
                    nc.tensor.transpose(mt_ps, mnew[:, :, :].rearrange("h g w -> h (g w)"),
                                        ident[0:HEADS, 0:HEADS]).then_inc(m_turned, 1)

                def turn_hot(s):
                    pe.wait_ge(hot_made, s.nth)
                    if not (isinstance(s.n, int) and s.n < 1):
                        pe.wait_ge(hot_copied, 3 * (s.nth - 1))
                    for j in range(J):
                        last = nc.tensor.transpose(ps_hot[:, j, :], hot[:, s.slot, G * j:G * (j + 1), :].rearrange(
                            "p g w -> p (g w)"), ident[:, :])
                    last.then_inc(hot_turned, 1)

                def turn_scores(s):
                    pe.wait_ge(split[3], s.nth)
                    for j in range(J):
                        last = nc.tensor.matmul(sct_ps[:, j, :], parts[:, j, :, :].rearrange("p a q -> p (a q)"),
                                                ident16[:, :], start=True, stop=True)
                    last.then_inc(sc_turned, 1)

                def bias(s):
                    k = s.slot
                    pe.wait_ge(attr_in[k], 16 * s.use)
                    s.freed(pe, sc_made, 1)
                    pe.wait_ge(hot_copied, 3 * s.nth)
                    for j in range(J):
                        last = nc.tensor.matmul(bias_ps[:, j * 32:(j + 1) * 32], att[:, k, j, :], we[:, :],
                                                start=True, stop=True)
                    last.then_inc(bias_made, 1)

                def spread_m(s):
                    pe.wait_ge(md_made, s.nth)
                    for j in range(J):
                        last = nc.tensor.matmul(me_ps[:, j * 32:(j + 1) * 32], hot_t[:, s.slot, j, :],
                                                md[:, :, :].rearrange("p g h -> p (g h)"), start=True, stop=True)
                    last.then_inc(m_spread, 1)

                def spread_scale(s):
                    pe.wait_ge(scale_made, s.nth)
                    if not (isinstance(s.n, int) and s.n < 1):
                        pe.wait_ge(added[G - 1], 2 * (s.nth - 1))
                    nc.tensor.matmul(sf_ps, sel_feat[:, :], scale[0:HEADS, :], start=True, stop=True)
                    nc.tensor.matmul(sa_ps, sel_aux[:, :], scale[:, :], start=True, stop=True
                                     ).then_inc(scale_spread, 1)

                steps(pe, sh.BLOCKS, SLOTS, [(4, sum_up), (4, spread_scale), (4, turn_sums), (1, spread_q(0)),
                                             (1, bias), (2, mask(1)), (2, turn_scores), (2, mask(0)),
                                             (2, spread_scores(1)), (2, spread_scores(0)), (3, turn_max),
                                             (2, mask(3)), (2, spread_scores(3)), (3, spread_m), (2, mask(2)),
                                             (2, spread_scores(2)), (0, turn_hot), (1, spread_q(1)),
                                             (2, turn_block_max)], w)

        @block.scalar
        def _(act):
            act.wait_ge(made, MADE)
            with passes(act, sh, env) as w:
                act.wait_ge(tables, w + 1)

                def scale_exp(s):
                    act.wait_ge(m_read[G - 1], 2 * s.nth)
                    nc.scalar.activation(fall[:, :], drop[:, :, :].rearrange("h g w -> h (g w)"), ACT.Relu,
                                         scale=-1.0).then_inc(fall_made, 1)
                    act.wait_ge(fall_made, s.nth)
                    s.freed(act, scale_spread, 1)
                    nc.scalar.activation(scale[0:HEADS, :], fall[:, :], ACT.Exp, bias=env["zero_t"][0:HEADS, :],
                                         scale=-1.0).then_inc(scale_made, 1)

                def high_part(s):
                    act.wait_ge(sc_made, s.nth)
                    nc.scalar.activation(parts[:, :, 0, :], sc[:, s.slot, :, :], ACT.Copy).then_inc(split[0], 1)

                def middle_part(s):
                    act.wait_ge(split[1], s.nth)
                    nc.scalar.activation(parts[:, :, 1, :], rest[:, :, :], ACT.Copy).then_inc(split[2], 1)

                def copy_hot(s):
                    k = s.slot
                    act.wait_ge(hot_turned, s.nth)
                    nc.scalar.activation(hot_b[:, k, :, :], ps_hot[:, :, :], ACT.Copy).then_inc(hot_copied, 1)
                    nc.scalar.activation(hot_t[:, k, :, :], ps_hot[:, :, :], ACT.Copy).then_inc(hot_copied, 1)
                    nc.scalar.activation(miss_b[:, k, :, :], ps_hot[:, :, :], ACT.Identity, bias=env["neg1_t"][:, :]
                                         ).then_inc(hot_copied, 1)

                def copy_scores(s):
                    act.wait_ge(sc_turned, s.nth)
                    s.freed(act, bc_made[2], 2)
                    nc.scalar.activation(sct[:, s.slot % 2, :, :], sct_ps, ACT.Copy).then_inc(sct_made, 1)

                def exp(s):
                    act.wait_ge(above_made, s.nth)
                    nc.scalar.activation(below[:, :], above[:, :], ACT.Relu, scale=-1.0).then_inc(below_made, 1)
                    act.wait_ge(below_made, s.nth)
                    s.freed(act, node_summed, 2)
                    nc.scalar.activation(msg[:, s.slot % 2, :, DIM:DIM + HEADS],
                                         below[:, :].rearrange("p (c h) -> p c h", h=HEADS), ACT.Exp,
                                         bias=env["zero_t"][:, :], scale=-1.0).then_inc(ex_made, 1)

                def copy_nodes(s):
                    act.wait_ge(node_summed, s.nth)
                    s.freed(act, summed, 2)
                    to = nodes[:, s.slot % 2, :]
                    nc.scalar.activation(to[:, 0:DIM], node_ps[:, 0:DIM], ACT.Copy).then_inc(nodes_copied, 1)
                    nc.scalar.activation(to[:, DIM + AUXD:DIM + AUXROWS], node_ps[:, DIM:MSG], ACT.Copy
                                         ).then_inc(nodes_copied, 1)

                steps(act, sh.BLOCKS, SLOTS, [(4, copy_nodes), (2, high_part), (2, middle_part), (2, copy_scores),
                                           (3, scale_exp), (3, exp), (0, copy_hot)], w)


def normalise(nc, sh, env):
    ident, state, aux = env["ident"], env["state"], env["aux"]
    with ExitStack() as c:
        def tile(name, shape, dt=F32):
            return c.enter_context(nc.sbuf_tensor("nm_" + name, shape, dt))

        def psum(name, shape, dt=F32):
            return [c.enter_context(nc.psum_tensor(f"nm_{name}{k}", shape, dt)) for k in range(2)]

        new = semaphores(nc, c)

        def sem(name):
            return new("nm_" + name)

        T = CH // P
        R = HEADS + 1
        xt = tile("xt", [P, SLOTS, T, DIM])
        sums = tile("sums", [P, 2, CH])
        dens = tile("dens", [AUXROWS, 2, CH])
        inv = tile("inv", [P, SLOTS, T, R])
        x1 = tile("x1", [P, SLOTS, T, DIM])
        stats = tile("stats", [P, SLOTS, T, 6])
        mv = tile("mv", [P, SLOTS, T, 2])
        root = tile("root", [P, SLOTS, T])
        rstd = tile("rstd", [P, SLOTS, T])
        hn = tile("hn", [P, SLOTS, T, DIM])
        row = tile("row", [P, SLOTS, T, DIM])
        aux_ps, at_ps, ht_ps, di_ps = (psum(s, [P, CH]) for s in ("aux", "at", "ht", "di"))
        sums_made = sem("sums_made")
        (aux_turned, den_cut, rooted, inverted, at_turned, divided, x1_made, stat, aggr, var_rooted, std, gained,
         normed, h_turned, state_made, row_made, d_turned, dinv_made) = (sem(s) for s in (
             "aux_turned", "den_cut", "rooted", "inverted", "at_turned", "divided", "x1_made", "stat", "aggr",
             "var_rooted", "std", "gained", "normed", "h_turned", "state_made", "row_made", "d_turned",
             "dinv_made"))
        x_in = [sem(f"x_in{k}") for k in range(SLOTS)]
        x1_out = [sem(f"x1_out{k}") for k in range(SLOTS)]
        row_out = [sem(f"row_out{k}") for k in range(SLOTS)]
        block = c.enter_context(nc.Block())
        width = chunk_width(sh)

        def tiles(s):
            return width(s.n) // P

        def by_node(ps, t):
            return ps[:, 0:t * R].rearrange("p (t r) -> p t r", r=R)

        @block.sync
        def _(sp):
            def load(s):
                s.freed(sp, x1_made, SLOTS)
                sp.dma_start(xt[:, s.slot, 0:tiles(s), :], rows_of(env["x"], s.n, width(s.n))
                             ).then_inc(x_in[s.slot], 16)

            def store(s):
                sp.wait_ge(x1_made, s.nth)
                sp.dma_start(rows_of(env["x1_tab"], s.n, width(s.n)), x1[:, s.slot, 0:tiles(s), :]
                             ).then_inc(x1_out[s.slot], 16)
                sp.wait_ge(row_made, s.nth)
                sp.dma_start(rows_of(env["g_tabs"][0], s.n, width(s.n)), row[:, s.slot, 0:tiles(s), :]
                             ).then_inc(row_out[s.slot], 16)

            steps(sp, sh.CHUNKS, SLOTS, [(0, load), (4, store)])
            for k in range(SLOTS):
                uses = len(range(k, sh.CHUNKS, SLOTS))
                sp.wait_ge(x1_out[k], 16 * uses)
                sp.wait_ge(row_out[k], 16 * uses)

        @block.vector
        def _(dve):
            def cut(s):
                k, t = s.slot, tiles(s)
                dve.wait_ge(aux_turned, s.nth)
                s.freed(dve, d_turned, SLOTS)
                nc.vector.tensor_scalar(inv[:, k, 0:t, 0:HEADS], by_node(aux_ps[k % 2], t)[:, :, 0:HEADS], 0.5,
                                        None, ALU.max).then_inc(den_cut, 1)

            def attention(s):
                k, t = s.slot, tiles(s)
                dve.wait_ge(den_cut, s.nth)
                dve.wait_ge(rooted, s.nth)
                nc.vector.reciprocal(inv[:, k, 0:t, :], inv[:, k, 0:t, :]).then_inc(inverted, 1)
                dve.wait_ge(inverted, s.nth)
                dve.wait_ge(at_turned, s.nth)
                s.slot_freed(dve, x1_out[k], 16)
                for i in range(t):
                    last = nc.vector.tensor_tensor(
                        x1[:, k, i, :].rearrange("p (h d) -> p h d", h=HEADS),
                        at_ps[k % 2][:, i * P:(i + 1) * P].rearrange("p (h d) -> p h d", h=HEADS),
                        inv[:, k, i, 0:HEADS].unsqueeze(2).to_broadcast([P, HEADS, HC]), ALU.mult)
                last.then_inc(divided, 1)
                dve.wait_ge(divided, s.nth)
                dve.wait_ge(x_in[k], 16 * s.use)
                nc.vector.tensor_tensor(x1[:, k, 0:t, :], x1[:, k, 0:t, :], xt[:, k, 0:t, :], ALU.add
                                        ).then_inc(x1_made, 1)
                dve.wait_ge(x1_made, s.nth)
                for i in range(t):
                    last = nc.vector.bn_stats(stats[:, k, i, :], x1[:, k, i, :])
                last.then_inc(stat, 1)
                dve.wait_ge(stat, s.nth)
                alone(dve)
                for i in range(t):
                    last = nc.vector.bn_aggr(mv[:, k, i, :], stats[:, k, i, :])
                last.then_inc(aggr, 1)

            def apply_norm(s):
                k, t = s.slot, tiles(s)
                dve.wait_ge(var_rooted, s.nth)
                nc.vector.reciprocal(rstd[:, k, 0:t], root[:, k, 0:t]).then_inc(std, 1)
                dve.wait_ge(std, s.nth)
                nc.vector.tensor_tensor(rstd[:, k, 0:t], rstd[:, k, 0:t],
                                        inv[:, k, 0:t, HEADS:R].rearrange("p t o -> p (t o)"), ALU.mult
                                        ).then_inc(gained, 1)
                dve.wait_ge(gained, s.nth)
                s.freed(dve, h_turned, SLOTS)
                s.freed(dve, row_made, SLOTS)
                for i in range(t):
                    last = nc.vector.tensor_scalar(hn[:, k, i, :], x1[:, k, i, :], mv[:, k, i, 0:1],
                                                   rstd[:, k, i:i + 1], ALU.subtract, ALU.mult)
                last.then_inc(normed, 1)

            steps(dve, sh.CHUNKS, SLOTS, [(2, cut), (3, apply_norm), (2, attention)])

        @block.tensor
        def _(pe):
            def turn_aux(s):
                pe.wait_ge(sums_made, 2 * s.nth)
                s.freed(pe, rooted, 2)
                alone(pe)
                for i in range(tiles(s)):
                    last = nc.tensor.transpose(by_node(aux_ps[s.slot % 2], tiles(s))[:, i, :],
                                               dens[AUXD:AUXROWS, s.slot % 2, i * P:(i + 1) * P],
                                               ident[AUXD:AUXROWS, AUXD:AUXROWS])
                last.then_inc(aux_turned, 1)

            def turn_state(s):
                s.freed(pe, divided, 2)
                for i in range(tiles(s)):
                    last = nc.tensor.transpose(at_ps[s.slot % 2][:, i * P:(i + 1) * P],
                                               sums[:, s.slot % 2, i * P:(i + 1) * P], ident[:, :])
                last.then_inc(at_turned, 1)

            def spread_dinv(s):
                pe.wait_ge(inverted, s.nth)
                s.freed(pe, dinv_made, 2)
                for i in range(tiles(s)):
                    last = nc.tensor.transpose(di_ps[s.slot % 2][:, i * P:(i + 1) * P],
                                               inv[:, s.slot, i, HEADS:R].to_broadcast([P, P]), ident[:, :])
                last.then_inc(d_turned, 1)

            def turn_h(s):
                pe.wait_ge(normed, s.nth)
                s.freed(pe, state_made, 2)
                for i in range(tiles(s)):
                    last = nc.tensor.transpose(ht_ps[s.slot % 2][:, i * P:(i + 1) * P], hn[:, s.slot, i, :],
                                               ident[:, :])
                last.then_inc(h_turned, 1)

            steps(pe, sh.CHUNKS, SLOTS, [(4, turn_h), (3, spread_dinv), (1, turn_aux), (1, turn_state)])

        @block.scalar
        def _(act):
            def copy_sums(s):
                k, cw = s.slot % 2, width(s.n)
                cols = bass.ds(s.n * CH, cw)
                s.freed(act, aux_turned, 2)
                s.freed(act, at_turned, 2)
                alone(act)
                nc.scalar.activation(dens[AUXD:AUXROWS, k, 0:cw], aux[AUXD:AUXROWS, cols], ACT.Copy
                                     ).then_inc(sums_made, 1)
                nc.scalar.activation(sums[:, k, 0:cw], state[:, cols], ACT.Copy).then_inc(sums_made, 1)

            def root_deg(s):
                k, t = s.slot, tiles(s)
                act.wait_ge(den_cut, s.nth)
                nc.scalar.activation(inv[:, k, 0:t, HEADS:R], by_node(aux_ps[k % 2], t)[:, :, HEADS:R], ACT.Sqrt,
                                     bias=env["one_t"][:, :]).then_inc(rooted, 1)

            def root_var(s):
                k, t = s.slot, tiles(s)
                act.wait_ge(aggr, s.nth)
                s.freed(act, std, SLOTS)
                nc.scalar.activation(root[:, k, 0:t], mv[:, k, 0:t, 1:2].rearrange("p t o -> p (t o)"), ACT.Sqrt,
                                     bias=env["eps_t"][:, :]).then_inc(var_rooted, 1)

            def copy_dinv(s):
                act.wait_ge(d_turned, s.nth)
                alone(act)
                nc.scalar.activation(aux[:, bass.ds(s.n * CH, width(s.n))], di_ps[s.slot % 2][:, 0:width(s.n)],
                                     ACT.Copy).then_inc(dinv_made, 1)

            def to_rows(s):
                k, t = s.slot, tiles(s)
                act.wait_ge(normed, s.nth)
                s.slot_freed(act, row_out[k], 16)
                nc.scalar.activation(row[:, k, 0:t, :], hn[:, k, 0:t, :], ACT.Relu).then_inc(row_made, 1)

            def to_state(s):
                act.wait_ge(h_turned, s.nth)
                alone(act)
                nc.scalar.activation(state[:, bass.ds(s.n * CH, width(s.n))], ht_ps[s.slot % 2][:, 0:width(s.n)],
                                     ACT.Relu).then_inc(state_made, 1)

            steps(act, sh.CHUNKS, SLOTS, [(2, root_deg), (0, copy_sums), (4, to_state), (3, copy_dinv), (3, to_rows),
                                        (2, root_var)])


def chunk_width(sh):
    return lambda n: sh.LW if isinstance(n, int) and n == sh.CHUNKS - 1 else CH


def rows_of(tab, n, cw):
    return tab[bass.ds(n * CH, cw), :].rearrange("(t p) d -> p t d", p=P)


def aggregate(nc, sh, layer, env):
    state = env["state"]
    with ExitStack() as c:
        def tile(name, shape, dt=F32):
            return c.enter_context(nc.sbuf_tensor(f"ag{layer}_{name}", shape, dt))

        new = semaphores(nc, c)

        def sem(name):
            return new(f"ag{layer}_{name}")

        idx = tile("idx", [P, SLOTS, C], U32)
        rows = tile("rows", [P, SLOTS, C, DIM])
        hot = tile("hot", [P, SLOTS, C, W])
        base_n = tile("base_n", [P, sh.GROUPS], I32)
        sum_ps = [c.enter_context(nc.psum_tensor(f"ag{layer}_sum{k}", [P, 512], F32)) for k in range(2)]
        base_in, tables, changed, hot_made, summed = (sem(s) for s in (
            "base_in", "tables", "changed", "hot_made", "summed"))
        idx_in = [sem(f"idx_in{k}") for k in range(SLOTS)]
        rows_in = [sem(f"rows_in{k}") for k in range(SLOTS)]
        added = [sem(f"added{g}") for g in range(G)]
        block = c.enter_context(nc.Block())

        @block.sync
        def _(sp):
            sp.dma_start(base_n[:, :], env["base_tab"].unsqueeze(0).to_broadcast([P, sh.GROUPS])
                         ).then_inc(base_in, 16)
            with passes(sp, sh, env) as w:
                sp.wait_ge(tables, w + 1)

                def load(s):
                    s.slot_freed(sp, rows_in[s.slot], 16 * C)
                    sp.dma_start(idx[:, s.slot, :], env["src_blocks"][bass.ds(s.n, 1), :, :].squeeze(0)
                                 ).then_inc(idx_in[s.slot], 16)

                steps(sp, sh.BLOCKS, SLOTS, [(0, load)], w)

        @block.gpsimd
        def _(pool):
            with passes(pool, sh, env) as w:
                pool.wait_ge(tables, w + 1)

                def gather(s):
                    pool.wait_ge(idx_in[s.slot], 16 * s.use)
                    s.freed(pool, summed, SLOTS)
                    alone(pool)
                    for ch in range(C):
                        nc.gpsimd.indirect_dma_start(
                            rows[:, s.slot, ch, :], None, env["g_tabs"][layer],
                            bass.IndirectOffsetOnAxis(ap=idx[:, s.slot, ch:ch + 1], axis=0)
                        ).then_inc(rows_in[s.slot], 16)

                steps(pool, sh.BLOCKS, SLOTS, [(0, gather)], w)

        @block.vector
        def _(dve):
            first_pass(nc, dve, env, base_n, base_in, tables, changed)
            with passes(dve, sh, env) as w:
                dve.wait_ge(changed, 2 * w + 2)
                dve.wait_ge(tables, w + 1)

                def hot_one(s):
                    s.freed(dve, summed, SLOTS)
                    one_hot(nc, dve, env, hot[:, s.slot, :, :], s.n).then_inc(hot_made, 1)

                def merge(s):
                    dve.wait_ge(summed, s.nth)
                    alone(dve)
                    for g, b in enumerate(bases(dve, sh, env, s.n)):
                        into = state[:, bass.ds(b, W)]
                        if g:
                            dve.wait_ge(added[g - 1], s.nth)
                        else:
                            s.freed(dve, added[G - 1], 1)
                        nc.vector.tensor_tensor(into, into, sum_ps[s.slot % 2][:, g * W:(g + 1) * W],
                                                ALU.add).then_inc(added[g], 1)

                steps(dve, sh.BLOCKS, SLOTS, [(0, hot_one), (1, merge)], w)
                next_pass(nc, dve, sh, env, tables, changed, w)

        @block.tensor
        def _(pe):
            with passes(pe, sh, env) as w:
                pe.wait_ge(tables, w + 1)

                def sum_up(s):
                    k = s.slot
                    pe.wait_ge(rows_in[k], 16 * C * s.use)
                    pe.wait_ge(hot_made, s.nth)
                    s.freed(pe, added[G - 1], 2)
                    for g in range(G):
                        for j in range(J):
                            last = nc.tensor.matmul(sum_ps[k % 2][:, g * W:(g + 1) * W], rows[:, k, j * G + g, :],
                                                    hot[:, k, j * G + g, :], start=j == 0, stop=j == J - 1)
                    last.then_inc(summed, 1)

                steps(pe, sh.BLOCKS, SLOTS, [(0, sum_up)], w)


def transform(nc, sh, layer, env):
    ident, state, dinv, vec = env["ident"], env["state"], env["aux"], env["vec_t"]
    w1, w2, w3 = env["weights"]
    with ExitStack() as c:
        def tile(name, shape, dt=F32):
            return c.enter_context(nc.sbuf_tensor(f"tr{layer}_{name}", shape, dt))

        new = semaphores(nc, c)

        def sem(name):
            return new(f"tr{layer}_{name}")

        T = CH // P
        halves = 2 if layer == 0 else 1
        lag = 1 if layer == 0 else 0
        stored = lag + 4 if layer < 2 else 3
        at = (0, 6, 9)[layer]
        act_fn = ACT.Identity if layer == 2 else ACT.Relu
        r = tile("r", [P, SLOTS, 2, CH]) if layer == 0 else None
        gs = tile("gs", [P, SLOTS, CH]) if layer < 2 else None
        hb = tile("hb", [P, SLOTS, CH]) if layer == 2 else None
        wg = tile("wg", [P, halves, DIM]) if layer < 2 else None
        offset = tile("offset", [P, 1]) if layer < 2 else None
        stats = tile("stats", [P, 2, sh.CHUNKS, 6])
        mv = tile("mv", [P, 2, 2])
        root = tile("root", [P, 2])
        gain = tile("gain", [P, 2])
        shift = tile("shift", [P, 2])
        row = tile("row", [P, SLOTS, T, DIM])
        x1 = tile("x1", [P, SLOTS, T, DIM])
        z_ps = [[c.enter_context(nc.psum_tensor(f"tr{layer}_z{k}{h}", [P, CH], F32)) for h in range(2)]
                for k in range(2)] if layer == 0 else None
        o_ps, row_ps = ([c.enter_context(nc.psum_tensor(f"tr{layer}_{name}{k}", [P, CH], F32)) for k in range(2)]
                        for name in ("o", "rowps"))
        o_shift = o_ps[0][:, 0:1]
        weighted, shift_spread, offset_made = sem("weighted"), sem("shift_spread"), sem("offset_made")
        w_next = (w2, w3)[layer] if layer < 2 else None
        (w_in, scaled, z_made, r_made, stat, aggr, std, gained, shifting, shifted, z2_made, r2_made, h_made, o_made,
         g_made, row_turned, row_made, rooted, state_made) = (sem(s) for s in (
             "w_in", "scaled", "z_made", "r_made", "stat", "aggr", "std", "gained", "shifting", "shifted", "z2_made",
             "r2_made", "h_made", "o_made", "g_made", "row_turned", "row_made", "rooted",
             "state_made"))
        x_in = [sem(f"x_in{k}") for k in range(SLOTS)]
        row_out = [sem(f"row_out{k}") for k in range(SLOTS)]
        block = c.enter_context(nc.Block())
        width = chunk_width(sh)
        dest = env["out"] if layer == 2 else env["g_tabs"][layer + 1]

        def cols_of(s):
            return bass.ds(s.n * CH, width(s.n))

        @block.sync
        def _(sp):
            if layer == 0:
                sp.dma_start(w1[:, :, :].rearrange("p a d -> p (a d)"), env["w1"]).then_inc(w_in, 16)
                sp.dma_start(w2[:, :, :], env["w2"].rearrange("(a p) d -> p a d", p=P)).then_inc(w_in, 16)
                sp.dma_start(w3[:, :], env["w3"]).then_inc(w_in, 16)

            def load(s):
                if layer == 2:
                    s.freed(sp, row_made, SLOTS)
                    sp.dma_start(x1[:, s.slot, 0:width(s.n) // P, :], rows_of(env["x1_tab"], s.n, width(s.n))
                                 ).then_inc(x_in[s.slot], 16)

            def store(s):
                sp.wait_ge(row_made, s.nth)
                sp.dma_start(rows_of(dest, s.n, width(s.n)), row[:, s.slot, 0:width(s.n) // P, :]
                             ).then_inc(row_out[s.slot], 16)

            steps(sp, sh.CHUNKS, SLOTS, [(0, load), (stored, store)])
            for k in range(SLOTS):
                sp.wait_ge(row_out[k], 16 * len(range(k, sh.CHUNKS, SLOTS)))

        @block.vector
        def _(dve):
            def scale(s):
                nc.vector.tensor_tensor(state[:, cols_of(s)], state[:, cols_of(s)], dinv[:, cols_of(s)],
                                        ALU.mult).then_inc(scaled, 1)

            def statistics(s):
                cv = sh.LV if width(s.n) != CH or (isinstance(s.n, int) and s.n == sh.CHUNKS - 1) else CH
                dve.wait_ge(r_made, halves * s.nth)
                for h in range(halves):
                    src = r[:, s.slot, h, 0:cv] if layer == 0 else state[:, bass.ds(s.n * CH, cv)]
                    last = nc.vector.bn_stats(stats[:, h, bass.ds(s.n, 1), :].rearrange("p a b -> p (a b)"), src)
                last.then_inc(stat, 1)

            steps(dve, sh.CHUNKS, SLOTS, [(0, scale), (3, statistics)])
            dve.wait_ge(stat, sh.CHUNKS)
            for h in range(halves):
                nc.vector.bn_aggr(mv[:, h, :], stats[:, h, :, :].rearrange("p a b -> p (a b)")).then_inc(aggr, 1)
            dve.wait_ge(aggr, halves)
            hs = slice(0, halves)
            dve.wait_ge(rooted, 1)
            nc.vector.reciprocal(gain[:, hs], root[:, hs]).then_inc(std, 1)
            dve.wait_ge(std, 1)
            nc.vector.tensor_tensor(gain[:, hs], gain[:, hs], vec[:, at + halves:at + 2 * halves],
                                    ALU.mult).then_inc(gained, 1)
            dve.wait_ge(gained, 1)
            nc.vector.tensor_tensor(shift[:, hs], mv[:, hs, 0:1].rearrange("p h o -> p (h o)"), gain[:, hs],
                                    ALU.mult).then_inc(shifting, 1)
            dve.wait_ge(shifting, 1)
            nc.vector.tensor_tensor(shift[:, hs], vec[:, at + 2 * halves:at + 3 * halves], shift[:, hs],
                                    ALU.subtract).then_inc(shifted, 1)
            dve.wait_ge(shifted, 1)

            if layer < 2:
                for h in range(halves):
                    w = w_next[:, h, :] if layer == 0 else w_next[:, :]
                    nc.vector.tensor_scalar(wg[:, h, :], w, gain[:, h:h + 1], None, ALU.mult).then_inc(weighted, 1)
                dve.wait_ge(shift_spread, 1)
                nc.vector.tensor_copy(offset[:, :], o_shift).then_inc(offset_made, 1)
                dve.wait_ge(offset_made, 1)

            def next_sum(s):
                dve.wait_ge(o_made, s.nth)
                s.freed(dve, row_turned, SLOTS)
                s.freed(dve, state_made, SLOTS)
                nc.vector.scalar_tensor_tensor(gs[:, s.slot, 0:width(s.n)], o_ps[s.slot % 2][:, 0:width(s.n)],
                                               offset[:, :], dinv[:, cols_of(s)], ALU.add, ALU.mult
                                               ).then_inc(g_made, 1)

            def normed(s):
                s.freed(dve, row_turned, SLOTS)
                nc.vector.tensor_scalar(hb[:, s.slot, 0:width(s.n)], state[:, cols_of(s)], gain[:, 0:1],
                                        shift[:, 0:1], ALU.mult, ALU.add).then_inc(h_made, 1)

            def residual(s):
                k, cw = s.slot, width(s.n)
                dve.wait_ge(row_turned, s.nth)
                dve.wait_ge(x_in[k], 16 * s.use)
                s.slot_freed(dve, row_out[k], 16)
                nc.vector.tensor_tensor(row[:, k, 0:cw // P, :].rearrange("p t d -> p (t d)"), row_ps[k % 2][:, 0:cw],
                                        x1[:, k, 0:cw // P, :].rearrange("p t d -> p (t d)"),
                                        ALU.add).then_inc(row_made, 1)

            if layer < 2:
                steps(dve, sh.CHUNKS, SLOTS, [(lag + 1, next_sum)])
            else:
                steps(dve, sh.CHUNKS, SLOTS, [(2, residual), (0, normed)])

        @block.tensor
        def _(pe):
            def before(freed_by, made):
                def run(s):
                    cw = width(s.n)
                    pe.wait_ge(scaled, s.nth)
                    if not (isinstance(s.n, int) and s.n < 2):
                        pe.wait_ge(freed_by, 2 * (s.nth - 2))
                    for h in range(2):
                        last = nc.tensor.matmul(z_ps[s.slot % 2][h][:, 0:cw], w1[:, h, :], state[:, cols_of(s)],
                                                start=True, stop=True)
                    last.then_inc(made, 1)
                return run

            def after(s):
                k, cw = s.slot, width(s.n)
                if layer == 0:
                    pe.wait_ge(r2_made, 2 * s.nth)
                s.freed(pe, g_made, 2)
                for h in range(halves):
                    last = nc.tensor.matmul(o_ps[k % 2][:, 0:cw], wg[:, h, :],
                                            r[:, k, h, 0:cw] if layer == 0 else state[:, cols_of(s)],
                                            start=h == 0, stop=h == halves - 1)
                last.then_inc(o_made, 1)

            def turn(s):
                k = s.slot
                pe.wait_ge(g_made if layer < 2 else h_made, s.nth)
                s.freed(pe, row_made, 2)
                for i in range(width(s.n) // P):
                    last = nc.tensor.transpose(row_ps[k % 2][:, i * P:(i + 1) * P],
                                               (gs if layer < 2 else hb)[:, k, i * P:(i + 1) * P], ident[:, :])
                last.then_inc(row_turned, 1)

            def spread_shift():
                pe.wait_ge(shifted, 1)
                for h in range(halves):
                    last = nc.tensor.matmul(o_shift, w_next[:, h, :] if layer == 0 else w_next[:, :],
                                            shift[:, h:h + 1], start=h == 0, stop=h == halves - 1)
                last.then_inc(shift_spread, 1)
                pe.wait_ge(offset_made, 1)
                pe.wait_ge(weighted, halves)

            if layer == 0:
                pe.wait_ge(w_in, 48)
                steps(pe, sh.CHUNKS, SLOTS, [(0, before(r_made, z_made))])
                pe.wait_ge(r_made, 2 * sh.CHUNKS)
                spread_shift()
                steps(pe, sh.CHUNKS, SLOTS, [(0, before(r2_made, z2_made)), (lag, after), (lag + 2, turn)])
            elif layer == 1:
                spread_shift()
                steps(pe, sh.CHUNKS, SLOTS, [(lag, after), (lag + 2, turn)])
            else:
                steps(pe, sh.CHUNKS, SLOTS, [(1, turn)])

        @block.scalar
        def _(act):
            def nonlinear(made_by, made, used_by):
                def run(s):
                    k, cw = s.slot, width(s.n)
                    act.wait_ge(made_by, s.nth)
                    if layer == 0:
                        s.freed(act, used_by, SLOTS)
                    for h in range(halves):
                        src = z_ps[k % 2][h][:, 0:cw] if layer == 0 else state[:, cols_of(s)]
                        to = r[:, k, h, 0:cw] if layer == 0 else state[:, cols_of(s)]
                        nc.scalar.activation(to, src, act_fn, bias=vec[:, at + h:at + h + 1]).then_inc(made, 1)
                return run

            def copy_row(s):
                k, cw = s.slot, width(s.n)
                act.wait_ge(row_turned, s.nth)
                s.slot_freed(act, row_out[k], 16)
                nc.scalar.activation(row[:, k, 0:cw // P, :].rearrange("p t d -> p (t d)"), row_ps[k % 2][:, 0:cw],
                                     ACT.Copy).then_inc(row_made, 1)

            def copy_state(s):
                act.wait_ge(g_made, s.nth)
                nc.scalar.activation(state[:, cols_of(s)], gs[:, s.slot, 0:width(s.n)], ACT.Copy
                                     ).then_inc(state_made, 1)

            steps(act, sh.CHUNKS, SLOTS, [(0, nonlinear(z_made if layer == 0 else scaled, r_made, stat))])
            act.wait_ge(aggr, halves)
            nc.scalar.activation(root[:, 0:halves], mv[:, 0:halves, 1:2].rearrange("p h o -> p (h o)"), ACT.Sqrt,
                                 bias=env["eps_t"][:, :]).then_inc(rooted, 1)
            if layer == 0:
                steps(act, sh.CHUNKS, SLOTS, [(lag + 3, copy_row), (lag + 2, copy_state),
                                            (0, nonlinear(z2_made, r2_made, o_made))])
            elif layer == 1:
                steps(act, sh.CHUNKS, SLOTS, [(lag + 3, copy_row), (lag + 2, copy_state)])


def kernel(**inputs):
    import numpy as np
    import concourse.bacc as bacc
    from concourse.bass_utils import run_bass_kernel_spmd

    a = {k: np.asarray(v) for k, v in inputs.items()}
    n_nodes, n_edges = a["x"].shape[0], a["src"].shape[0]
    sh = Shapes(n_nodes, n_edges)
    pad = sh.BLOCKS * BLOCK - n_edges

    def by_chunk(v, fill):
        v = np.concatenate([v, np.full(pad, fill, v.dtype)]).reshape(sh.BLOCKS, G, J, P)
        return v.transpose(3, 0, 2, 1).reshape(P, sh.BLOCKS, C)

    dst = np.concatenate([a["dst"], np.full(pad, SENTINEL, a["dst"].dtype)])
    attr = np.concatenate([a["edge_attr_32"], np.zeros((pad, EDIM), a["edge_attr_32"].dtype)])
    attr = attr.reshape(sh.BLOCKS, G, J, P, EDIM).transpose(0, 1, 4, 2, 3).reshape(sh.BLOCKS, P, J * P)

    def halves(name):
        return a[name].reshape(-1, P).T

    arrays = {
        "x": np.concatenate([a["x"], np.zeros((sh.NS - n_nodes, DIM), a["x"].dtype)]),
        "src_blocks": by_chunk(a["src"], 0).transpose(1, 0, 2).view(np.uint32),
        "dst_cols": by_chunk(a["dst"], SENTINEL).reshape(P, -1),
        "dst_groups": dst.reshape(sh.GP, -1),
        "attr": attr,
        "wqkv": np.concatenate([a["L0_gnn_Wq"].T, a["L0_gnn_Wk"].T, a["L0_gnn_Wv"].T], 1),
        "wet": a["L0_gnn_We"].T,
        "w1": a["L1_gnn_W1"], "w2": a["L1_gnn_W2"], "w3": a["L1_gnn_W3"],
        "vecs": np.concatenate([halves(f"L1_gnn_{v}{i}") for i in (1, 2, 3) for v in ("b", "g", "beta")], 1),
    }
    arrays = {k: np.ascontiguousarray(v) for k, v in arrays.items()}
    nc = bacc.Bacc("TRN2", target_bir_lowering=False, num_devices=1)
    args = [nc.dram_tensor(k, v.shape, mybir.dt.from_np(v.dtype), kind="ExternalInput").ap()
            for k, v in arrays.items()]
    out = nc.dram_tensor("out", (sh.NS, DIM), F32, kind="ExternalOutput").ap()
    build(nc, sh, *args, out)
    result = run_bass_kernel_spmd(nc, [arrays], core_ids=[0])
    return result.results[0]["out"][:n_nodes]
```
